# Optimizing a Trainium2 kernel written in Bass

```python
import numpy as np
import jax
import jax.numpy as jnp

def _softmax(x, axis=-1):
    return jax.nn.softmax(x, axis=axis)

def _gelu(x):
    return jax.nn.gelu(x, approximate=True)

def _silu(x):
    return jax.nn.silu(x)

def _sigmoid(x):
    return jax.nn.sigmoid(x)

def _layernorm(x, axis=-1, eps=1e-05):
    m = jnp.mean(x, axis=axis, keepdims=True)
    v = jnp.var(x, axis=axis, keepdims=True)
    return (x - m) / jnp.sqrt(v + eps)

def _scatter_add(tgt, idx, src, axis=0):
    return tgt.at[idx].add(src)

def _segment_sum(src, seg, n):
    return jax.ops.segment_sum(src, seg, n)
kernel_name = 'mk_perceiver_d1_seqx_r8_dd0bd0'

def setup_inputs(seed: int=0):
    np.random.seed(seed)
    _w = jnp.asarray

    def _rec_inputs():
        import jax
        import jax.numpy as jnp
        _rk = jax.random.key(seed)
        x = -0.0002928 + 1 * jax.random.normal(jax.random.fold_in(_rk, 1), (32, 64, 128), jnp.float32)
        _lenS = 64 - jax.random.randint(jax.random.fold_in(_rk, 7), (32,), 0, max(1, 64 // 4) + 1, jnp.int32)
        _lenS2 = 1601 - jax.random.randint(jax.random.fold_in(_rk, 8), (32,), 0, max(1, 1601 // 4) + 1, jnp.int32)
        _ctx_512P = jax.random.normal(jax.random.fold_in(_rk, 11), (32, 16, 64), jnp.float32)
        _ctx_512c = jax.random.dirichlet(jax.random.fold_in(_rk, 511), 0.3 * jnp.ones((16,), jnp.float32), (32, 1601))
        _ctx_512t = jnp.einsum('bsk,bkd->bsd', _ctx_512c, _ctx_512P)
        _ctx_512t = _ctx_512t * jax.lax.rsqrt(jnp.mean(jnp.square(_ctx_512t)) + 1e-12) * 0.953939
        ctx_512 = 0.00222621 + 0.99962 * (_ctx_512t + 0.3 * jax.random.normal(jax.random.fold_in(_rk, 611), (32, 1601, 64), jnp.float32))
        return (x, ctx_512)
    x, ctx_512 = _rec_inputs()

    def _L0_xattn_setup():
        import jax, jax.numpy as jnp
        import numpy as np
        H, D, C1, C2, S, M, B, W = (16, 32, 128, 64, 256, 64, 2, 4)

        def _ln(x, g, b):
            m = jnp.mean(x, -1, keepdims=True)
            v = jnp.var(x, -1, keepdims=True)
            return (x - m) * jax.lax.rsqrt(v + 1e-05) * g + b

        def _mha(x, y, wq, wk, wv, li1_w, li1_b, lnx_g, lnx_b, lny_g, lny_b, ln3_g, ln3_b, li2_w, li2_b, li3_w, li3_b, causal):
            xn = _ln(x, lnx_g, lnx_b)
            yn = _ln(y, lny_g, lny_b)
            q = jnp.einsum('bsc,hcd->bhsd', xn, wq)
            k = jnp.einsum('btc,hcd->bhtd', yn, wk)
            v = jnp.einsum('btc,hcd->bhtd', yn, wv)
            a = jax.nn.softmax(jnp.einsum('bhsd,bhtd->bhst', q, k) * D ** (-0.5), axis=-1)
            if causal:
                s, t = (a.shape[-2], a.shape[-1])
                mask = (jnp.arange(t)[None, :] > jnp.arange(s)[:, None]).astype(a.dtype)
                a = a * mask
            o = jnp.einsum('bhst,bhtd->bhsd', a, v)
            o = o.transpose(0, 2, 1, 3).reshape(x.shape[0], x.shape[1], H * D)
            x_out = x + o @ li1_w + li1_b
            h = jax.nn.gelu(_ln(x_out, ln3_g, ln3_b) @ li2_w + li2_b, approximate=False)
            return x_out + h @ li3_w + li3_b
        key = jax.random.key(seed)
        ks = iter(jax.random.split(key, 64))

        def w(shape, scale=0.02):
            return jax.random.normal(next(ks), shape, jnp.float32) * scale
        inp = {'xx': jax.random.normal(next(ks), (B, S, C1), jnp.float32), 'ee': jax.random.normal(next(ks), (B, M, C2), jnp.float32), 'ln1_g': jnp.ones(C1, jnp.float32), 'ln1_b': jnp.zeros(C1, jnp.float32), 'ln2_g': jnp.ones(C1, jnp.float32), 'ln2_b': jnp.zeros(C1, jnp.float32)}
        for pfx, cy in (('a1', C1), ('a2', C2)):
            inp[pfx + '_wq'] = w((H, C1, D))
            inp[pfx + '_wk'] = w((H, cy, D))
            inp[pfx + '_wv'] = w((H, cy, D))
            inp[pfx + '_li1_w'] = w((H * D, C1))
            inp[pfx + '_li1_b'] = jnp.zeros(C1, jnp.float32)
            inp[pfx + '_lnx_g'] = jnp.ones(C1, jnp.float32)
            inp[pfx + '_lnx_b'] = jnp.zeros(C1, jnp.float32)
            inp[pfx + '_lny_g'] = jnp.ones(cy, jnp.float32)
            inp[pfx + '_lny_b'] = jnp.zeros(cy, jnp.float32)
            inp[pfx + '_ln3_g'] = jnp.ones(C1, jnp.float32)
            inp[pfx + '_ln3_b'] = jnp.zeros(C1, jnp.float32)
            inp[pfx + '_li2_w'] = w((C1, C1 * W))
            inp[pfx + '_li2_b'] = jnp.zeros(C1 * W, jnp.float32)
            inp[pfx + '_li3_w'] = w((C1 * W, C1))
            inp[pfx + '_li3_b'] = jnp.zeros(C1, jnp.float32)
        inp['training'] = 0
        return inp
    _L0_xattn_all = _L0_xattn_setup()
    _L0_xattn_in = {k: v for k, v in _L0_xattn_all.items() if k in ('ln1_g', 'ln1_b', 'ln2_g', 'ln2_b', 'a1_wq', 'a1_wk', 'a1_wv', 'a1_li1_w', 'a1_li1_b', 'a1_lnx_g', 'a1_lnx_b', 'a1_lny_g', 'a1_lny_b', 'a1_ln3_g', 'a1_ln3_b', 'a1_li2_w', 'a1_li2_b', 'a1_li3_w', 'a1_li3_b', 'a2_wq', 'a2_wk', 'a2_wv', 'a2_li1_w', 'a2_li1_b', 'a2_lnx_g', 'a2_lnx_b', 'a2_lny_g', 'a2_lny_b', 'a2_ln3_g', 'a2_ln3_b', 'a2_li2_w', 'a2_li2_b', 'a2_li3_w', 'a2_li3_b')}
    del _L0_xattn_all

    def _L0_attn_setup():
        import jax, jax.numpy as jnp
        import numpy as np
        B, L, D, H = (2, 128, 128, 16)
        Dh = D // H
        key = jax.random.key(seed)
        ks = jax.random.split(key, 11)
        w_scale = 1.0 / np.sqrt(D).astype(np.float32)

        def w(k):
            return jax.random.normal(k, (D, D), dtype=jnp.float32) * w_scale

        def b(k):
            return jax.random.normal(k, (D,), dtype=jnp.float32) * 0.01
        return {'x': jax.random.normal(ks[0], (B, L, D), dtype=jnp.float32), 'Wq': w(ks[1]), 'bq': b(ks[2]), 'Wk1': w(ks[3]), 'bk1': b(ks[4]), 'Wv': w(ks[5]), 'bv': b(ks[6]), 'Wk2': w(ks[7]), 'bk2': b(ks[8]), 'Wp': w(ks[9]), 'bp': b(ks[10])}
    _L0_attn_all = _L0_attn_setup()
    _L0_attn_in = {k: v for k, v in _L0_attn_all.items() if k in ('Wq', 'bq', 'Wk1', 'bk1', 'Wv', 'bv', 'Wk2', 'bk2', 'Wp', 'bp')}
    del _L0_attn_all

    def _L0_ffn_setup():
        import jax, jax.numpy as jnp
        import numpy as np
        D_MODEL = 128
        EXPERT_DIM = 256
        N_EXPERTS = 8
        LN_EPS = 1e-05

        def _bit_quant(W):
            scale = jnp.clip(jnp.mean(jnp.abs(W), axis=-1, keepdims=True), 1e-05, None)
            w_q = jnp.clip(jnp.round(W / scale), -1.0, 1.0) * scale
            return W + jax.lax.stop_gradient(w_q - W)
        key = jax.random.key(seed)
        ks = jax.random.split(key, 7)
        x = jax.random.normal(ks[0], (4, 256, D_MODEL), dtype=jnp.float32)
        shared_w1 = jax.random.normal(ks[1], (EXPERT_DIM, D_MODEL), dtype=jnp.float32) / np.sqrt(EXPERT_DIM)
        shared_w2 = jax.random.normal(ks[2], (D_MODEL, EXPERT_DIM), dtype=jnp.float32) / np.sqrt(D_MODEL)
        expert_w1 = jax.random.normal(ks[3], (N_EXPERTS, EXPERT_DIM, D_MODEL), dtype=jnp.float32) / np.sqrt(EXPERT_DIM)
        expert_w2 = jax.random.normal(ks[4], (N_EXPERTS, D_MODEL, EXPERT_DIM), dtype=jnp.float32) / np.sqrt(D_MODEL)
        router_w = 0.02 * jax.random.normal(ks[5], (N_EXPERTS, D_MODEL), dtype=jnp.float32)
        ln_gamma = jnp.ones((D_MODEL,), dtype=jnp.float32)
        ln_beta = jnp.zeros((D_MODEL,), dtype=jnp.float32)
        return {'x': x, 'shared_w1': shared_w1, 'shared_w2': shared_w2, 'expert_w1': expert_w1, 'expert_w2': expert_w2, 'router_w': router_w, 'ln_gamma': ln_gamma, 'ln_beta': ln_beta}
    _L0_ffn_all = _L0_ffn_setup()
    _L0_ffn_in = {k: v for k, v in _L0_ffn_all.items() if k in ('shared_w1', 'shared_w2', 'expert_w1', 'expert_w2', 'router_w', 'ln_gamma', 'ln_beta')}
    del _L0_ffn_all
    return {'x': x, 'ctx_512': ctx_512, 'L0_xattn_ln1_g': _L0_xattn_in['ln1_g'], 'L0_xattn_ln1_b': _L0_xattn_in['ln1_b'], 'L0_xattn_ln2_g': _L0_xattn_in['ln2_g'], 'L0_xattn_ln2_b': _L0_xattn_in['ln2_b'], 'L0_xattn_a1_wq': _L0_xattn_in['a1_wq'], 'L0_xattn_a1_wk': _L0_xattn_in['a1_wk'], 'L0_xattn_a1_wv': _L0_xattn_in['a1_wv'], 'L0_xattn_a1_li1_w': _L0_xattn_in['a1_li1_w'], 'L0_xattn_a1_li1_b': _L0_xattn_in['a1_li1_b'], 'L0_xattn_a1_lnx_g': _L0_xattn_in['a1_lnx_g'], 'L0_xattn_a1_lnx_b': _L0_xattn_in['a1_lnx_b'], 'L0_xattn_a1_lny_g': _L0_xattn_in['a1_lny_g'], 'L0_xattn_a1_lny_b': _L0_xattn_in['a1_lny_b'], 'L0_xattn_a1_ln3_g': _L0_xattn_in['a1_ln3_g'], 'L0_xattn_a1_ln3_b': _L0_xattn_in['a1_ln3_b'], 'L0_xattn_a1_li2_w': _L0_xattn_in['a1_li2_w'], 'L0_xattn_a1_li2_b': _L0_xattn_in['a1_li2_b'], 'L0_xattn_a1_li3_w': _L0_xattn_in['a1_li3_w'], 'L0_xattn_a1_li3_b': _L0_xattn_in['a1_li3_b'], 'L0_xattn_a2_wq': _L0_xattn_in['a2_wq'], 'L0_xattn_a2_wk': _L0_xattn_in['a2_wk'], 'L0_xattn_a2_wv': _L0_xattn_in['a2_wv'], 'L0_xattn_a2_li1_w': _L0_xattn_in['a2_li1_w'], 'L0_xattn_a2_li1_b': _L0_xattn_in['a2_li1_b'], 'L0_xattn_a2_lnx_g': _L0_xattn_in['a2_lnx_g'], 'L0_xattn_a2_lnx_b': _L0_xattn_in['a2_lnx_b'], 'L0_xattn_a2_lny_g': _L0_xattn_in['a2_lny_g'], 'L0_xattn_a2_lny_b': _L0_xattn_in['a2_lny_b'], 'L0_xattn_a2_ln3_g': _L0_xattn_in['a2_ln3_g'], 'L0_xattn_a2_ln3_b': _L0_xattn_in['a2_ln3_b'], 'L0_xattn_a2_li2_w': _L0_xattn_in['a2_li2_w'], 'L0_xattn_a2_li2_b': _L0_xattn_in['a2_li2_b'], 'L0_xattn_a2_li3_w': _L0_xattn_in['a2_li3_w'], 'L0_xattn_a2_li3_b': _L0_xattn_in['a2_li3_b'], 'L0_attn_Wq': _L0_attn_in['Wq'], 'L0_attn_bq': _L0_attn_in['bq'], 'L0_attn_Wk1': _L0_attn_in['Wk1'], 'L0_attn_bk1': _L0_attn_in['bk1'], 'L0_attn_Wv': _L0_attn_in['Wv'], 'L0_attn_bv': _L0_attn_in['bv'], 'L0_attn_Wk2': _L0_attn_in['Wk2'], 'L0_attn_bk2': _L0_attn_in['bk2'], 'L0_attn_Wp': _L0_attn_in['Wp'], 'L0_attn_bp': _L0_attn_in['bp'], 'L0_ffn_shared_w1': _L0_ffn_in['shared_w1'], 'L0_ffn_shared_w2': _L0_ffn_in['shared_w2'], 'L0_ffn_expert_w1': _L0_ffn_in['expert_w1'], 'L0_ffn_expert_w2': _L0_ffn_in['expert_w2'], 'L0_ffn_router_w': _L0_ffn_in['router_w'], 'L0_ffn_ln_gamma': _L0_ffn_in['ln_gamma'], 'L0_ffn_ln_beta': _L0_ffn_in['ln_beta']}

def reference(x, ctx_512, L0_xattn_ln1_g, L0_xattn_ln1_b, L0_xattn_ln2_g, L0_xattn_ln2_b, L0_xattn_a1_wq, L0_xattn_a1_wk, L0_xattn_a1_wv, L0_xattn_a1_li1_w, L0_xattn_a1_li1_b, L0_xattn_a1_lnx_g, L0_xattn_a1_lnx_b, L0_xattn_a1_lny_g, L0_xattn_a1_lny_b, L0_xattn_a1_ln3_g, L0_xattn_a1_ln3_b, L0_xattn_a1_li2_w, L0_xattn_a1_li2_b, L0_xattn_a1_li3_w, L0_xattn_a1_li3_b, L0_xattn_a2_wq, L0_xattn_a2_wk, L0_xattn_a2_wv, L0_xattn_a2_li1_w, L0_xattn_a2_li1_b, L0_xattn_a2_lnx_g, L0_xattn_a2_lnx_b, L0_xattn_a2_lny_g, L0_xattn_a2_lny_b, L0_xattn_a2_ln3_g, L0_xattn_a2_ln3_b, L0_xattn_a2_li2_w, L0_xattn_a2_li2_b, L0_xattn_a2_li3_w, L0_xattn_a2_li3_b, L0_attn_Wq, L0_attn_bq, L0_attn_Wk1, L0_attn_bk1, L0_attn_Wv, L0_attn_bv, L0_attn_Wk2, L0_attn_bk2, L0_attn_Wp, L0_attn_bp, L0_ffn_shared_w1, L0_ffn_shared_w2, L0_ffn_expert_w1, L0_ffn_expert_w2, L0_ffn_router_w, L0_ffn_ln_gamma, L0_ffn_ln_beta):
    import jax
    import jax.numpy as jnp

    def _L0_xattn_ref(xx, ee, ln1_g, ln1_b, ln2_g, ln2_b, a1_wq, a1_wk, a1_wv, a1_li1_w, a1_li1_b, a1_lnx_g, a1_lnx_b, a1_lny_g, a1_lny_b, a1_ln3_g, a1_ln3_b, a1_li2_w, a1_li2_b, a1_li3_w, a1_li3_b, a2_wq, a2_wk, a2_wv, a2_li1_w, a2_li1_b, a2_lnx_g, a2_lnx_b, a2_lny_g, a2_lny_b, a2_ln3_g, a2_ln3_b, a2_li2_w, a2_li2_b, a2_li3_w, a2_li3_b, training):
        import jax, jax.numpy as jnp
        import numpy as np
        H, D, C1, C2, S, M, B, W = (16, 32, 128, 64, 256, 64, 2, 4)

        def _ln(x, g, b):
            m = jnp.mean(x, -1, keepdims=True)
            v = jnp.var(x, -1, keepdims=True)
            return (x - m) * jax.lax.rsqrt(v + 1e-05) * g + b

        def _mha(x, y, wq, wk, wv, li1_w, li1_b, lnx_g, lnx_b, lny_g, lny_b, ln3_g, ln3_b, li2_w, li2_b, li3_w, li3_b, causal):
            xn = _ln(x, lnx_g, lnx_b)
            yn = _ln(y, lny_g, lny_b)
            q = jnp.einsum('bsc,hcd->bhsd', xn, wq)
            k = jnp.einsum('btc,hcd->bhtd', yn, wk)
            v = jnp.einsum('btc,hcd->bhtd', yn, wv)
            a = jax.nn.softmax(jnp.einsum('bhsd,bhtd->bhst', q, k) * D ** (-0.5), axis=-1)
            if causal:
                s, t = (a.shape[-2], a.shape[-1])
                mask = (jnp.arange(t)[None, :] > jnp.arange(s)[:, None]).astype(a.dtype)
                a = a * mask
            o = jnp.einsum('bhst,bhtd->bhsd', a, v)
            o = o.transpose(0, 2, 1, 3).reshape(x.shape[0], x.shape[1], H * D)
            x_out = x + o @ li1_w + li1_b
            h = jax.nn.gelu(_ln(x_out, ln3_g, ln3_b) @ li2_w + li2_b, approximate=False)
            return x_out + h @ li3_w + li3_b
        x = _ln(xx, ln1_g, ln1_b)
        x = x + _mha(x, x, a1_wq, a1_wk, a1_wv, a1_li1_w, a1_li1_b, a1_lnx_g, a1_lnx_b, a1_lny_g, a1_lny_b, a1_ln3_g, a1_ln3_b, a1_li2_w, a1_li2_b, a1_li3_w, a1_li3_b, causal=True)
        x = _ln(x, ln2_g, ln2_b)
        return x + _mha(x, ee, a2_wq, a2_wk, a2_wv, a2_li1_w, a2_li1_b, a2_lnx_g, a2_lnx_b, a2_lny_g, a2_lny_b, a2_ln3_g, a2_ln3_b, a2_li2_w, a2_li2_b, a2_li3_w, a2_li3_b, causal=False)

    def _L0_attn_ref(x, Wq, bq, Wk1, bk1, Wv, bv, Wk2, bk2, Wp, bp):
        import jax, jax.numpy as jnp
        import numpy as np
        B, L, D, H = (2, 128, 128, 16)
        Dh = D // H
        Bx, Lx, Dx = x.shape
        lin = lambda t, W, b_: t @ W + b_
        Q = lin(x, Wq, bq).reshape(Bx, Lx, H, Dh)
        K = lin(x, Wk1, bk1).reshape(Bx, Lx, H, Dh)
        V = lin(x, Wv, bv).reshape(Bx, Lx, H, Dh)
        Wacc = jnp.cumsum(jnp.einsum('blhd,blhe->blhde', K, V), axis=1)
        O1 = jnp.einsum('blhd,blhde->blhe', Q, Wacc)
        V_raw = x.reshape(Bx, Lx, H, Dh)
        E = V_raw[:, 1:] - O1[:, :-1]
        z = lin(x[:, :-1], Wk2, bk2) / jnp.sqrt(jnp.float32(Dx))
        k2 = jax.nn.sigmoid(z * 0.02).reshape(Bx, Lx - 1, H, Dh)
        q2 = -jax.nn.leaky_relu(-Q[:, :-1] / jnp.sqrt(jnp.float32(Dh)), negative_slope=0.02)
        WE = jnp.cumsum(jnp.einsum('blhd,blhe->blhde', k2, E), axis=1)
        O2 = jnp.einsum('blhd,blhde->blhe', q2, WE)
        O2 = jnp.concatenate([jnp.zeros_like(O2[:, :1]), O2], axis=1)
        y = (O1 + O2).reshape(Bx, Lx, Dx)
        return lin(y, Wp, bp)

    def _L0_ffn_ref(x, shared_w1, shared_w2, expert_w1, expert_w2, router_w, ln_gamma, ln_beta):
        import jax, jax.numpy as jnp
        import numpy as np
        D_MODEL = 128
        EXPERT_DIM = 256
        N_EXPERTS = 8
        LN_EPS = 1e-05

        def _bit_quant(W):
            scale = jnp.clip(jnp.mean(jnp.abs(W), axis=-1, keepdims=True), 1e-05, None)
            w_q = jnp.clip(jnp.round(W / scale), -1.0, 1.0) * scale
            return W + jax.lax.stop_gradient(w_q - W)
        mu = jnp.mean(x, axis=-1, keepdims=True)
        var = jnp.mean(jnp.square(x - mu), axis=-1, keepdims=True)
        h = (x - mu) / jnp.sqrt(var + LN_EPS) * ln_gamma + ln_beta
        sw1, sw2 = (_bit_quant(shared_w1), _bit_quant(shared_w2))
        shared_out = jax.nn.silu(jnp.einsum('btd,fd->btf', h, sw1)) @ sw2.T
        probs = jax.nn.softmax(h @ router_w.T, axis=-1)
        top_prob = jnp.max(probs, axis=-1)
        top_idx = jnp.argmax(probs, axis=-1)
        ew1, ew2 = (_bit_quant(expert_w1), _bit_quant(expert_w2))
        h1 = jax.nn.silu(jnp.einsum('btd,efd->ebtf', h, ew1))
        eo = jnp.einsum('ebtf,edf->ebtd', h1, ew2)
        gate = jax.nn.one_hot(top_idx, N_EXPERTS, dtype=h.dtype) * top_prob[..., None]
        routed_out = jnp.einsum('ebtd,bte->btd', eo, gate)
        return shared_out + routed_out
    x = x + _L0_xattn_ref(_layernorm(x, axis=-1), ctx_512, L0_xattn_ln1_g, L0_xattn_ln1_b, L0_xattn_ln2_g, L0_xattn_ln2_b, L0_xattn_a1_wq, L0_xattn_a1_wk, L0_xattn_a1_wv, L0_xattn_a1_li1_w, L0_xattn_a1_li1_b, L0_xattn_a1_lnx_g, L0_xattn_a1_lnx_b, L0_xattn_a1_lny_g, L0_xattn_a1_lny_b, L0_xattn_a1_ln3_g, L0_xattn_a1_ln3_b, L0_xattn_a1_li2_w, L0_xattn_a1_li2_b, L0_xattn_a1_li3_w, L0_xattn_a1_li3_b, L0_xattn_a2_wq, L0_xattn_a2_wk, L0_xattn_a2_wv, L0_xattn_a2_li1_w, L0_xattn_a2_li1_b, L0_xattn_a2_lnx_g, L0_xattn_a2_lnx_b, L0_xattn_a2_lny_g, L0_xattn_a2_lny_b, L0_xattn_a2_ln3_g, L0_xattn_a2_ln3_b, L0_xattn_a2_li2_w, L0_xattn_a2_li2_b, L0_xattn_a2_li3_w, L0_xattn_a2_li3_b, 0)
    x = x + _L0_attn_ref(_layernorm(x, axis=-1), L0_attn_Wq, L0_attn_bq, L0_attn_Wk1, L0_attn_bk1, L0_attn_Wv, L0_attn_bv, L0_attn_Wk2, L0_attn_bk2, L0_attn_Wp, L0_attn_bp)
    x = x + _L0_ffn_ref(_layernorm(x, axis=-1), L0_ffn_shared_w1, L0_ffn_shared_w2, L0_ffn_expert_w1, L0_ffn_expert_w2, L0_ffn_router_w, L0_ffn_ln_gamma, L0_ffn_ln_beta)
    return x

_drawn_inputs = setup_inputs


def setup_inputs(seed=0):
    import zlib

    import numpy as np

    out = dict(_drawn_inputs(seed))
    spreads = {'L0_xattn_ln1_g': (1.0, 0.2),
     'L0_xattn_ln1_b': (0.0, 0.1),
     'L0_xattn_ln2_g': (1.0, 0.2),
     'L0_xattn_ln2_b': (0.0, 0.1),
     'L0_xattn_a1_li1_b': (0.0, 0.1),
     'L0_xattn_a1_lnx_g': (1.0, 0.6),
     'L0_xattn_a1_lnx_b': (0.0, 0.8),
     'L0_xattn_a1_lny_g': (1.0, 0.6),
     'L0_xattn_a1_lny_b': (0.0, 0.8),
     'L0_xattn_a1_ln3_g': (1.0, 0.6),
     'L0_xattn_a1_ln3_b': (0.0, 0.8),
     'L0_xattn_a1_li2_b': (0.0, 0.1),
     'L0_xattn_a1_li3_b': (0.0, 0.1),
     'L0_xattn_a2_li1_b': (0.0, 0.1),
     'L0_xattn_a2_lnx_g': (1.0, 0.6),
     'L0_xattn_a2_lnx_b': (0.0, 0.8),
     'L0_xattn_a2_lny_g': (1.0, 0.6),
     'L0_xattn_a2_lny_b': (0.0, 0.762),
     'L0_xattn_a2_ln3_g': (1.0, 0.6),
     'L0_xattn_a2_ln3_b': (0.0, 0.8),
     'L0_xattn_a2_li2_b': (0.0, 0.1),
     'L0_xattn_a2_li3_b': (0.0, 0.1),
     'L0_ffn_ln_gamma': (1.0, 0.6),
     'L0_ffn_ln_beta': (0.0, 0.8)}
    factors = {'L0_xattn_a1_wq': 8.0,
     'L0_xattn_a1_wk': 8.0,
     'L0_xattn_a1_wv': 2.927,
     'L0_xattn_a1_li1_w': 3.107,
     'L0_xattn_a2_wq': 8.0,
     'L0_xattn_a2_wk': 8.0,
     'L0_attn_bk1': 4.708,
     'L0_attn_bv': 5.335,
     'L0_attn_Wk2': 64.0,
     'L0_attn_bk2': 64.0,
     'L0_attn_bp': 64.0,
     'L0_ffn_shared_w1': 8.0,
     'L0_ffn_shared_w2': 8.0,
     'L0_ffn_expert_w1': 8.0,
     'L0_ffn_expert_w2': 8.0,
     'L0_ffn_router_w': 8.0}
    for name, (base, spread) in spreads.items():
        noise = np.random.default_rng([zlib.crc32(name.encode()), seed]).standard_normal(out[name].shape)
        drawn = base * np.exp(spread * noise) if base else spread * noise
        out[name] = jnp.asarray(drawn.astype(out[name].dtype))
    for name, factor in factors.items():
        out[name] = (out[name] * factor).astype(out[name].dtype)
    return out
```

```python
from contextlib import ExitStack

import concourse.bass as bass
from concourse import mybir

F32 = mybir.dt.float32
F16 = mybir.dt.float16
ALU = mybir.AluOpType
ACT = mybir.ActivationFunctionType
AX = mybir.AxisListType

P = 128
B, S, C = 32, 64, 128
T, CY = 1601, 64
H, D = 16, 32
TOK = B * S
GROUPS = 4
GB = B // GROUPS
GT = GB * S // P
GN = GB * S
FF = 4 * C
FT = FF // P
HL, DL = 16, 8
NE, FE = 8, 256
NX = NE + 1
EPS = 1e-5
MAGIC_MIN_SCALE = 1e-5
SCORE_SCALE = float(D) ** -0.5
QUERY_SCALE = 0.125
TJ = (T + P - 1) // P
TLAST = T - (TJ - 1) * P
HB = 4
HS = H * S


class Chain:

    def __init__(self, eng, sem, base):
        self.eng, self.sem, self.base, self.n = eng, sem, base, 0

    def __call__(self, ins):
        self.n += 1
        ins.then_inc(self.sem, 1)
        self.eng.wait_ge(self.sem, self.base + self.n)


def spread(ap, shape):
    return ap.unsqueeze(len(ap.shape)).broadcast_to(shape)


def perceiver_kernel(nc, a, out):
    with ExitStack() as whole:
        def sb(name, shape, dt=F32, scope=whole):
            return scope.enter_context(nc.sbuf_tensor(name, shape, dt))

        ps = whole.enter_context(nc.psum_tensor("banks", [P, 8, 512], F32))
        w = {}
        w["ident"] = sb("ident", [P, P])
        w["ident16"] = sb("ident16", [P, P], F16)
        w["minus_half"] = sb("minus_half", [P, 16])
        names = ["a1_lnx_g", "a1_lnx_b", "a1_lny_g", "a1_lny_b", "a1_ln3_g", "a1_ln3_b",
                 "a2_lnx_g", "a2_lnx_b", "a2_ln3_g", "a2_ln3_b"]
        w["vec"] = sb("vec", [P, 32])
        w["vec_of"] = {"L0_xattn_" + n: i for i, n in enumerate(names)}
        w["vec_of"].update({"L0_ffn_ln_gamma": 10, "L0_ffn_ln_beta": 11,
                            "L0_xattn_a2_lny_g": 12, "L0_xattn_a2_lny_b": 13})
        w["li2_b"] = {n: sb(f"li2_b_{n}", [P, FT]) for n in ("a1", "a2")}
        rows = ["xattn_ln1_g", "xattn_ln1_b", "xattn_ln2_g", "xattn_ln2_b", "xattn_a1_li1_b", "xattn_a1_li3_b",
                "xattn_a2_li1_b", "xattn_a2_li3_b", "attn_bp"]
        w["row"] = sb("row", [P, len(rows), C])
        w["row_of"] = {"L0_" + n: i for i, n in enumerate(rows)}
        w["qkvz_b"] = sb("qkvz_b", [P, 4, C])
        w["li2"] = {n: sb(f"li2_{n}", [P, FF]) for n in ("a1", "a2")}
        w["li3"] = {n: sb(f"li3_{n}", [P, FT, C]) for n in ("a1", "a2")}
        w["query_fold"] = sb("query_fold", [P, H, 2, CY])
        w["value_fold"] = sb("value_fold", [P, H // 2, C])
        w["qkvz"] = sb("qkvz", [P, 4, C])
        w["wp"] = sb("wp", [P, C])
        w["upto"] = sb("upto", [P, P])
        w["before"] = sb("before", [P, P])
        w["prev"] = sb("prev", [P, P])
        w["next"] = sb("next", [P, P])
        w["sel"] = sb("sel", [P, 2, CY])
        w["later"] = sb("later", [P, S])
        w["t1T"] = sb("t1T", [P, 2 * NX, P])
        w["t2T"] = sb("t2T", [P, 2 * NX, P])
        w["s1"] = sb("s1", [P, 2 * NX])
        w["s2"] = sb("s2", [P, NX])
        w["router"] = sb("router", [P, NE])
        w["iota_down"] = sb("iota_down", [P, NE])
        w["x3"] = sb("x3", [P, TOK // P, C])
        w["xqT"] = sb("xqT", [P, TOK])

        with ExitStack() as scope:
            w["key_fold"] = sb("key_fold", [P, H, C], F32, scope)
            w["value_fold1"] = sb("value_fold1", [P, 2, H // 2, C], F32, scope)
            with ExitStack() as inner:
                prepare_weights(nc, a, w, ps, lambda n, s, d=F32: sb("prep_" + n, s, d, inner))
            with ExitStack() as inner:
                latent_self_attention(nc, a, w, ps, lambda n, s, d=F32: sb("self_" + n, s, d, inner))
        w["attended"] = sb("attended", [P, B, 512])
        with ExitStack() as inner:
            cross_attention(nc, a, w, ps, lambda n, s, d=F32: sb("cross_" + n, s, d, inner))
        with ExitStack() as inner:
            finish_tokens(nc, a, out, w, ps, lambda n, s, d=F32: sb("fin_" + n, s, d, inner))


def prepare_weights(nc, a, w, ps, sb):
    with ExitStack() as ctx:
        sem = lambda n: ctx.enter_context(nc.semaphore("p_" + n))
        wide = {n: sb(f"w_{n}", [P, H, D]) for n in ("a1_wq", "a1_wk", "a1_wv", "a2_wq")}
        narrow = {n: sb(f"w_{n}", [CY, H, D]) for n in ("a2_wk", "a2_wv")}
        narrow_g = {n: sb(f"wg_{n}", [CY, H, D]) for n in ("a2_wk", "a2_wv")}
        turned = {n: sb(f"t_{n}", [P, 4, P]) for n in wide}
        turned_raw = {n: sb(f"tr_{n}", [P, 4, CY]) for n in narrow}
        key_turned = sb("key_turned", [P, 4, 2, CY])
        value_turned = sb("value_turned", [P, 4, CY])
        li1 = {n: sb(f"li1_{n}", [P, 4, C]) for n in ("a1", "a2")}
        w1 = sb("w1", [P, 2 * NX, C])
        w2 = sb("w2", [P, NX, FE])
        low1 = sb("low1", [P, 2 * NX, C])
        low2 = sb("low2", [P, NX, FE])
        half1 = sb("half1", [P, 2 * NX])
        half2 = sb("half2", [P, NX])
        neg1 = sb("neg1", [P, 2 * NX])
        neg2 = sb("neg2", [P, NX])
        router_rows = sb("router_rows", [NE, C])
        attn_in, ffn_in, vec_in, rest_in = sem("attn_in"), sem("ffn_in"), sem("vec_in"), sem("rest_in")
        masks, pool_steps = sem("masks"), sem("pool_steps")
        dve_steps = sem("dve_steps")
        scaled, tern1, tern2 = sem("scaled"), sem("tern1"), sem("tern2")
        filled, emptied = sem("filled"), sem("emptied")
        values_ready = sem("values_ready")
        attn_n = [0]
        ffn_n = [0]
        vec_n = [0]
        rest_n = [0]

        items = [("turn_wide", n) for n in wide] + [("turn_narrow", n) for n in narrow]
        items += [("value_bias", None)]
        items += [(k, r) for r in range(4) for k in ("key_fold", "value_fold1", "query_fold", "value_fold")]
        items += [("router", None)]
        items += [("t1", q) for q in range(5)] + [("t2", q) for q in range(5)]

        with nc.Block() as block:
            @block.sync
            def _(sp):
                for n, t in list(wide.items()) + list(narrow.items()):
                    sp.dma_start(t[:, :, :], a["L0_xattn_" + n].rearrange("h c d -> c h d")).then_inc(attn_in, 16)
                    attn_n[0] += 16
                for n, t in li1.items():
                    sp.dma_start(t[:, :, :], a[f"L0_xattn_{n}_li1_w"].rearrange("(k p) c -> p k c", p=P)).then_inc(attn_in, 16)
                    attn_n[0] += 16
                sp.dma_start(w1[:, 0:2, :], a["L0_ffn_shared_w1"].rearrange("(k p) d -> p k d", p=P)).then_inc(ffn_in, 16)
                sp.dma_start(w1[:, 2:, :], a["L0_ffn_expert_w1"].rearrange("e (k p) d -> p (e k) d", p=P)).then_inc(ffn_in, 16)
                sp.dma_start(w2[:, 0, :], a["L0_ffn_shared_w2"]).then_inc(ffn_in, 16)
                sp.dma_start(w2[:, 1:, :], a["L0_ffn_expert_w2"].rearrange("e d f -> d e f")).then_inc(ffn_in, 16)
                sp.dma_start(router_rows[:, :], a["L0_ffn_router_w"]).then_inc(ffn_in, 16)
                ffn_n[0] = 80
                for n in ("a1", "a2"):
                    sp.dma_start(w["li2"][n][:, :], a[f"L0_xattn_{n}_li2_w"]).then_inc(rest_in, 16)
                    sp.dma_start(w["li3"][n][:, :, :], a[f"L0_xattn_{n}_li3_w"].rearrange("(k p) c -> p k c", p=P)).then_inc(rest_in, 16)
                    rest_n[0] += 32
                for k, n in enumerate(("Wq", "Wk1", "Wv", "Wk2")):
                    sp.dma_start(w["qkvz"][:, k, :], a["L0_attn_" + n]).then_inc(rest_in, 16)
                    rest_n[0] += 16
                sp.dma_start(w["wp"][:, :], a["L0_attn_Wp"]).then_inc(rest_in, 16)
                rest_n[0] += 16
                sp.wait_ge(rest_in, rest_n[0])

            @block.scalar
            def _(act):
                for n, i in w["vec_of"].items():
                    src = a[n]
                    act.dma_start(w["vec"][0:src.shape[0], i:i + 1], src.unsqueeze(1)).then_inc(vec_in, 16)
                    vec_n[0] += 16
                row_n = 0
                for n in ("a1", "a2"):
                    for f in range(FT):
                        src = a[f"L0_xattn_{n}_li2_b"][P * f:P * f + P]
                        act.dma_start(w["li2_b"][n][:, f:f + 1], src.unsqueeze(1)).then_inc(masks, 16)
                        row_n += 16
                for n, i in w["row_of"].items():
                    act.dma_start(w["row"][:, i, :], a[n].partition_broadcast(P)).then_inc(masks, 16)
                    row_n += 16
                for k, n in enumerate(("bq", "bk1", "bv", "bk2")):
                    act.dma_start(w["qkvz_b"][:, k, :], a["L0_attn_" + n].partition_broadcast(P)).then_inc(masks, 16)
                    row_n += 16
                act.wait_ge(masks, row_n)

            @block.gpsimd
            def _(pool):
                step = Chain(pool, pool_steps, 0)

                def blocks(name):
                    return w[name][:, :].rearrange("p (b j) -> p b j", b=2)

                def keep(name, op, base, pattern, mult, fill=0.0, ap=None):
                    v = blocks(name) if ap is None else ap
                    step(pool.affine_select(out=v, in_=v, compare_op=op, fill=fill, base=base, pattern=pattern,
                                            channel_multiplier=mult))

                step(pool.memset(w["ident"][:, :], 0.0))
                keep("ident", ALU.not_equal, 0, [[-1, P]], 1, 1.0, w["ident"][:, :])
                step(pool.tensor_copy(w["ident16"][:, :], w["ident"][:, :]))
                step(pool.memset(w["minus_half"][:, :], -0.5))
                for name, base in (("upto", 0), ("before", -1)):
                    step(pool.memset(w[name][:, :], 1.0))
                    keep(name, ALU.is_ge, base, [[64, 2], [1, 64]], -1)
                    keep(name, ALU.is_ge, 0, [[-64, 2], [0, 64]], 1)
                step(pool.memset(w["prev"][:, :], 0.0))
                keep("prev", ALU.not_equal, 1, [[-64, 2], [-1, 64]], 1, 1.0)
                keep("prev", ALU.is_ge, 0, [[-64, 2], [0, 64]], 1)
                step(pool.memset(w["next"][:, :], 0.0))
                keep("next", ALU.not_equal, -1, [[-64, 2], [-1, 64]], 1, 1.0)
                keep("next", ALU.is_ge, 63, [[64, 2], [0, 64]], -1)
                step(pool.memset(w["sel"][:, :, :], 0.0))
                step(pool.affine_select(out=w["sel"][:, :, :], in_=w["sel"][:, :, :], compare_op=ALU.not_equal, fill=1.0,
                                        base=0, pattern=[[-64, 2], [0, CY]], channel_multiplier=1))
                step(pool.memset(w["later"][:, :], 1.0))
                for p0 in (0, S):
                    v = w["later"][p0:p0 + S, :]
                    step(pool.affine_select(out=v, in_=v, compare_op=ALU.is_ge, fill=0.0, base=-1,
                                            pattern=[[1, S]], channel_multiplier=-1))
                for e in range(NE):
                    step(pool.memset(w["iota_down"][:, e:e + 1], float(NE - e)))

            @block.vector
            def _(dve):
                step = Chain(dve, dve_steps, 0)
                dve.wait_ge(attn_in, attn_n[0])
                dve.wait_ge(vec_in, vec_n[0])
                g_y = w["vec_of"]["L0_xattn_a2_lny_g"]
                for n in narrow:
                    nc.vector.tensor_scalar(narrow_g[n][:, :, :], narrow[n][:, :, :], w["vec"][0:CY, g_y:g_y + 1], None,
                                            ALU.mult).then_inc(scaled, 1)

                def ternary(wide_w, low, scale, half, neg, n, width, done):
                    step(nc.vector.tensor_reduce(half[:, :], wide_w[:, :, :], AX.X, ALU.add, apply_absolute_value=True))
                    step(nc.vector.tensor_scalar(scale[:, :], half[:, :], 1.0 / width, MAGIC_MIN_SCALE, ALU.mult, ALU.max))
                    step(nc.vector.tensor_scalar(half[:, :], scale[:, :], 0.5, None, ALU.mult))
                    step(nc.vector.tensor_scalar(neg[:, :], scale[:, :], -0.5, None, ALU.mult))
                    step(nc.vector.tensor_tensor(low[:, :, :], wide_w[:, :, :], spread(neg[:, :], [P, n, width]), ALU.is_lt))
                    step(nc.vector.tensor_tensor(wide_w[:, :, :], wide_w[:, :, :], spread(half[:, :], [P, n, width]), ALU.is_gt))
                    nc.vector.tensor_tensor(wide_w[:, :, :], wide_w[:, :, :], low[:, :, :], ALU.subtract).then_inc(done, 1)

                for n, (kind, k) in enumerate(items):
                    if kind == "router":
                        dve.wait_ge(ffn_in, ffn_n[0])
                        ternary(w1, low1, w["s1"], half1, neg1, 2 * NX, C, tern1)
                        ternary(w2, low2, w["s2"], half2, neg2, NX, FE, tern2)
                    dve.wait_ge(filled, n + 1)
                    bank = ps[:, n % 4, :]
                    four = bank.rearrange("p (k c) -> p k c", k=4)
                    copy = nc.vector.tensor_copy
                    if kind == "turn_wide":
                        last = copy(turned[k][:, :, :], four)
                    elif kind == "turn_narrow":
                        raw = turned_raw[k]
                        step(copy(raw[:, :, :], bank[:, 0:4 * CY].rearrange("p (k c) -> p k c", k=4)))
                        for q in range(4):
                            for u in range(2 if k == "a2_wk" else 1):
                                dst = key_turned[:, q, u, :] if k == "a2_wk" else value_turned[:, q, :]
                                last = nc.vector.tensor_scalar(dst, raw[:, q, :], raw[:, q, 0:1],
                                                               QUERY_SCALE if k == "a2_wk" else 1.0, ALU.subtract, ALU.mult)
                    elif kind == "value_bias":
                        dve.wait_ge(emptied, n)
                        last = copy(value_turned[:, :, 0], bank[:, 0:4])
                    elif kind in ("key_fold", "value_fold1"):
                        if kind == "key_fold":
                            dst = w["key_fold"][:, :, :].rearrange("p (q r) c -> p q r c", r=4)[:, :, k, :]
                            last = copy(dst, four)
                        else:
                            for q in range(4):
                                h = 4 * q + k
                                last = copy(w["value_fold1"][:, h % 2, h // 2, :], four[:, q, :])
                    elif kind == "query_fold":
                        dst = w["query_fold"][:, :, :, :].rearrange("p (q r) u c -> p q r (u c)", r=4)[:, :, k, :]
                        last = copy(dst, four)
                    elif kind == "value_fold":
                        dst = w["value_fold"][:, :, :].rearrange("p (q r) c -> p q r c", r=4)[:, :, k, :]
                        last = copy(dst, bank[:, 0:2 * C].rearrange("p (k c) -> p k c", k=2))
                    elif kind == "router":
                        last = copy(w["router"][:, :], bank[:, 0:NE])
                    else:
                        m = min(4, 2 * NX - 4 * k)
                        last = copy(w[kind + "T"][:, 4 * k:4 * k + m, :], four[:, 0:m, :])
                    last.then_inc(emptied, 1)
                dve.wait_ge(emptied, len(items))

            @block.tensor
            def _(pe):
                pe.wait_ge(attn_in, attn_n[0])
                pe.wait_ge(pool_steps, 2)
                ident = w["ident"]
                for n, (kind, k) in enumerate(items):
                    if n >= 4:
                        pe.wait_ge(emptied, n - 3)
                    bank = ps[:, n % 4, :]
                    four = bank.rearrange("p (k c) -> p k c", k=4)
                    r0 = 32 * k if isinstance(k, int) and k < 4 else 0
                    if kind == "turn_wide":
                        flat = wide[k][:, :, :].rearrange("p (q r) d -> p q (r d)", q=4)
                        for q in range(4):
                            last = nc.tensor.transpose(four[:, q, :], flat[:, q, :], ident[:, :])
                    elif kind == "turn_narrow":
                        pe.wait_ge(scaled, 2)
                        flat = narrow_g[k][:, :, :].rearrange("p (q r) d -> p q (r d)", q=4)
                        for q in range(4):
                            last = nc.tensor.transpose(bank[:, CY * q:CY * q + CY], flat[:, q, :], ident[0:CY, 0:CY])
                    elif kind == "value_bias":
                        pe.wait_ge(vec_in, vec_n[0])
                        flat = narrow["a2_wv"][:, :, :].rearrange("p (q r) d -> p q (r d)", q=4)
                        b_y = w["vec_of"]["L0_xattn_a2_lny_b"]
                        for q in range(4):
                            last = nc.tensor.matmul(bank[:, q:q + 1], flat[:, q, :], w["vec"][0:CY, b_y:b_y + 1], start=True, stop=True)
                    elif kind == "router":
                        pe.wait_ge(ffn_in, ffn_n[0])
                        last = nc.tensor.transpose(bank[:, 0:NE], router_rows[:, :], ident[0:NE, 0:NE])
                    elif kind in ("t1", "t2"):
                        pe.wait_ge(tern1 if kind == "t1" else tern2, 1)
                        src = w1[:, :, :] if kind == "t1" else w2[:, :, :].rearrange("p e (k f) -> p (e k) f", k=2)
                        for q in range(min(4, 2 * NX - 4 * k)):
                            last = nc.tensor.transpose(four[:, q, :], src[:, 4 * k + q, :], ident[:, :])
                    else:
                        pe.wait_ge(emptied, 7)
                        for q in range(4):
                            rows = slice(r0, r0 + D)
                            if kind == "key_fold":
                                o, l, r = four[:, q, :], turned["a1_wk"][rows, q, :], turned["a1_wq"][rows, q, :]
                            elif kind == "value_fold1":
                                o, l, r = four[:, q, :], turned["a1_wv"][rows, q, :], li1["a1"][rows, q, :]
                            elif kind == "query_fold":
                                o, l = four[:, q, :], turned["a2_wq"][rows, q, :]
                                r = key_turned[rows, q, :, :].rearrange("p u c -> p (u c)")
                            else:
                                o = ps[CY * (q // 2):CY * (q // 2) + CY, n % 4, C * (q % 2):C * (q % 2) + C]
                                l, r = value_turned[rows, q, :], li1["a2"][rows, q, :]
                            last = nc.tensor.matmul(o, l, r, start=True, stop=True)
                    last.then_inc(filled, 1)


class Norms:

    def __init__(self, nc, sb, var_ready, rstd_ready, per, tag):
        self.nc, self.per, self.var_ready, self.rstd_ready = nc, per, var_ready, rstd_ready
        self.stats = sb("stats_" + tag, [P, GT, 6])
        self.mv = sb("mv_" + tag, [P, GT, 2])
        self.var = sb("var_" + tag, [P, GT])
        self.rstd = sb("rstd_" + tag, [P, GT])

    def on_vector(self, dve, step, g, k, dst, src):
        nc = self.nc
        for i in range(GT):
            last = nc.vector.bn_stats(self.stats[:, i, :], src[:, i, :])
        dve.drain()
        for i in range(GT):
            last = nc.vector.bn_aggr(self.mv[:, i, :], self.stats[:, i, :])
        step(last)
        nc.vector.tensor_scalar(self.var[:, :], self.mv[:, :, 1], EPS, None, ALU.add).then_inc(self.var_ready, 1)
        dve.wait_ge(self.rstd_ready, g * self.per + (k + 1))
        for i in range(GT):
            last = nc.vector.tensor_scalar(dst[:, i, :], src[:, i, :], self.mv[:, i, 0:1], self.rstd[:, i:i + 1],
                                           ALU.subtract, ALU.mult)
        return last

    def on_pool(self, pool, g, k, minus_half):
        pool.wait_ge(self.var_ready, g * self.per + (k + 1))
        pool.tensor_tensor(self.rstd[:, :], self.var[:, :], minus_half[:, 0:GT], ALU.pow).then_inc(self.rstd_ready, 1)


def wide_row(w, name):
    i = w["row_of"][name]
    return w["row"][:, i:i + 1, :].broadcast_to([P, GT, C])


def latent_self_attention(nc, a, w, ps, sb):
    with ExitStack() as ctx:
        sem = lambda n: ctx.enter_context(nc.semaphore("s_" + n))
        x = sb("x", [P, GT, C])
        n0 = sb("n0", [P, GT, C])
        x1 = sb("x1", [P, GT, C])
        xo = sb("xo", [P, GT, C])
        x3 = sb("x3_group", [P, GT, C])
        xnT = sb("xnT", [P, GN])
        ynT = sb("ynT", [P, GN])
        keys = sb("keys", [P, GB, H, S])
        values = sb("values", [P, GB, H // 2, C])
        mx = sb("mx", [P, 2, H])
        den = sb("den", [P, 2, H])
        rden = sb("rden", [P, 2, H])
        prob = sb("prob", [P, 2, H, S])
        probT = sb("probT", [P, H // 2, P])
        hid = sb("hid", [P, FT, GN])
        x_in, dve_steps, pass_done = sem("x_in"), sem("dve_steps"), sem("pass_done")
        var_ready, rstd_ready = sem("var_ready"), sem("rstd_ready")
        x_normed, x_turned, xy_ready = sem("x_normed"), sem("x_turned"), sem("xy_ready")
        keys_filled, keys_by_act, keys_by_dve = sem("keys_filled"), sem("keys_by_act"), sem("keys_by_dve")
        vals_filled, vals_by_act, vals_by_dve = sem("vals_filled"), sem("vals_by_act"), sem("vals_by_dve")
        scored, shifted, exped, normed, masked = (sem("scored"), sem("shifted"), sem("exped"), sem("normed"), sem("masked"))
        probs_turned, probT_ready, attended_pair = sem("probs_turned"), sem("probT_ready"), sem("attended_pair")
        n3_ready, n3_turned, h3_ready = sem("n3_ready"), sem("n3_turned"), sem("h3_ready")
        hid_filled, hid_ready, mlp_done = sem("hid_filled"), sem("hid_ready"), sem("mlp_done")
        x3_ready, q_normed, q_turned = sem("x3_ready"), sem("q_normed"), sem("q_turned")
        norms = Norms(nc, sb, var_ready, rstd_ready, 6, "s")
        STEPS = 30
        pairs = GT
        vec = lambda n: w["vec"][:, w["vec_of"]["L0_xattn_" + n]:w["vec_of"]["L0_xattn_" + n] + 1]
        xv = a["x"].rearrange("(i b) s c -> (b s) i c", b=2)

        with nc.Block() as block:
            @block.sync
            def _(sp):
                with sp.Fori(0, GROUPS) as g:
                    sp.wait_ge(pass_done, g + 1)
                    sp.dma_start(x[:, :, :], xv[:, bass.ds(g * GT, GT), :]).then_inc(x_in, 16)

            @block.gpsimd
            def _(pool):
                with pool.Fori(0, GROUPS) as g:
                    for k in range(3):
                        norms.on_pool(pool, g, k, w["minus_half"])
                    for p in range(pairs):
                        pool.wait_ge(normed, g * pairs + (p + 1))
                        pool.tensor_tensor(prob[:, p % 2, :, :], prob[:, p % 2, :, :],
                                           w["later"][:, :].unsqueeze(1).broadcast_to([P, H, S]), ALU.mult).then_inc(masked, 1)
                    norms.on_pool(pool, g, 3, w["minus_half"])
                    norms.on_pool(pool, g, 4, w["minus_half"])
                    norms.on_pool(pool, g, 5, w["minus_half"])

            @block.vector
            def _(dve):
                with dve.Fori(0, GROUPS) as g:
                    step = Chain(dve, dve_steps, g * STEPS)
                    tt = nc.vector.tensor_tensor
                    dve.wait_ge(x_in, g * 16 + 16)
                    step_l = norms.on_vector(dve, step, g, 0, n0, x)
                    step(step_l)
                    step(norms.on_vector(dve, step, g, 1, n0, n0))
                    step(tt(n0[:, :, :], n0[:, :, :], wide_row(w, "L0_xattn_ln1_g"), ALU.mult))
                    step(tt(x1[:, :, :], n0[:, :, :], wide_row(w, "L0_xattn_ln1_b"), ALU.add))
                    norms.on_vector(dve, step, g, 2, n0, x1).then_inc(x_normed, 1)
                    for h in range(1, H, 2):
                        dve.wait_ge(keys_filled, g * H + (h + 1))
                        nc.vector.tensor_copy(keys[:, :, h, :], ps[:, h % 4, :].rearrange("p (b t) -> p b t", b=GB)).then_inc(keys_by_dve, 1)
                    for n in range(1, 2 * GB, 2):
                        dve.wait_ge(vals_filled, g * 2 * GB + (n + 1))
                        nc.vector.tensor_copy(values[:, n // 2, 4:8, :], ps[:, 4 + n % 4, :].rearrange("p (h c) -> p h c", h=4)).then_inc(vals_by_dve, 1)
                    step(tt(xo[:, :, :], x1[:, :, :], wide_row(w, "L0_xattn_a1_li1_b"), ALU.add))

                    def shift(p):
                        dve.wait_ge(scored, g * pairs + (p + 1))
                        sc = ps[:, 2 * (p % 2):2 * (p % 2) + 2, :].rearrange("p k (h t) -> p (k h) t", t=S)
                        step(nc.vector.tensor_reduce(mx[:, p % 2, :], sc, AX.X, ALU.max))
                        if p >= 2:
                            dve.wait_ge(probs_turned, g * pairs + (p - 1))
                        tt(prob[:, p % 2, :, :], sc, spread(mx[:, p % 2, :], [P, H, S]), ALU.subtract).then_inc(shifted, 1)

                    def normalise(p):
                        dve.wait_ge(exped, g * pairs + (p + 1))
                        step(nc.vector.tensor_reduce(den[:, p % 2, :], prob[:, p % 2, :, :], AX.X, ALU.add))
                        step(nc.vector.reciprocal(rden[:, p % 2, :], den[:, p % 2, :]))
                        tt(prob[:, p % 2, :, :], prob[:, p % 2, :, :], spread(rden[:, p % 2, :], [P, H, S]), ALU.mult).then_inc(normed, 1)

                    shift(0)
                    for p in range(pairs):
                        if p + 1 < pairs:
                            shift(p + 1)
                        normalise(p)
                    dve.wait_ge(attended_pair, g * pairs + pairs)
                    step(tt(xo[:, :, :], xo[:, :, :], ps[:, 6, :].rearrange("p (i c) -> p i c", i=GT), ALU.add))
                    norms.on_vector(dve, step, g, 3, n0, xo).then_inc(n3_ready, 1)
                    dve.wait_ge(n3_ready, g + 1)
                    step(tt(xo[:, :, :], xo[:, :, :], x1[:, :, :], ALU.add))
                    step(tt(xo[:, :, :], xo[:, :, :], wide_row(w, "L0_xattn_a1_li3_b"), ALU.add))
                    dve.wait_ge(mlp_done, g + 1)
                    step(tt(xo[:, :, :], xo[:, :, :], ps[:, 5, :].rearrange("p (i c) -> p i c", i=GT), ALU.add))
                    step(norms.on_vector(dve, step, g, 4, xo, xo))
                    step(tt(xo[:, :, :], xo[:, :, :], wide_row(w, "L0_xattn_ln2_g"), ALU.mult))
                    tt(x3[:, :, :], xo[:, :, :], wide_row(w, "L0_xattn_ln2_b"), ALU.add).then_inc(x3_ready, 1)
                    step(tt(w["x3"][:, bass.ds(g * GT, GT), :], xo[:, :, :], wide_row(w, "L0_xattn_ln2_b"), ALU.add))
                    dve.wait_ge(x3_ready, g + 1)
                    norms.on_vector(dve, step, g, 5, n0, x3).then_inc(q_normed, 1)
                    assert step.n == STEPS, step.n

            def turn_out(act, g, p):
                act.wait_ge(probs_turned, g * pairs + (p + 1))
                if p >= 1:
                    act.wait_ge(attended_pair, g * pairs + p)
                act.copy(probT[:, :, :], ps[:, 4:6, :].rearrange("p k (h s) -> p (k h) s", s=P)).then_inc(probT_ready, 1)

            @block.scalar
            def _(act):
                act.sem_inc(pass_done, 1)
                with act.Fori(0, GROUPS) as g:
                    act.wait_ge(x_turned, g + 1)
                    act.activation(xnT[:, :], ps[:, 0, :], ACT.Identity, scale=vec("a1_lnx_g"), bias=vec("a1_lnx_b")).then_inc(xy_ready, 1)
                    act.activation(ynT[:, :], ps[:, 0, :], ACT.Identity, scale=vec("a1_lny_g"), bias=vec("a1_lny_b")).then_inc(xy_ready, 1)
                    for h in range(0, H, 2):
                        act.wait_ge(keys_filled, g * H + (h + 1))
                        act.copy(keys[:, :, h, :], ps[:, h % 4, :].rearrange("p (b t) -> p b t", b=GB)).then_inc(keys_by_act, 1)
                    for n in range(0, 2 * GB, 2):
                        act.wait_ge(vals_filled, g * 2 * GB + (n + 1))
                        act.copy(values[:, n // 2, 0:4, :], ps[:, 4 + n % 4, :].rearrange("p (h c) -> p h c", h=4)).then_inc(vals_by_act, 1)
                    for p in range(pairs):
                        act.wait_ge(shifted, g * pairs + (p + 1))
                        act.activation(prob[:, p % 2, :, :], prob[:, p % 2, :, :], ACT.Exp, scale=SCORE_SCALE).then_inc(exped, 1)
                        if p >= 1:
                            turn_out(act, g, p - 1)
                    turn_out(act, g, pairs - 1)
                    act.wait_ge(n3_turned, g + 1)
                    act.activation(xnT[:, :], ps[:, 0, :], ACT.Identity, scale=vec("a1_ln3_g"), bias=vec("a1_ln3_b")).then_inc(h3_ready, 1)
                    for f in range(FT):
                        act.wait_ge(hid_filled, g * FT + (f + 1))
                        act.activation(hid[:, f, :], ps[:, 1 + f, :], ACT.Gelu, bias=w["li2_b"]["a1"][:, f:f + 1]).then_inc(hid_ready, 1)
                    act.wait_ge(q_turned, g + 1)
                    act.activation(w["xqT"][:, bass.ds(g * GN, GN)], ps[:, 0, :], ACT.Identity, scale=vec("a2_lnx_g"),
                                   bias=vec("a2_lnx_b")).then_inc(pass_done, 1)
                act.wait_ge(pass_done, GROUPS + 1)

            @block.tensor
            def _(pe):
                with pe.Fori(0, GROUPS) as g:
                    ident = w["ident"]

                    def turn(src, ready, done):
                        pe.wait_ge(ready, g + 1)
                        for i in range(GT):
                            last = nc.tensor.transpose(ps[:, 0, P * i:P * i + P], src[:, i, :], ident[:, :])
                        last.then_inc(done, 1)

                    pe.wait_ge(pass_done, g + 1)
                    turn(n0, x_normed, x_turned)
                    pe.wait_ge(xy_ready, g * 2 + 2)
                    for h in range(H):
                        if h >= 4:
                            pe.wait_ge(keys_by_act if h % 2 == 0 else keys_by_dve, g * (H // 2) + (h // 2 - 1))
                        nc.tensor.matmul(ps[:, h % 4, :], w["key_fold"][:, h, :], ynT[:, :], start=True, stop=True).then_inc(keys_filled, 1)
                    for n in range(2 * GB):
                        b, half = n // 2, n % 2
                        if n >= 4:
                            pe.wait_ge(vals_by_act if n % 2 == 0 else vals_by_dve, g * GB + (n // 2 - 1))
                        for par in range(2):
                            last = nc.tensor.matmul(ps[S * par:S * par + S, 4 + n % 4, :], ynT[:, S * b:S * b + S],
                                                    w["value_fold1"][:, par, 4 * half:4 * half + 4, :].rearrange("p h c -> p (h c)"),
                                                    start=True, stop=True)
                        last.then_inc(vals_filled, 1)
                    pe.wait_ge(keys_by_act, g * (H // 2) + H // 2)
                    pe.wait_ge(keys_by_dve, g * (H // 2) + H // 2)

                    def scores(p):
                        if p >= 2:
                            pe.wait_ge(shifted, g * pairs + (p - 1))
                        for half in range(2):
                            for u in range(2):
                                b = 2 * p + u
                                last = nc.tensor.matmul(ps[S * u:S * u + S, 2 * (p % 2) + half, :], xnT[:, S * b:S * b + S],
                                                        keys[:, b, 8 * half:8 * half + 8, :].rearrange("p h t -> p (h t)"),
                                                        start=True, stop=True)
                        last.then_inc(scored, 1)

                    scores(0)
                    pe.wait_ge(vals_by_act, g * GB + GB)
                    pe.wait_ge(vals_by_dve, g * GB + GB)
                    for p in range(pairs):
                        if p + 1 < pairs:
                            scores(p + 1)
                        pe.wait_ge(masked, g * pairs + (p + 1))
                        if p >= 1:
                            pe.wait_ge(probT_ready, g * pairs + p)
                        flat = prob[:, p % 2, :, :].rearrange("p (k j) t -> p k (j t)", j=2)
                        for k in range(H // 2):
                            last = nc.tensor.transpose(ps[:, 4 + k // 4, P * (k % 4):P * (k % 4) + P], flat[:, k, :], ident[:, :])
                        last.then_inc(probs_turned, 1)
                        pe.wait_ge(probT_ready, g * pairs + (p + 1))
                        for k in range(H // 2):
                            for u in range(2):
                                last = nc.tensor.matmul(ps[S * u:S * u + S, 6, C * p:C * p + C], probT[:, k, S * u:S * u + S],
                                                        values[:, 2 * p + u, k, :], start=(k == 0), stop=(k == H // 2 - 1))
                        last.then_inc(attended_pair, 1)
                    turn(n0, n3_ready, n3_turned)
                    pe.wait_ge(h3_ready, g + 1)
                    for f in range(FT):
                        nc.tensor.matmul(ps[:, 1 + f, :], w["li2"]["a1"][:, P * f:P * f + P], xnT[:, :], start=True, stop=True).then_inc(hid_filled, 1)
                    pe.wait_ge(hid_ready, g * FT + FT)
                    for i in range(GT):
                        for f in range(FT):
                            last = nc.tensor.matmul(ps[:, 5, C * i:C * i + C], hid[:, f, P * i:P * i + P], w["li3"]["a1"][:, f, :],
                                                    start=(f == 0), stop=(f == FT - 1))
                    last.then_inc(mlp_done, 1)
                    turn(n0, q_normed, q_turned)


def cross_attention(nc, a, w, ps, sb):
    RING, SCORE, SUM = 4, 0, 7
    with ExitStack() as ctx:
        sem = lambda n: ctx.enter_context(nc.semaphore("c_" + n))
        raw = sb("raw", [P, 2, TJ, CY])
        ones = sb("ones", [P, TJ])
        squares = sb("squares", [P, TJ, CY])
        total = sb("total", [P, TJ])
        mean = sb("mean", [P, 2, TJ])
        square_sum = sb("square_sum", [P, TJ])
        var = sb("var", [P, TJ])
        rstd = sb("rstd", [P, TJ])
        ctx_n = sb("ctx_n", [P, HB, TJ, CY])
        ctx_parts = sb("ctx_parts", [P, TJ, 2, CY], F16)
        ctx_T = sb("ctx_T", [P, HB, TJ * P], F16)
        q_hi = sb("q_hi", [P, HB, HS], F16)
        q_lo = sb("q_lo", [P, HB, HS], F16)
        part_max = sb("part_max", [P, H // 2, 4])
        neg_max = sb("neg_max", [P, H // 2])
        max_rows = sb("max_rows", [H // 2, P], F16)
        expd = sb("expd", [P, 2, HS])
        raw_in = [sem(f"raw_in{k}") for k in range(2)]
        raw_free, mean_ready, squares_ready, var_ready, rstd_ready = (
            sem("raw_free"), sem("mean_ready"), sem("squares_ready"), sem("var_ready"), sem("rstd_ready"))
        pool_steps, ctx_ready, parts_ready, parts_turned = sem("pool_steps"), sem("ctx_ready"), sem("parts_ready"), sem("parts_turned")
        ring_filled, ring_done, hi_done = sem("ring_filled"), sem("ring_done"), sem("hi_done")
        max_ready, rows_ready, rows_in = sem("max_ready"), sem("rows_ready"), sem("rows_in")
        dve_steps = sem("dve_steps")
        scored, exp_done, summed, sum_out = sem("scored"), sem("exp_done"), sem("summed"), sem("sum_out")

        FULL = T // 512
        REST = T - 512 * FULL
        turn = [("turn", 0), ("turn", 1)]
        query = [("query", k) for k in range(4)]
        score = []
        for q in range(2):
            score += [("score", k, u) for k in range(4 * q, 4 * q + 4) for u in range(FULL)] + [("rest", q)]
        rows = [("rows",)]
        first = turn + query + [("turn2", 0), ("turn2", 1)] + score + rows

        def schedule(i, last):
            ahead1, ahead2 = not (last and i == HB - 1), not (last and i >= HB - 2)
            steps = [[] for _ in range(TJ)]
            if ahead1:
                counts = [3, 3, 3, 3, 3, 3, 2, 2, 2, 2]
                n = 0
                for j, m in enumerate(counts):
                    steps[j] += score[n:n + m]
                    n += m
                assert n == len(score)
                steps[11] += rows
            if ahead2:
                steps[10].append(turn[0])
                steps[12].append(turn[1])
                if i % 2 == 0:
                    steps[10].append(query[0])
                    steps[11].append(query[1])
                    steps[12] += query[2:]
            return steps

        ITEMS = sum(len(s) for i in range(HB) for s in schedule(i, False))
        QUERIES, FIRST = 4 * (HB // 2), len(first)
        PASSES = B // HB

        class Ring:

            def __init__(self, base):
                self.base, self.n = base, 0

            def take(self):
                n = self.n
                self.n += 1
                return n

        def slot_of(x):
            return x % HB

        with nc.Block() as block:
            @block.sync
            def _(sp):
                def load(x, slot):
                    sp.wait_ge(raw_free, x + 1)
                    src = a["ctx_512"][bass.ds(x, 1), :, :].rearrange("o t c -> (o t) c")
                    sp.dma_start(raw[:, slot % 2, 0:TJ - 1, :], src[0:P * (TJ - 1), :].rearrange("(p j) c -> p j c", j=TJ - 1)).then_inc(raw_in[slot % 2], 16)
                    sp.dma_start(raw[0:TLAST, slot % 2, TJ - 1, :], src[P * (TJ - 1):T, :]).then_inc(raw_in[slot % 2], 16)

                def place_max(x, slot):
                    sp.wait_ge(rows_ready, x + 1)
                    sp.dma_start(q_hi[0:1, slot, :], max_rows[:, :]).then_inc(rows_in, 16)

                load(0, 0)
                load(1, 1)
                place_max(0, 0)

                def one_pass(g, last):
                    for i in range(HB):
                        if not (last and i >= HB - 2):
                            load(g * HB + (i + 2), slot_of(i + 2))
                        if not (last and i == HB - 1):
                            place_max(g * HB + (i + 1), slot_of(i + 1))

                with sp.Fori(0, PASSES - 1) as g:
                    one_pass(g, False)
                one_pass(PASSES - 1, True)

            @block.gpsimd
            def _(pool):
                raw_clear = raw[64:P, :, TJ - 1, :]
                pool.memset(raw_clear, 0.0).then_inc(raw_free, 1)
                pool.wait_ge(raw_free, 1)
                pool.memset(ones[:, :], 1.0).then_inc(pool_steps, 1)
                pool.wait_ge(pool_steps, 1)
                pool.sem_inc(raw_free, 1)

                def normalise(x, slot):
                    base = x * 3 + 1
                    r = raw[:, slot % 2, :, :]
                    n = ctx_n[:, slot, :, :]
                    pool.wait_ge(mean_ready, x + 1)
                    pool.tensor_tensor(n, r, spread(mean[:, slot % 2, :], [P, TJ, CY]), ALU.subtract).then_inc(raw_free, 1)
                    pool.wait_ge(raw_free, x + 3)
                    pool.tensor_tensor(squares[:, :, :], n, n, ALU.mult).then_inc(squares_ready, 1)
                    pool.wait_ge(var_ready, x + 1)
                    pool.tensor_tensor(rstd[:, :], var[:, :], w["minus_half"][:, 0:TJ], ALU.pow).then_inc(pool_steps, 1)
                    pool.wait_ge(pool_steps, base + 1)
                    pool.tensor_tensor(n, n, spread(rstd[:, :], [P, TJ, CY]), ALU.mult).then_inc(pool_steps, 1)
                    pool.wait_ge(pool_steps, base + 2)
                    pool.tensor_tensor(n[:, :, 0:1], spread(ones[:, :], [P, TJ, 1]), spread(ones[:, :], [P, TJ, 1]), ALU.mult).then_inc(ctx_ready, 1)
                    pool.wait_ge(ctx_ready, x + 1)
                    pool.wait_ge(parts_turned, x + 1)
                    pool.tensor_tensor(ctx_parts[:, :, 0, :], n, spread(ones[:, :], [P, TJ, CY]), ALU.mult).then_inc(pool_steps, 1)
                    pool.wait_ge(pool_steps, base + 3)
                    pool.tensor_tensor(ctx_parts[:, :, 1, :], n, ctx_parts[:, :, 0, :], ALU.subtract).then_inc(parts_ready, 1)

                normalise(0, 0)
                normalise(1, 1)

                def one_pass(g, last):
                    for i in range(HB if not last else HB - 2):
                        pool.wait_ge(summed, (g * HB + i) * TJ + 2)
                        normalise(g * HB + (i + 2), slot_of(i + 2))

                with pool.Fori(0, PASSES - 1) as g:
                    one_pass(g, False)
                one_pass(PASSES - 1, True)
                pool.wait_ge(parts_ready, B)

            @block.vector
            def _(dve):
                copy = nc.vector.tensor_copy

                def means(x, slot):
                    dve.wait_ge(raw_in[slot % 2], (x - slot % 2) * 16 + 32)
                    nc.vector.tensor_reduce(total[:, :], raw[:, slot % 2, :, :], AX.X, ALU.add).then_inc(dve_steps, 1)
                    dve.wait_ge(dve_steps, x * 2 + 1)
                    nc.vector.tensor_scalar(mean[:, slot % 2, :], total[:, :], 1.0 / CY, None, ALU.mult).then_inc(mean_ready, 1)

                def variances(x):
                    dve.wait_ge(squares_ready, x + 1)
                    nc.vector.tensor_reduce(square_sum[:, :], squares[:, :, :], AX.X, ALU.add).then_inc(dve_steps, 1)
                    dve.wait_ge(dve_steps, x * 2 + 2)
                    nc.vector.tensor_scalar(var[:, :], square_sum[:, :], 1.0 / CY, EPS, ALU.mult, ALU.add).then_inc(var_ready, 1)

                def take(ring, item, x, slot):
                    n = ring.take()
                    bank = ps[:, RING + n % 3, :]
                    kind = item[0]
                    dve.wait_ge(ring_filled, ring.base + (n + 1))
                    if kind == "turn":
                        m = (P * 8, P * (TJ - 8))[item[1]]
                        last = copy(ctx_T[:, slot, P * 8 * item[1]:P * 8 * item[1] + m], bank.bitcast(F16)[:, 0:m])
                    elif kind == "query":
                        dve.wait_ge(hi_done, ring.queries + 1)
                        ring.queries += 1
                        k = item[1]
                        v = lambda t: t[:, slot:slot + 2, :].rearrange("p b (h s) -> p h b s", h=H)[:, 4 * k:4 * k + 4, :, :]
                        last = nc.vector.tensor_tensor(v(q_lo), bank.rearrange("p (h b s) -> p h b s", h=4, b=2), v(q_hi), ALU.subtract)
                    elif kind == "score":
                        last = nc.vector.tensor_reduce(part_max[:, item[1], item[2]:item[2] + 1], bank, AX.X, ALU.max)
                    elif kind == "rest":
                        q = item[1]
                        last = nc.vector.tensor_reduce(part_max[:, 4 * q:4 * q + 4, FULL], bank[:, 0:4 * REST].rearrange("p (k t) -> p k t", k=4),
                                                       AX.X, ALU.max)
                    else:
                        last = copy(max_rows[:, :], ps[0:H // 2, RING + n % 3, 0:P])
                    last.then_inc(ring_done, 1)
                    if kind == "rows":
                        dve.wait_ge(ring_done, ring.base + (n + 1))
                        dve.sem_inc(rows_ready, 1)

                def maxima(ring, x):
                    dve.wait_ge(ring_done, ring.base + ring.n)
                    nc.vector.tensor_reduce(neg_max[:, :], part_max[:, :, :], AX.X, ALU.max, negate=True).then_inc(max_ready, 1)

                ring = Ring(0)
                ring.queries = 0
                means(0, 0)
                variances(0)
                means(1, 1)
                variances(1)
                for item in first:
                    if item[0] == "rows":
                        maxima(ring, 0)
                    if item[0] == "turn2":
                        take(ring, ("turn", item[1]), 1, 1)
                    else:
                        take(ring, item, 0, 0)

                def one_pass(g, last):
                    ring = Ring(g * ITEMS + FIRST)
                    ring.queries = g * QUERIES + 4
                    for i in range(HB):
                        x = g * HB + i
                        ahead2 = not (last and i >= HB - 2)
                        for j, items in enumerate(schedule(i, last)):
                            if ahead2 and j == 0:
                                means(x + 2, slot_of(i + 2))
                            if ahead2 and j == 3:
                                variances(x + 2)
                            for item in items:
                                if item[0] == "rows":
                                    take(ring, item, x + 1, slot_of(i + 1))
                                elif item[0] in ("turn", "query"):
                                    take(ring, item, x + 2, slot_of(i + 2))
                                else:
                                    take(ring, item, x + 1, slot_of(i + 1))
                            if j == 9 and items:
                                maxima(ring, x + 1)

                with dve.Fori(0, PASSES - 1) as g:
                    one_pass(g, False)
                one_pass(PASSES - 1, True)

            @block.scalar
            def _(act):
                act.sem_inc(exp_done, 2)
                act.sem_inc(sum_out, 1)

                def high(n, base, k, slot):
                    act.wait_ge(ring_filled, base + (n + 1))
                    v = q_hi[:, slot:slot + 2, :].rearrange("p b (h s) -> p h b s", h=H)[:, 4 * k:4 * k + 4, :, :]
                    act.copy(v, ps[:, RING + n % 3, :].rearrange("p (h b s) -> p h b s", h=4, b=2)).then_inc(hi_done, 1)

                def sums_out(x):
                    act.wait_ge(summed, x * TJ + (TJ + 2))
                    act.copy(w["attended"][:, bass.ds(x, 1), :].rearrange("p o n -> p (o n)"), ps[:, SUM, :]).then_inc(sum_out, 1)

                for n, item in enumerate(first):
                    if item[0] == "query":
                        high(n, 0, item[1], 0)

                def one_pass(g, last):
                    ring = Ring(g * ITEMS + FIRST)
                    for i in range(HB):
                        x = g * HB + i
                        for j, items in enumerate(schedule(i, last)):
                            t = x * TJ + j
                            act.wait_ge(scored, t + 1)
                            act.wait_ge(summed, t + 1)
                            m = P if j < TJ - 1 else TLAST
                            k = (i * TJ + j) % 2
                            act.activation(expd[0:m, k, :], ps[0:m, SCORE + 2 * k:SCORE + 2 * k + 2, :].rearrange("p k n -> p (k n)"),
                                           ACT.Exp, scale=SCORE_SCALE / QUERY_SCALE).then_inc(exp_done, 1)
                            for item in items:
                                n = ring.take()
                                if item[0] == "query":
                                    high(n, ring.base, item[1], slot_of(i + 2))
                        sums_out(x)

                with act.Fori(0, PASSES - 1) as g:
                    one_pass(g, False)
                one_pass(PASSES - 1, True)
                act.wait_ge(sum_out, B + 1)

            @block.tensor
            def _(pe):
                pe.sem_inc(summed, 2)
                pe.sem_inc(parts_turned, 1)

                def put(ring, item, x, slot):
                    n = ring.take()
                    bank = ps[:, RING + n % 3, :]
                    kind = item[0]
                    if not (isinstance(ring.base, int) and ring.base == 0 and n < 3):
                        pe.wait_ge(ring_done, ring.base + (n - 2 if n else 0))
                    if kind == "turn":
                        if item[1] == 0:
                            pe.wait_ge(parts_ready, x + 1)
                        for j in range(8 * item[1], min(8 * item[1] + 8, TJ)):
                            last = nc.tensor.transpose(bank.bitcast(F16)[:, P * (j % 8):P * (j % 8) + P],
                                                       ctx_parts[:, j, :, :].rearrange("p u c -> p (u c)"), w["ident16"][:, :])
                    elif kind == "query":
                        k = item[1]
                        for h in range(4):
                            last = nc.tensor.matmul(bank[:, P * h:P * h + P], w["query_fold"][:, 4 * k + h, :, :].rearrange("p u c -> p (u c)"),
                                                    w["xqT"][:, bass.ds(x * S, 2 * S)], start=True, stop=True)
                    elif kind == "score":
                        k, u = item[1:]
                        last = nc.tensor.matmul(bank, q_hi[:, slot, P * k:P * k + P], ctx_T[:, slot, 512 * u:512 * u + 512], start=True, stop=True)
                    elif kind == "rest":
                        for k in range(4):
                            last = nc.tensor.matmul(bank[:, REST * k:REST * k + REST], q_hi[:, slot, P * (4 * item[1] + k):P * (4 * item[1] + k) + P],
                                                    ctx_T[:, slot, 512 * FULL:T], start=True, stop=True)
                    else:
                        pe.wait_ge(max_ready, x + 1)
                        last = nc.tensor.transpose(ps[0:H // 2, RING + n % 3, 0:P], neg_max[:, :], w["ident"][:, :])
                    last.then_inc(ring_filled, 1)
                    if kind == "turn" and item[1] == 1:
                        pe.wait_ge(ring_filled, ring.base + (n + 1))
                        pe.sem_inc(parts_turned, 1)

                ring = Ring(0)
                for item in first:
                    if item[0] == "turn2":
                        put(ring, ("turn", item[1]), 1, 1)
                    else:
                        if item == score[0]:
                            pe.wait_ge(ring_done, ring.n)
                        put(ring, item, 0, 0)

                def tile_scores(x, i, j):
                    t = x * TJ + j
                    m = P if j < TJ - 1 else TLAST
                    k = (i * TJ + j) % 2
                    pe.wait_ge(exp_done, t + 1)
                    for half in range(2):
                        for part, q in enumerate((q_hi, q_lo)):
                            last = nc.tensor.matmul(ps[0:m, SCORE + 2 * k + half, :], ctx_T[:, slot_of(i), P * j:P * j + m],
                                                    q[:, slot_of(i), 512 * half:512 * half + 512], start=(part == 0), stop=(part == 1))
                    last.then_inc(scored, 1)

                def tile_sum(x, i, j):
                    t = x * TJ + j
                    m = P if j < TJ - 1 else TLAST
                    k = (i * TJ + j) % 2
                    pe.wait_ge(exp_done, t + 3)
                    if j == 0:
                        pe.wait_ge(sum_out, x + 1)
                        pe.wait_ge(ctx_ready, x + 1)
                    for half in range(2):
                        last = nc.tensor.matmul(ps[CY * half:CY * half + CY, SUM, :], ctx_n[0:m, slot_of(i), j, :],
                                                expd[0:m, k, 512 * half:512 * half + 512], start=(j == 0), stop=(j == TJ - 1))
                    last.then_inc(summed, 1)

                def one_pass(g, last):
                    ring = Ring(g * ITEMS + FIRST)
                    for i in range(HB):
                        x = g * HB + i
                        pe.wait_ge(rows_in, x * 16 + 16)
                        for j, items in enumerate(schedule(i, last)):
                            tile_scores(x, i, j)
                            if j:
                                tile_sum(x, i, j - 1)
                            for item in items:
                                if item[0] in ("turn", "query"):
                                    put(ring, item, x + 2, slot_of(i + 2))
                                else:
                                    put(ring, item, x + 1, slot_of(i + 1))
                        tile_sum(x, i, TJ - 1)

                with pe.Fori(0, PASSES - 1) as g:
                    one_pass(g, False)
                one_pass(PASSES - 1, True)


def finish_tokens(nc, a, out, w, ps, sb):
    with ExitStack() as ctx:
        sem = lambda n: ctx.enter_context(nc.semaphore("f_" + n))
        den = sb("den", [P, 2, GB * 4])
        att = sb("att", [P, GB, H // 2, S])
        x0 = sb("x0", [P, GT, C])
        xo = sb("xo", [P, GT, C])
        n0 = sb("n0", [P, GT, C])
        nT = sb("nT", [P, GN])
        hid = sb("hid", [P, FT, GN])
        qkvz = sb("qkvz_tok", [P, GT, 4, C])
        q2 = sb("q2", [P, GT, C])
        q2b = sb("q2b", [P, GT, C])
        err = sb("err", [P, GT, C])
        o1 = sb("o1", [P, GT, C])
        o2 = sb("o2", [P, GT, C])
        spare = att[:, :, :, :].rearrange("p b h s -> p b (h s)")
        pairs = spare[:, 0:4, :].rearrange("p (u k) (d c) -> p u (k d) c", u=2, c=C)
        prods = spare[:, 4:6, :].rearrange("p k (d c) -> p (k d) c", c=C)
        logit_max = sb("logit_max", [P, GT])
        shifted_l = sb("shifted_l", [P, GT, NE])
        exp_l = sb("exp_l", [P, GT, NE])
        den_l = sb("den_l", [P, GT])
        top = sb("top", [P, GT])
        rank = sb("rank", [P, GT, NE])
        best = sb("best", [P, GT])
        onehot = sb("onehot", [P, GT, NE], F16)
        gate = qkvz[:, :, :, :].rearrange("p i k c -> p (i k c)").bitcast(F16).rearrange("p (e n) -> p e n", e=NE)
        act1 = hid[:, :, :].rearrange("p (u k) n -> p u k n", u=2)
        part = spare[:, 4:6, :]
        shared = spare[:, 6, :]
        routed = spare[:, 7, :]
        final = sb("final", [P, GT, C])
        x0_in, den_in, den_inv, inv_in = sem("x0_in"), sem("den_in"), sem("den_inv"), sem("inv_in")
        pass_done, dve_steps, pool_steps = sem("pass_done"), sem("dve_steps"), sem("pool_steps")
        var_ready, rstd_ready = sem("var_ready"), sem("rstd_ready")
        inv_spread, att_out, att_ready, projected = sem("inv_spread"), sem("att_out"), sem("att_ready"), sem("projected")
        norm_ready, turned, nT_ready = sem("norm_ready"), sem("turned"), sem("nT_ready")
        hid_filled, hid_ready, mlp_done = sem("hid_filled"), sem("hid_ready"), sem("mlp_done")
        qkvz_filled, qkvz_out, qkvz_ready = sem("qkvz_filled"), sem("qkvz_out"), sem("qkvz_ready")
        shifted_up, prev_filled, sig_ready = sem("shifted_up"), sem("prev_filled"), sem("sig_ready")
        pairs_ready, pairs_summed, sums_read = sem("pairs_ready"), sem("pairs_summed"), sem("sums_read")
        err_ready, lin_done, norm_ready_y = sem("err_ready"), sem("lin_done"), sem("norm_ready_y")
        logits_filled, logits_shifted, logits_exped, chosen = (
            sem("logits_filled"), sem("logits_shifted"), sem("logits_exped"), sem("chosen"))
        gate_filled, gate_ready = sem("gate_filled"), sem("gate_ready")
        up_filled, up_ready, down_filled, down_out = sem("up_filled"), sem("up_ready"), sem("down_filled"), sem("down_out")
        parts_ready, routed_added, out_turned, out_ready, out_stored = (
            sem("parts_ready"), sem("routed_added"), sem("out_turned"), sem("out_ready"), sem("out_stored"))
        norms = Norms(nc, sb, var_ready, rstd_ready, 4, "f")
        NORMS = 3
        STEPS = 32
        INV = float(C) ** -0.5
        xv = a["x"].rearrange("(i b) s c -> (b s) i c", b=2)
        ov = out.rearrange("(i b) s c -> (b s) i c", b=2)
        vec = lambda n: w["vec"][:, w["vec_of"][n]:w["vec_of"][n] + 1]

        with nc.Block() as block:
            @block.sync
            def _(sp):
                with sp.Fori(0, GROUPS) as g:
                    sp.wait_ge(pass_done, g + 1)
                    for half in range(2):
                        rows = w["attended"][CY * half:CY * half + 1, bass.ds(g * GB, GB), :].rearrange("p b n -> p (b n)")
                        sp.dma_start(den[:, half, :], rows).then_inc(den_in, 16)
                    sp.dma_start(x0[:, :, :], xv[:, bass.ds(g * GT, GT), :]).then_inc(x0_in, 16)
                    sp.wait_ge(den_inv, g + 1)
                    for half in range(2):
                        rows = w["attended"][CY * half:CY * half + 1, bass.ds(g * GB, GB), :].rearrange("p b n -> p (b n)")
                        sp.dma_start(rows, den[:, half, :]).then_inc(inv_in, 16)
                    sp.wait_ge(out_ready, g + 1)
                    sp.dma_start(ov[:, bass.ds(g * GT, GT), :], final[:, :, :]).then_inc(out_stored, 16)
                sp.wait_ge(out_stored, 16 * GROUPS)

            @block.gpsimd
            def _(pool):
                with pool.Fori(0, GROUPS) as g:
                    norms.on_pool(pool, g, 0, w["minus_half"])
                    norms.on_pool(pool, g, 1, w["minus_half"])
                    for n in range(2 * GT):
                        i = n % GT
                        if n == 0:
                            pool.wait_ge(qkvz_ready, g + 1)
                        if n >= GT:
                            pool.wait_ge(err_ready, g * GT + (i + 1))
                        if n >= 2:
                            pool.wait_ge(pairs_summed, g * 2 * GT + (n - 1))
                        if n == GT:
                            pool.wait_ge(sig_ready, g + 1)
                        key = qkvz[:, i, 1 if n < GT else 3, :].rearrange("p (h d) -> p d h", d=DL)
                        val = (qkvz[:, i, 2, :] if n < GT else err[:, i, :]).rearrange("p (h e) -> p h e", e=DL)
                        o = pairs[:, n % 2, :, :].rearrange("p d (h e) -> p d h e", e=DL)
                        for d in range(DL):
                            last = pool.tensor_tensor(o[:, d, :, :], spread(key[:, d, :], [P, HL, DL]), val, ALU.mult)
                        last.then_inc(pairs_ready, 1)
                    norms.on_pool(pool, g, 2, w["minus_half"])
                    norms.on_pool(pool, g, 3, w["minus_half"])
                    for e in range(1, NE):
                        pool.wait_ge(parts_ready, g * NE + (e + 1))
                        if e > 1:
                            pool.wait_ge(routed_added, g * (NE - 1) + (e - 1))
                        pool.tensor_tensor(routed, routed, part[:, e % 2, :], ALU.add).then_inc(routed_added, 1)

            @block.vector
            def _(dve):
                tt = nc.vector.tensor_tensor
                with dve.Fori(0, GROUPS) as g:
                    step = Chain(dve, dve_steps, g * STEPS)
                    banks4 = lambda b: ps[:, b, :].rearrange("p (i c) -> p i c", i=GT)

                    def normed(k):
                        dve.wait_ge(norm_ready, g * NORMS + (k + 1))

                    dve.wait_ge(den_in, g * 32 + 32)
                    nc.vector.reciprocal(den[:, :, :], den[:, :, :]).then_inc(den_inv, 1)
                    x3 = w["x3"][:, bass.ds(g * GT, GT), :]
                    step(tt(xo[:, :, :], x3, wide_row(w, "L0_xattn_a2_li1_b"), ALU.add))
                    for b in range(GB):
                        dve.wait_ge(inv_spread, g * GB + (b + 1))
                        tt(att[:, b, :, :].rearrange("p h s -> p (h s)"), w["attended"][:, bass.ds(g * GB + b, 1), :].rearrange("p o n -> p (o n)"),
                           ps[:, b % 4, :], ALU.mult).then_inc(att_out, 1)
                    dve.wait_ge(att_out, g * GB + GB)
                    step(nc.vector.memset(att[0:1, :, :, :], 1.0))
                    nc.vector.memset(att[CY:CY + 1, :, :, :], 1.0).then_inc(att_ready, 1)
                    dve.wait_ge(projected, g + 1)
                    step(tt(xo[:, :, :], xo[:, :, :], banks4(4), ALU.add))
                    norms.on_vector(dve, step, g, 0, n0, xo).then_inc(norm_ready, 1)
                    normed(0)
                    dve.wait_ge(x0_in, g * 16 + 16)
                    step(tt(xo[:, :, :], xo[:, :, :], x3, ALU.add))
                    step(tt(xo[:, :, :], xo[:, :, :], wide_row(w, "L0_xattn_a2_li3_b"), ALU.add))
                    dve.wait_ge(mlp_done, g + 1)
                    step(tt(xo[:, :, :], xo[:, :, :], banks4(5), ALU.add))
                    step(tt(xo[:, :, :], xo[:, :, :], x0[:, :, :], ALU.add))
                    norms.on_vector(dve, step, g, 1, n0, xo).then_inc(norm_ready, 1)
                    normed(1)
                    for i in range(GT):
                        dve.wait_ge(qkvz_filled, g * GT + (i + 1))
                        last = tt(qkvz[:, i, :, :].rearrange("p k c -> p (k c)"), ps[:, i, :], w["qkvz_b"][:, :, :].rearrange("p k c -> p (k c)"), ALU.add)
                        if i < GT - 1:
                            last.then_inc(qkvz_out, 1)
                        else:
                            last.then_inc(qkvz_ready, 1)
                    dve.wait_ge(qkvz_ready, g + 1)
                    dve.wait_ge(prev_filled, g + 1)
                    step(nc.vector.tensor_scalar(q2b[:, :, :], banks4(4), float(DL) ** -0.5, None, ALU.mult))
                    step(nc.vector.tensor_scalar(q2[:, :, :], q2b[:, :, :], 0.02, None, ALU.mult))
                    step(tt(q2[:, :, :], q2[:, :, :], q2b[:, :, :], ALU.min))

                    def contract(n, q, dst):
                        dve.wait_ge(pairs_summed, g * 2 * GT + (n + 1))
                        b = 2 * (n % 2)
                        for d in range(DL):
                            s = ps[:, b + d // 4, C * (d % 4):C * (d % 4) + C].rearrange("p (h e) -> p h e", e=DL)
                            last = tt(prods[:, d, :].rearrange("p (h e) -> p h e", e=DL), s, spread(q.rearrange("p (h d) -> p d h", d=DL)[:, d, :], [P, HL, DL]), ALU.mult)
                        last.then_inc(sums_read, 1)
                        dve.wait_ge(sums_read, g * 2 * GT + (n + 1))
                        return nc.vector.tensor_reduce(dst, prods[:, :, :].rearrange("p d c -> p c d"), AX.X, ALU.add)

                    dve.wait_ge(shifted_up, g + 1)
                    for i in range(GT):
                        step(contract(i, qkvz[:, i, 0, :], o1[:, i, :]))
                        tt(err[:, i, :], ps[:, 5, C * i:C * i + C], o1[:, i, :], ALU.subtract).then_inc(err_ready, 1)
                    for i in range(GT):
                        step(contract(GT + i, q2[:, i, :], o2[:, i, :]))
                    tt(n0[:, :, :], o1[:, :, :], o2[:, :, :], ALU.add).then_inc(norm_ready_y, 1)
                    step(tt(xo[:, :, :], xo[:, :, :], wide_row(w, "L0_attn_bp"), ALU.add))
                    dve.wait_ge(lin_done, g + 1)
                    step(tt(xo[:, :, :], xo[:, :, :], banks4(5), ALU.add))
                    step(norms.on_vector(dve, step, g, 2, n0, xo))
                    norms.on_vector(dve, step, g, 3, n0, n0).then_inc(norm_ready, 1)

                    dve.wait_ge(logits_filled, g + 1)
                    logits = ps[:, 1, 0:GT * NE].rearrange("p (i e) -> p i e", i=GT)
                    step(nc.vector.tensor_reduce(logit_max[:, :], logits, AX.X, ALU.max))
                    tt(shifted_l[:, :, :], logits, spread(logit_max[:, :], [P, GT, NE]), ALU.subtract).then_inc(logits_shifted, 1)
                    dve.wait_ge(logits_shifted, g + 1)
                    step(nc.vector.tensor_scalar(rank[:, :, :], shifted_l[:, :, :], 0.0, None, ALU.is_equal))
                    step(tt(rank[:, :, :], rank[:, :, :], w["iota_down"][:, :].unsqueeze(1).broadcast_to([P, GT, NE]), ALU.mult))
                    step(nc.vector.tensor_reduce(best[:, :], rank[:, :, :], AX.X, ALU.max))
                    tt(onehot[:, :, :], rank[:, :, :], spread(best[:, :], [P, GT, NE]), ALU.is_equal).then_inc(chosen, 1)
                    dve.wait_ge(logits_exped, g + 1)
                    step(nc.vector.tensor_reduce(den_l[:, :], exp_l[:, :, :], AX.X, ALU.add))
                    step(nc.vector.reciprocal(top[:, :], den_l[:, :]))
                    for e in range(NX):
                        dve.wait_ge(down_filled, g * NX + (e + 1))
                        bank = ps[:, 4 + e % 2, :]
                        if e == 0:
                            nc.vector.tensor_scalar(shared[:, :], bank, w["s2"][:, 0:1], None, ALU.mult).then_inc(down_out, 1)
                        else:
                            if e >= 4:
                                dve.wait_ge(routed_added, g * (NE - 1) + (e - 3))
                            nc.vector.scalar_tensor_tensor(out=routed if e == 1 else part[:, (e - 1) % 2, :], in0=bank, scalar=w["s2"][:, e:e + 1],
                                                           in1=gate[:, e - 1, :], op0=ALU.mult, op1=ALU.mult).then_inc(parts_ready, 1)
                    dve.wait_ge(out_turned, g + 1)
                    step(tt(xo[:, :, :], xo[:, :, :], banks4(6), ALU.add))
                    for i in range(GT):
                        last = nc.vector.scalar_tensor_tensor(out=final[:, i, :], in0=ps[:, 7, C * i:C * i + C], scalar=top[:, i:i + 1],
                                                              in1=xo[:, i, :], op0=ALU.mult, op1=ALU.add)
                    last.then_inc(out_ready, 1)
                    dve.wait_ge(out_ready, g + 1)
                    dve.wait_ge(out_stored, g * 16 + 16)
                    dve.sem_inc(pass_done, 1)
                    assert step.n == STEPS, step.n

            @block.scalar
            def _(act):
                act.sem_inc(pass_done, 1)
                with act.Fori(0, GROUPS) as g:
                    def features(k, **affine):
                        act.wait_ge(turned, g * 4 + (k + 1))
                        act.activation(nT[:, :], ps[:, 0, :], ACT.Identity, **affine).then_inc(nT_ready, 1)

                    features(0, scale=vec("L0_xattn_a2_ln3_g"), bias=vec("L0_xattn_a2_ln3_b"))
                    for f in range(FT):
                        act.wait_ge(hid_filled, g * FT + (f + 1))
                        act.activation(hid[:, f, :], ps[:, 1 + f, :], ACT.Gelu, bias=w["li2_b"]["a2"][:, f:f + 1]).then_inc(hid_ready, 1)
                    features(1)
                    act.wait_ge(qkvz_ready, g + 1)
                    act.activation(qkvz[:, :, 3, :], qkvz[:, :, 3, :], ACT.Sigmoid, scale=0.02 * INV).then_inc(sig_ready, 1)
                    features(2)
                    features(3, scale=vec("L0_ffn_ln_gamma"), bias=vec("L0_ffn_ln_beta"))
                    act.wait_ge(logits_shifted, g + 1)
                    act.activation(exp_l[:, :, :], shifted_l[:, :, :], ACT.Exp).then_inc(logits_exped, 1)

                    def up(e):
                        for k in range(2):
                            n = 2 * e + k
                            act.wait_ge(up_filled, g * 2 * NX + (n + 1))
                            if e >= 2:
                                act.wait_ge(down_filled, g * NX + (e - 1))
                            act.activation(act1[:, e % 2, k, :], ps[:, 2 + n % 2, :], ACT.Silu, scale=w["s1"][:, n:n + 1]).then_inc(up_ready, 1)

                    up(0)
                    for e in range(NE):
                        act.wait_ge(gate_filled, g * NE + (e + 1))
                        act.copy(gate[:, e, :], ps[:, 6 + e % 2, :]).then_inc(gate_ready, 1)
                        up(e + 1)

            @block.tensor
            def _(pe):
                with pe.Fori(0, GROUPS) as g:
                    ident = w["ident"]
                    pe.wait_ge(pass_done, g + 1)

                    def turn(src, ready, count, k):
                        pe.wait_ge(ready, count)
                        for i in range(GT):
                            last = nc.tensor.transpose(ps[:, 0, P * i:P * i + P], src[:, i, :], ident[:, :])
                        last.then_inc(turned, 1)
                        pe.wait_ge(nT_ready, g * 4 + (k + 1))

                    pe.wait_ge(inv_in, g * 32 + 32)
                    for b in range(GB):
                        if b >= 4:
                            pe.wait_ge(att_out, g * GB + (b - 3))
                        nc.tensor.matmul(ps[:, b % 4, :], w["sel"][:, :, :].rearrange("p u c -> p (u c)"),
                                         w["attended"][:, bass.ds(g * GB + b, 1), :].rearrange("p o n -> p (o n)"), start=True, stop=True).then_inc(inv_spread, 1)
                    pe.wait_ge(att_ready, g + 1)
                    for p in range(GT):
                        for k in range(H // 2):
                            for u in range(2):
                                last = nc.tensor.matmul(ps[S * u:S * u + S, 4, C * p:C * p + C], att[:, 2 * p + u, k, :], w["value_fold"][:, k, :],
                                                        start=(k == 0), stop=(k == H // 2 - 1))
                    last.then_inc(projected, 1)
                    turn(n0, norm_ready, g * NORMS + 1, 0)
                    for f in range(FT):
                        nc.tensor.matmul(ps[:, 1 + f, :], w["li2"]["a2"][:, P * f:P * f + P], nT[:, :], start=True, stop=True).then_inc(hid_filled, 1)
                    pe.wait_ge(hid_ready, g * FT + FT)
                    for i in range(GT):
                        for f in range(FT):
                            last = nc.tensor.matmul(ps[:, 5, C * i:C * i + C], hid[:, f, P * i:P * i + P], w["li3"]["a2"][:, f, :],
                                                    start=(f == 0), stop=(f == FT - 1))
                    last.then_inc(mlp_done, 1)

                    turn(n0, norm_ready, g * NORMS + 2, 1)
                    for i in range(GT):
                        nc.tensor.matmul(ps[:, i, :], nT[:, P * i:P * i + P], w["qkvz"][:, :, :].rearrange("p k c -> p (k c)"),
                                         start=True, stop=True).then_inc(qkvz_filled, 1)
                    nc.tensor.matmul(ps[:, 5, :], w["next"][:, :], n0[:, :, :].rearrange("p i c -> p (i c)"), start=True, stop=True).then_inc(shifted_up, 1)
                    pe.wait_ge(qkvz_ready, g + 1)
                    nc.tensor.matmul(ps[:, 4, :], w["prev"][:, :], qkvz[:, :, 0, :], start=True, stop=True).then_inc(prev_filled, 1)
                    for n in range(2 * GT):
                        pe.wait_ge(pairs_ready, g * 2 * GT + (n + 1))
                        if n >= 2:
                            pe.wait_ge(sums_read, g * 2 * GT + (n - 1))
                        tri = w["upto"] if n < GT else w["before"]
                        for k in range(2):
                            last = nc.tensor.matmul(ps[:, 2 * (n % 2) + k, :], tri[:, :], pairs[:, n % 2, 4 * k:4 * k + 4, :].rearrange("p d c -> p (d c)"),
                                                    start=True, stop=True)
                        last.then_inc(pairs_summed, 1)
                    pe.wait_ge(sums_read, g * 2 * GT + 2 * GT)
                    turn(n0, norm_ready_y, g + 1, 2)
                    for i in range(GT):
                        last = nc.tensor.matmul(ps[:, 5, C * i:C * i + C], nT[:, P * i:P * i + P], w["wp"][:, :], start=True, stop=True)
                    last.then_inc(lin_done, 1)

                    turn(n0, norm_ready, g * NORMS + 3, 3)
                    for i in range(GT):
                        last = nc.tensor.matmul(ps[:, 1, NE * i:NE * i + NE], nT[:, P * i:P * i + P], w["router"][:, :], start=True, stop=True)
                    last.then_inc(logits_filled, 1)

                    def up(e):
                        for k in range(2):
                            n = 2 * e + k
                            if n >= 2:
                                pe.wait_ge(up_ready, g * 2 * NX + (n - 1))
                            nc.tensor.matmul(ps[:, 2 + n % 2, :], w["t1T"][:, n, :], nT[:, :], start=True, stop=True).then_inc(up_filled, 1)

                    def down(e):
                        pe.wait_ge(up_ready, g * 2 * NX + (2 * e + 2))
                        if e == 2:
                            pe.wait_ge(down_out, g + 1)
                        elif e >= 3:
                            pe.wait_ge(parts_ready, g * NE + (e - 2))
                        for k in range(2):
                            last = nc.tensor.matmul(ps[:, 4 + e % 2, :], w["t2T"][:, 2 * e + k, :], act1[:, e % 2, k, :], start=(k == 0), stop=(k == 1))
                        last.then_inc(down_filled, 1)

                    up(0)
                    pe.wait_ge(chosen, g + 1)
                    for e in range(NE):
                        if e >= 2:
                            pe.wait_ge(gate_ready, g * NE + (e - 1))
                        for i in range(GT):
                            last = nc.tensor.matmul(ps[:, 6 + e % 2, P * i:P * i + P], onehot[:, i, e:e + 1].broadcast_to([P, P]), w["ident16"][:, :],
                                                    start=True, stop=True)
                        last.then_inc(gate_filled, 1)
                        up(e + 1)
                        if e == 1:
                            pe.wait_ge(gate_ready, g * NE + 1)
                        down(e)
                    down(NE)
                    pe.wait_ge(gate_ready, g * NE + NE)
                    pe.wait_ge(down_out, g + 1)
                    for i in range(GT):
                        nc.tensor.transpose(ps[:, 6, P * i:P * i + P], shared[:, P * i:P * i + P], ident[:, :])
                    pe.wait_ge(routed_added, g * (NE - 1) + (NE - 1))
                    for i in range(GT):
                        last = nc.tensor.transpose(ps[:, 7, P * i:P * i + P], routed[:, P * i:P * i + P], ident[:, :])
                    last.then_inc(out_turned, 1)


_OUT = ((B, S, C), "float32")


def kernel(**inputs):
    import numpy as np
    import concourse.bacc as bacc
    from concourse.bass_utils import run_bass_kernel_spmd

    nc = bacc.Bacc("TRN2", target_bir_lowering=False, num_devices=1)
    arrays, args = {}, {}
    for name, value in inputs.items():
        value = np.ascontiguousarray(value)
        arrays[f"in_{name}"] = value
        args[name] = nc.dram_tensor(f"in_{name}", value.shape, mybir.dt.from_np(value.dtype), kind="ExternalInput").ap()
    out = nc.dram_tensor("out_x", _OUT[0], mybir.dt.from_np(np.dtype(_OUT[1])), kind="ExternalOutput").ap()
    perceiver_kernel(nc, args, out)
    r = run_bass_kernel_spmd(nc, [arrays], core_ids=[0])
    return r.results[0]["out_x"]
```

```python
from contextlib import ExitStack

import concourse.bass as bass
from concourse import mybir

F32 = mybir.dt.float32
F16 = mybir.dt.float16
ALU = mybir.AluOpType
ACT = mybir.ActivationFunctionType
AX = mybir.AxisListType

P = 128
B, S, C = 32, 64, 128
T, CY = 1601, 64
H, D = 16, 32
TOK = B * S
GROUPS = 4
GB = B // GROUPS
GT = GB * S // P
GN = GB * S
FF = 4 * C
FT = FF // P
HL, DL = 16, 8
NE, FE = 8, 256
NX = NE + 1
EPS = 1e-5
MAGIC_MIN_SCALE = 1e-5
SCORE_SCALE = float(D) ** -0.5
QUERY_SCALE = 0.125
TJ = (T + P - 1) // P
TLAST = T - (TJ - 1) * P
HB = 4
HS = H * S


class Chain:

    def __init__(self, eng, sem, base):
        self.eng, self.sem, self.base, self.n = eng, sem, base, 0

    def __call__(self, ins):
        self.n += 1
        ins.then_inc(self.sem, 1)
        self.eng.wait_ge(self.sem, self.base + self.n)


def spread(ap, shape):
    return ap.unsqueeze(len(ap.shape)).broadcast_to(shape)


def perceiver_kernel(nc, a, out):
    with ExitStack() as whole:
        def sb(name, shape, dt=F32, scope=whole):
            return scope.enter_context(nc.sbuf_tensor(name, shape, dt))

        ps = whole.enter_context(nc.psum_tensor("banks", [P, 8, 512], F32))
        w = {}
        w["ident"] = sb("ident", [P, P])
        w["ident16"] = sb("ident16", [P, P], F16)
        w["minus_half"] = sb("minus_half", [P, 16])
        names = ["a1_lnx_g", "a1_lnx_b", "a1_lny_g", "a1_lny_b", "a1_ln3_g", "a1_ln3_b",
                 "a2_lnx_g", "a2_lnx_b", "a2_ln3_g", "a2_ln3_b"]
        w["vec"] = sb("vec", [P, 32])
        w["vec_of"] = {"L0_xattn_" + n: i for i, n in enumerate(names)}
        w["vec_of"].update({"L0_ffn_ln_gamma": 10, "L0_ffn_ln_beta": 11,
                            "L0_xattn_a2_lny_g": 12, "L0_xattn_a2_lny_b": 13})
        w["li2_b"] = {n: sb(f"li2_b_{n}", [P, FT]) for n in ("a1", "a2")}
        rows = ["xattn_ln1_g", "xattn_ln1_b", "xattn_ln2_g", "xattn_ln2_b", "xattn_a1_li1_b", "xattn_a1_li3_b",
                "xattn_a2_li1_b", "xattn_a2_li3_b", "attn_bp"]
        w["row"] = sb("row", [P, len(rows), C])
        w["row_of"] = {"L0_" + n: i for i, n in enumerate(rows)}
        w["qkvz_b"] = sb("qkvz_b", [P, 4, C])
        w["li2"] = {n: sb(f"li2_{n}", [P, FF]) for n in ("a1", "a2")}
        w["li3"] = {n: sb(f"li3_{n}", [P, FT, C]) for n in ("a1", "a2")}
        w["query_fold"] = sb("query_fold", [P, H, 2, CY])
        w["value_fold"] = sb("value_fold", [P, H // 2, C])
        w["qkvz"] = sb("qkvz", [P, 4, C])
        w["wp"] = sb("wp", [P, C])
        w["upto"] = sb("upto", [P, P])
        w["before"] = sb("before", [P, P])
        w["prev"] = sb("prev", [P, P])
        w["next"] = sb("next", [P, P])
        w["sel"] = sb("sel", [P, 2, CY])
        w["later"] = sb("later", [P, S])
        w["t1T"] = sb("t1T", [P, 2 * NX, P])
        w["t2T"] = sb("t2T", [P, 2 * NX, P])
        w["s1"] = sb("s1", [P, 2 * NX])
        w["s2"] = sb("s2", [P, NX])
        w["router"] = sb("router", [P, NE])
        w["iota_down"] = sb("iota_down", [P, NE])
        w["x3"] = sb("x3", [P, TOK // P, C])
        w["xqT"] = sb("xqT", [P, TOK])

        with ExitStack() as scope:
            w["key_fold"] = sb("key_fold", [P, H, C], F32, scope)
            w["value_fold1"] = sb("value_fold1", [P, 2, H // 2, C], F32, scope)
            with ExitStack() as inner:
                prepare_weights(nc, a, w, ps, lambda n, s, d=F32: sb("prep_" + n, s, d, inner))
            with ExitStack() as inner:
                latent_self_attention(nc, a, w, ps, lambda n, s, d=F32: sb("self_" + n, s, d, inner))
        w["attended"] = sb("attended", [P, B, 512])
        with ExitStack() as inner:
            cross_attention(nc, a, w, ps, lambda n, s, d=F32: sb("cross_" + n, s, d, inner))
        with ExitStack() as inner:
            finish_tokens(nc, a, out, w, ps, lambda n, s, d=F32: sb("fin_" + n, s, d, inner))


def prepare_weights(nc, a, w, ps, sb):
    with ExitStack() as ctx:
        sem = lambda n: ctx.enter_context(nc.semaphore("p_" + n))
        wide = {n: sb(f"w_{n}", [P, H, D]) for n in ("a1_wq", "a1_wk", "a1_wv", "a2_wq")}
        narrow = {n: sb(f"w_{n}", [CY, H, D]) for n in ("a2_wk", "a2_wv")}
        narrow_g = {n: sb(f"wg_{n}", [CY, H, D]) for n in ("a2_wk", "a2_wv")}
        turned = {n: sb(f"t_{n}", [P, 4, P]) for n in wide}
        turned_raw = {n: sb(f"tr_{n}", [P, 4, CY]) for n in narrow}
        key_turned = sb("key_turned", [P, 4, 2, CY])
        value_turned = sb("value_turned", [P, 4, CY])
        li1 = {n: sb(f"li1_{n}", [P, 4, C]) for n in ("a1", "a2")}
        w1 = sb("w1", [P, 2 * NX, C])
        w2 = sb("w2", [P, NX, FE])
        low1 = sb("low1", [P, 2 * NX, C])
        low2 = sb("low2", [P, NX, FE])
        half1 = sb("half1", [P, 2 * NX])
        half2 = sb("half2", [P, NX])
        neg1 = sb("neg1", [P, 2 * NX])
        neg2 = sb("neg2", [P, NX])
        router_rows = sb("router_rows", [NE, C])
        NT = TOK // P
        x = sb("x", [P, NT, C])
        n0 = sb("n0", [P, NT, C])
        var_ready, rstd_ready, x_in, x_normed = sem("var_ready"), sem("rstd_ready"), sem("x_in"), sem("x_normed")
        ln1_in = sem("ln1_in")
        norms = Norms(nc, sb, var_ready, rstd_ready, 3, "p", NT)
        attn_in, ffn_in, vec_in, rest_in = sem("attn_in"), sem("ffn_in"), sem("vec_in"), sem("rest_in")
        pool_steps = sem("pool_steps")
        dve_steps = sem("dve_steps")
        scaled, tern1, tern2 = sem("scaled"), sem("tern1"), sem("tern2")
        filled, by_act, by_dve = sem("filled"), sem("by_act"), sem("by_dve")
        attn_n = [0]
        ffn_n = [0]
        vec_n = [0]
        rest_n = [0]

        items = [("turn_wide", n) for n in wide] + [("turn_narrow", n) for n in narrow]
        items += [("value_bias", None)]
        items += [(k, r) for r in range(4) for k in ("key_fold", "value_fold1", "query_fold", "value_fold")]
        items += [("turn_x", q) for q in range(NT // 4)] + [("router", None)]
        items += [("t1", q) for q in range(5)] + [("t2", q) for q in range(5)]

        NARROW = 3
        assert [n for n, (kind, k) in enumerate(items) if kind in ("turn_narrow", "value_bias")] == [4, 5, 6]

        def wait_taken(eng, n):
            if n >= 4:
                eng.wait_ge(by_dve, min(n - 3, NARROW))
            eng.wait_ge(by_act, n + 1 if n < 4 else max(4, n + 1 - NARROW))

        with nc.Block() as block:
            @block.sync
            def _(sp):
                sp.dma_start(x[:, :, :], a["x"].rearrange("(i b) s c -> (b s) i c", b=2)).then_inc(x_in, 16)
                for n in ("L0_xattn_ln1_g", "L0_xattn_ln1_b"):
                    sp.dma_start(w["row"][:, w["row_of"][n], :], a[n].partition_broadcast(P)).then_inc(ln1_in, 16)
                for n, t in list(wide.items()) + list(narrow.items()):
                    sp.dma_start(t[:, :, :], a["L0_xattn_" + n].rearrange("h c d -> c h d")).then_inc(attn_in, 16)
                    attn_n[0] += 16
                for n, t in li1.items():
                    sp.dma_start(t[:, :, :], a[f"L0_xattn_{n}_li1_w"].rearrange("(k p) c -> p k c", p=P)).then_inc(attn_in, 16)
                    attn_n[0] += 16
                sp.dma_start(w1[:, 0:2, :], a["L0_ffn_shared_w1"].rearrange("(k p) d -> p k d", p=P)).then_inc(ffn_in, 16)
                sp.dma_start(w1[:, 2:, :], a["L0_ffn_expert_w1"].rearrange("e (k p) d -> p (e k) d", p=P)).then_inc(ffn_in, 16)
                sp.dma_start(w2[:, 0, :], a["L0_ffn_shared_w2"]).then_inc(ffn_in, 16)
                sp.dma_start(w2[:, 1:, :], a["L0_ffn_expert_w2"].rearrange("e d f -> d e f")).then_inc(ffn_in, 16)
                sp.dma_start(router_rows[:, :], a["L0_ffn_router_w"]).then_inc(ffn_in, 16)
                ffn_n[0] = 80
                for n in ("a1", "a2"):
                    sp.dma_start(w["li2"][n][:, :], a[f"L0_xattn_{n}_li2_w"]).then_inc(rest_in, 16)
                    sp.dma_start(w["li3"][n][:, :, :], a[f"L0_xattn_{n}_li3_w"].rearrange("(k p) c -> p k c", p=P)).then_inc(rest_in, 16)
                    rest_n[0] += 32
                for k, n in enumerate(("Wq", "Wk1", "Wv", "Wk2")):
                    sp.dma_start(w["qkvz"][:, k, :], a["L0_attn_" + n]).then_inc(rest_in, 16)
                    rest_n[0] += 16
                sp.dma_start(w["wp"][:, :], a["L0_attn_Wp"]).then_inc(rest_in, 16)
                rest_n[0] += 16
                for n in ("a1", "a2"):
                    for f in range(FT):
                        src = a[f"L0_xattn_{n}_li2_b"][P * f:P * f + P]
                        sp.dma_start(w["li2_b"][n][:, f:f + 1], src.unsqueeze(1)).then_inc(rest_in, 16)
                        rest_n[0] += 16
                for n, i in w["row_of"].items():
                    if n in ("L0_xattn_ln1_g", "L0_xattn_ln1_b"):
                        continue
                    sp.dma_start(w["row"][:, i, :], a[n].partition_broadcast(P)).then_inc(rest_in, 16)
                    rest_n[0] += 16
                for k, n in enumerate(("bq", "bk1", "bv", "bk2")):
                    sp.dma_start(w["qkvz_b"][:, k, :], a["L0_attn_" + n].partition_broadcast(P)).then_inc(rest_in, 16)
                    rest_n[0] += 16
                sp.wait_ge(rest_in, rest_n[0])

            @block.scalar
            def _(act):
                for n, i in w["vec_of"].items():
                    src = a[n]
                    act.dma_start(w["vec"][0:src.shape[0], i:i + 1], src.unsqueeze(1)).then_inc(vec_in, 16)
                    vec_n[0] += 16
                for n, (kind, k) in enumerate(items):
                    if n in (4, 5, 6):
                        continue
                    act.wait_ge(filled, n + 1)
                    bank = ps[:, n % 4, :]
                    four = bank.rearrange("p (k c) -> p k c", k=4)
                    if kind == "turn_wide":
                        last = act.copy(turned[k][:, :, :], four)
                    elif kind == "key_fold":
                        last = act.copy(w["key_fold"][:, :, :].rearrange("p (q r) c -> p q r c", r=4)[:, :, k, :], four)
                    elif kind == "value_fold1":
                        last = act.copy(w["value_fold1"][:, k % 2, k // 2::2, :], four)
                    elif kind == "query_fold":
                        dst = w["query_fold"][:, :, :, :].rearrange("p (q r) u c -> p q r (u c)", r=4)[:, :, k, :]
                        last = act.copy(dst, four)
                    elif kind == "value_fold":
                        dst = w["value_fold"][:, :, :].rearrange("p (q r) c -> p q r c", r=4)[:, :, k, :]
                        last = act.copy(dst, bank[:, 0:2 * C].rearrange("p (k c) -> p k c", k=2))
                    elif kind == "turn_x":
                        last = act.copy(w["xqT"][:, 4 * P * k:4 * P * k + 4 * P], bank)
                    elif kind == "router":
                        last = act.copy(w["router"][:, :], bank[:, 0:NE])
                    else:
                        m = min(4, 2 * NX - 4 * k)
                        last = act.copy(w[kind + "T"][:, 4 * k:4 * k + m, :], four[:, 0:m, :])
                    last.then_inc(by_act, 1)

            @block.gpsimd
            def _(pool):
                step = Chain(pool, pool_steps, 0)

                def blocks(name):
                    return w[name][:, :].rearrange("p (b j) -> p b j", b=2)

                def keep(name, op, base, pattern, mult, fill=0.0, ap=None):
                    v = blocks(name) if ap is None else ap
                    step(pool.affine_select(out=v, in_=v, compare_op=op, fill=fill, base=base, pattern=pattern,
                                            channel_multiplier=mult))

                step(pool.memset(w["ident"][:, :], 0.0))
                keep("ident", ALU.not_equal, 0, [[-1, P]], 1, 1.0, w["ident"][:, :])
                step(pool.tensor_copy(w["ident16"][:, :], w["ident"][:, :]))
                step(pool.memset(w["minus_half"][:, :], -0.5))
                for k in range(3):
                    norms.on_pool(pool, 0, k, w["minus_half"])
                for name, base in (("upto", 0), ("before", -1)):
                    step(pool.memset(w[name][:, :], 1.0))
                    keep(name, ALU.is_ge, base, [[64, 2], [1, 64]], -1)
                    keep(name, ALU.is_ge, 0, [[-64, 2], [0, 64]], 1)
                step(pool.memset(w["prev"][:, :], 0.0))
                keep("prev", ALU.not_equal, 1, [[-64, 2], [-1, 64]], 1, 1.0)
                keep("prev", ALU.is_ge, 0, [[-64, 2], [0, 64]], 1)
                step(pool.memset(w["next"][:, :], 0.0))
                keep("next", ALU.not_equal, -1, [[-64, 2], [-1, 64]], 1, 1.0)
                keep("next", ALU.is_ge, 63, [[64, 2], [0, 64]], -1)
                step(pool.memset(w["sel"][:, :, :], 0.0))
                step(pool.affine_select(out=w["sel"][:, :, :], in_=w["sel"][:, :, :], compare_op=ALU.not_equal, fill=1.0,
                                        base=0, pattern=[[-64, 2], [0, CY]], channel_multiplier=1))
                step(pool.memset(w["later"][:, :], 1.0))
                for p0 in (0, S):
                    v = w["later"][p0:p0 + S, :]
                    step(pool.affine_select(out=v, in_=v, compare_op=ALU.is_ge, fill=0.0, base=-1,
                                            pattern=[[1, S]], channel_multiplier=-1))
                for e in range(NE):
                    step(pool.memset(w["iota_down"][:, e:e + 1], float(NE - e)))

            @block.vector
            def _(dve):
                step = Chain(dve, dve_steps, 0)
                dve.wait_ge(x_in, 16)
                step(norms.on_vector(dve, step, 0, 0, n0, x))
                dve.wait_ge(attn_in, attn_n[0])
                dve.wait_ge(vec_in, vec_n[0])
                g_y = w["vec_of"]["L0_xattn_a2_lny_g"]
                for n in narrow:
                    nc.vector.tensor_scalar(narrow_g[n][:, :, :], narrow[n][:, :, :], w["vec"][0:CY, g_y:g_y + 1], None,
                                            ALU.mult).then_inc(scaled, 1)

                def ternary(wide_w, low, scale, half, neg, n, width, done, scaled_too=False):
                    step(nc.vector.tensor_reduce(half[:, :], wide_w[:, :, :], AX.X, ALU.add, apply_absolute_value=True))
                    step(nc.vector.tensor_scalar(scale[:, :], half[:, :], 1.0 / width, MAGIC_MIN_SCALE, ALU.mult, ALU.max))
                    step(nc.vector.tensor_scalar(half[:, :], scale[:, :], 0.5, None, ALU.mult))
                    step(nc.vector.tensor_scalar(neg[:, :], scale[:, :], -0.5, None, ALU.mult))
                    step(nc.vector.tensor_tensor(low[:, :, :], wide_w[:, :, :], spread(neg[:, :], [P, n, width]), ALU.is_lt))
                    step(nc.vector.tensor_tensor(wide_w[:, :, :], wide_w[:, :, :], spread(half[:, :], [P, n, width]), ALU.is_gt))
                    last = nc.vector.tensor_tensor(wide_w[:, :, :], wide_w[:, :, :], low[:, :, :], ALU.subtract)
                    if scaled_too:
                        step(last)
                        last = nc.vector.tensor_tensor(wide_w[:, :, :], wide_w[:, :, :], spread(scale[:, :], [P, n, width]), ALU.mult)
                    last.then_inc(done, 1)

                for n, (kind, k) in enumerate(items):
                    if n not in (4, 5, 6):
                        continue
                    dve.wait_ge(filled, n + 1)
                    bank = ps[:, n % 4, :]
                    if kind == "turn_narrow":
                        raw = turned_raw[k]
                        step(nc.vector.tensor_copy(raw[:, :, :], bank[:, 0:4 * CY].rearrange("p (k c) -> p k c", k=4)))
                        for q in range(4):
                            for u in range(2 if k == "a2_wk" else 1):
                                dst = key_turned[:, q, u, :] if k == "a2_wk" else value_turned[:, q, :]
                                last = nc.vector.tensor_scalar(dst, raw[:, q, :], raw[:, q, 0:1],
                                                               QUERY_SCALE if k == "a2_wk" else 1.0, ALU.subtract, ALU.mult)
                    else:
                        dve.wait_ge(by_dve, n - 4)
                        last = nc.vector.tensor_copy(value_turned[:, :, 0], bank[:, 0:4])
                    last.then_inc(by_dve, 1)
                step(norms.on_vector(dve, step, 0, 1, n0, n0))
                dve.wait_ge(ln1_in, 32)
                step(nc.vector.tensor_tensor(n0[:, :, :], n0[:, :, :], wide_row(w, "L0_xattn_ln1_g", NT), ALU.mult))
                step(nc.vector.tensor_tensor(w["x3"][:, :, :], n0[:, :, :], wide_row(w, "L0_xattn_ln1_b", NT), ALU.add))
                norms.on_vector(dve, step, 0, 2, n0, w["x3"]).then_inc(x_normed, 1)
                dve.wait_ge(ffn_in, ffn_n[0])
                ternary(w1, low1, w["s1"], half1, neg1, 2 * NX, C, tern1)
                ternary(w2, low2, w["s2"], half2, neg2, NX, FE, tern2, scaled_too=True)
                dve.wait_ge(tern2, 1)

            @block.tensor
            def _(pe):
                pe.wait_ge(attn_in, attn_n[0])
                pe.wait_ge(pool_steps, 2)
                ident = w["ident"]
                for n, (kind, k) in enumerate(items):
                    if n >= 4:
                        wait_taken(pe, n - 4)
                    bank = ps[:, n % 4, :]
                    four = bank.rearrange("p (k c) -> p k c", k=4)
                    r0 = 32 * k if isinstance(k, int) and k < 4 else 0
                    if kind == "turn_wide":
                        flat = wide[k][:, :, :].rearrange("p (q r) d -> p q (r d)", q=4)
                        for q in range(4):
                            last = nc.tensor.transpose(four[:, q, :], flat[:, q, :], ident[:, :])
                    elif kind == "turn_narrow":
                        pe.wait_ge(scaled, 2)
                        flat = narrow_g[k][:, :, :].rearrange("p (q r) d -> p q (r d)", q=4)
                        for q in range(4):
                            last = nc.tensor.transpose(bank[:, CY * q:CY * q + CY], flat[:, q, :], ident[0:CY, 0:CY])
                    elif kind == "value_bias":
                        pe.wait_ge(vec_in, vec_n[0])
                        flat = narrow["a2_wv"][:, :, :].rearrange("p (q r) d -> p q (r d)", q=4)
                        b_y = w["vec_of"]["L0_xattn_a2_lny_b"]
                        for q in range(4):
                            last = nc.tensor.matmul(bank[:, q:q + 1], flat[:, q, :], w["vec"][0:CY, b_y:b_y + 1], start=True, stop=True)
                    elif kind == "router":
                        pe.wait_ge(ffn_in, ffn_n[0])
                        last = nc.tensor.transpose(bank[:, 0:NE], router_rows[:, :], ident[0:NE, 0:NE])
                    elif kind == "turn_x":
                        pe.wait_ge(x_normed, 1)
                        for q in range(4):
                            last = nc.tensor.transpose(four[:, q, :], n0[:, 4 * k + q, :], ident[:, :])
                    elif kind in ("t1", "t2"):
                        pe.wait_ge(tern1 if kind == "t1" else tern2, 1)
                        src = w1[:, :, :] if kind == "t1" else w2[:, :, :].rearrange("p e (k f) -> p (e k) f", k=2)
                        for q in range(min(4, 2 * NX - 4 * k)):
                            last = nc.tensor.transpose(four[:, q, :], src[:, 4 * k + q, :], ident[:, :])
                    else:
                        wait_taken(pe, 6)
                        for q in range(4):
                            rows = slice(r0, r0 + D)
                            if kind == "key_fold":
                                o, l, r = four[:, q, :], turned["a1_wk"][rows, q, :], turned["a1_wq"][rows, q, :]
                            elif kind == "value_fold1":
                                o, l, r = four[:, q, :], turned["a1_wv"][rows, q, :], li1["a1"][rows, q, :]
                            elif kind == "query_fold":
                                o, l = four[:, q, :], turned["a2_wq"][rows, q, :]
                                r = key_turned[rows, q, :, :].rearrange("p u c -> p (u c)")
                            else:
                                o = ps[CY * (q // 2):CY * (q // 2) + CY, n % 4, C * (q % 2):C * (q % 2) + C]
                                l, r = value_turned[rows, q, :], li1["a2"][rows, q, :]
                            last = nc.tensor.matmul(o, l, r, start=True, stop=True)
                    last.then_inc(filled, 1)


class Norms:

    def __init__(self, nc, sb, var_ready, rstd_ready, per, tag, tiles=GT):
        self.nc, self.per, self.var_ready, self.rstd_ready, self.tiles = nc, per, var_ready, rstd_ready, tiles
        self.stats = sb("stats_" + tag, [P, tiles, 6])
        self.mv = sb("mv_" + tag, [P, tiles, 2])
        self.var = sb("var_" + tag, [P, tiles])
        self.rstd = sb("rstd_" + tag, [P, tiles])

    def moments(self, dve, step, src):
        nc = self.nc
        for i in range(self.tiles):
            last = nc.vector.bn_stats(self.stats[:, i, :], src[:, i, :])
        dve.drain()
        for i in range(self.tiles):
            last = nc.vector.bn_aggr(self.mv[:, i, :], self.stats[:, i, :])
        step(last)
        nc.vector.tensor_scalar(self.var[:, :], self.mv[:, :, 1], EPS, None, ALU.add).then_inc(self.var_ready, 1)

    def apply(self, dve, g, k, dst, src):
        dve.wait_ge(self.rstd_ready, g * self.per + (k + 1))
        for i in range(self.tiles):
            last = self.nc.vector.tensor_scalar(dst[:, i, :], src[:, i, :], self.mv[:, i, 0:1], self.rstd[:, i:i + 1],
                                                ALU.subtract, ALU.mult)
        return last

    def on_vector(self, dve, step, g, k, dst, src):
        self.moments(dve, step, src)
        return self.apply(dve, g, k, dst, src)

    def on_pool(self, pool, g, k, minus_half):
        pool.wait_ge(self.var_ready, g * self.per + (k + 1))
        pool.tensor_tensor(self.rstd[:, :], self.var[:, :], minus_half[:, 0:self.tiles], ALU.pow).then_inc(self.rstd_ready, 1)


def wide_row(w, name, tiles=GT):
    i = w["row_of"][name]
    return w["row"][:, i:i + 1, :].broadcast_to([P, tiles, C])


def latent_self_attention(nc, a, w, ps, sb):
    with ExitStack() as ctx:
        sem = lambda n: ctx.enter_context(nc.semaphore("s_" + n))
        n0 = sb("n0", [P, GT, C])
        xo = sb("xo", [P, GT, C])
        x3 = sb("x3_group", [P, GT, C])
        xnT = sb("xnT", [P, GN])
        ynT = sb("ynT", [P, GN])
        h3T = sb("h3T", [P, GN])
        keys = sb("keys", [P, GB, H, S])
        values = sb("values", [P, GB, H // 2, C])
        mx = sb("mx", [P, 2, H])
        den = sb("den", [P, 2, H])
        rden = sb("rden", [P, 2, H])
        prob = sb("prob", [P, 2, H, S])
        probT = sb("probT", [P, 2, H // 2, P])
        hid = sb("hid", [P, FT, GN])
        dve_steps = sem("dve_steps")
        var_ready, rstd_ready = sem("var_ready"), sem("rstd_ready")
        xy_ready = sem("xy_ready")
        items_filled, items_by_act, items_by_dve = sem("items_filled"), sem("items_by_act"), sem("items_by_dve")
        scored, shifted, exped, normed, masked = (sem("scored"), sem("shifted"), sem("exped"), sem("normed"), sem("masked"))
        probs_turned, probT_ready, attended_pair = sem("probs_turned"), sem("probT_ready"), sem("attended_pair")
        n3_ready, n3_turned, h3_ready = sem("n3_ready"), sem("n3_turned"), sem("h3_ready")
        hid_filled, hid_ready, mlp_done = sem("hid_filled"), sem("hid_ready"), sem("mlp_done")
        x3_ready, q_normed, q_turned, q_taken = sem("x3_ready"), sem("q_normed"), sem("q_turned"), sem("q_taken")
        NORMS = 3
        norms = Norms(nc, sb, var_ready, rstd_ready, NORMS, "s")
        STEPS = 23
        pairs = GT
        KEYS = H
        ITEMS = KEYS + 2 * GB
        TURN, SUMS = 7, 6
        HID = 4
        vec = lambda n: w["vec"][:, w["vec_of"]["L0_xattn_" + n]:w["vec_of"]["L0_xattn_" + n] + 1]
        item = lambda *ns: [("item", n) for n in range(*ns)]
        SCHEDULE = [("moments3",)] + item(0, 6) + [("apply3",)] + item(6, 7) + [("turn3",)] + item(7, 8) + [("hid", f) for f in range(FT)] + [("mlp",)]
        SCHEDULE += [("moments4",)] + item(8, 12) + [("apply4",), ("moments5",)] + item(12, 15) + [("apply5",), ("turnq",)] + item(15, KEYS)
        LAST = [s for s in SCHEDULE if s[0] != "item"]
        FIRST = item(0, KEYS)
        stage = lambda kind, p: [(kind, p)]
        ON_PE = stage("scores", 0) + stage("scores", 1) + item(16, 24) + stage("probs", 0) + stage("scores", 2) + item(24, 28)
        ON_PE += stage("probs", 1) + stage("scores", 3) + item(28, ITEMS) + stage("sums", 0) + stage("sums", 1) + stage("probs", 2)
        ON_PE += stage("probs", 3) + stage("sums", 2) + stage("sums", 3)
        ON_DVE = stage("shift", 0) + stage("shift", 1) + stage("normalise", 0) + stage("normalise", 1)
        ON_DVE += stage("shift", 2) + stage("normalise", 2) + stage("shift", 3) + stage("normalise", 3)
        ON_ACT = stage("exp", 0) + item(16, 18) + stage("exp", 1) + item(18, 24) + stage("out", 0) + item(24, 26) + stage("exp", 2)
        ON_ACT += item(26, 28) + stage("out", 1) + item(28, 30) + stage("exp", 3) + item(30, ITEMS) + stage("features", 0) + stage("out", 2) + stage("out", 3)
        BY_DVE = KEYS // 2
        BY_ACT = ITEMS - BY_DVE
        assert GT == 4 and ITEMS == 32

        def item_bank(n):
            return n % 4 if n < KEYS else 6 + n % 2

        def item_out(n):
            bank = ps[:, item_bank(n), :]
            if n < KEYS:
                return keys[:, :, n, :], bank.rearrange("p (b t) -> p b t", b=GB)
            m = n - KEYS
            return values[:, m // 2, 4 * (m % 2):4 * (m % 2) + 4, :], bank.rearrange("p (h c) -> p h c", h=4)

        with nc.Block() as block:
            @block.gpsimd
            def _(pool):
                with pool.Fori(0, GROUPS) as g:
                    for p in range(pairs):
                        pool.wait_ge(normed, g * pairs + (p + 1))
                        pool.tensor_tensor(prob[:, p % 2, :, :], prob[:, p % 2, :, :],
                                           w["later"][:, :].unsqueeze(1).broadcast_to([P, H, S]), ALU.mult).then_inc(masked, 1)
                    for k in range(NORMS):
                        norms.on_pool(pool, g, k, w["minus_half"])

            @block.vector
            def _(dve):
                tt = nc.vector.tensor_tensor
                four = lambda b: ps[:, b, :].rearrange("p (i c) -> p i c", i=GT)

                def attention(g, step):
                    step(tt(xo[:, :, :], w["x3"][:, bass.ds(g * GT, GT), :], wide_row(w, "L0_xattn_a1_li1_b"), ALU.add))

                    def shift(p):
                        dve.wait_ge(scored, g * pairs + (p + 1))
                        sc = ps[:, 2 * (p % 2):2 * (p % 2) + 2, :].rearrange("p k (h t) -> p (k h) t", t=S)
                        step(nc.vector.tensor_reduce(mx[:, p % 2, :], sc, AX.X, ALU.max))
                        if p >= 2:
                            dve.wait_ge(probs_turned, g * pairs + (p - 1))
                        tt(prob[:, p % 2, :, :], sc, spread(mx[:, p % 2, :], [P, H, S]), ALU.subtract).then_inc(shifted, 1)

                    def normalise(p):
                        dve.wait_ge(exped, g * pairs + (p + 1))
                        step(nc.vector.tensor_reduce(den[:, p % 2, :], prob[:, p % 2, :, :], AX.X, ALU.add))
                        step(nc.vector.reciprocal(rden[:, p % 2, :], den[:, p % 2, :]))
                        tt(prob[:, p % 2, :, :], prob[:, p % 2, :, :], spread(rden[:, p % 2, :], [P, H, S]), ALU.mult).then_inc(normed, 1)

                    for kind, n in ON_DVE:
                        (shift if kind == "shift" else normalise)(n)

                def take(n, x):
                    if n < KEYS and n % 2 == 1:
                        dve.wait_ge(items_filled, x * ITEMS + (n + 1))
                        dst, src = item_out(n)
                        nc.vector.tensor_copy(dst, src).then_inc(items_by_dve, 1)

                def walk(schedule, x, g=None, step=None):
                    for kind, *arg in schedule:
                        if kind == "item":
                            take(arg[0], x)
                        elif kind == "moments3":
                            dve.wait_ge(attended_pair, g * pairs + pairs)
                            step(tt(xo[:, :, :], xo[:, :, :], four(SUMS), ALU.add))
                            norms.moments(dve, step, xo)
                        elif kind == "apply3":
                            norms.apply(dve, g, 0, n0, xo).then_inc(n3_ready, 1)
                            dve.wait_ge(n3_ready, g + 1)
                            step(tt(xo[:, :, :], xo[:, :, :], w["x3"][:, bass.ds(g * GT, GT), :], ALU.add))
                            step(tt(xo[:, :, :], xo[:, :, :], wide_row(w, "L0_xattn_a1_li3_b"), ALU.add))
                        elif kind == "moments4":
                            dve.wait_ge(mlp_done, g + 1)
                            step(tt(xo[:, :, :], xo[:, :, :], four(SUMS), ALU.add))
                            norms.moments(dve, step, xo)
                        elif kind == "apply4":
                            step(norms.apply(dve, g, 1, xo, xo))
                            step(tt(xo[:, :, :], xo[:, :, :], wide_row(w, "L0_xattn_ln2_g"), ALU.mult))
                            tt(x3[:, :, :], xo[:, :, :], wide_row(w, "L0_xattn_ln2_b"), ALU.add).then_inc(x3_ready, 1)
                            step(tt(w["x3"][:, bass.ds(g * GT, GT), :], xo[:, :, :], wide_row(w, "L0_xattn_ln2_b"), ALU.add))
                        elif kind == "moments5":
                            dve.wait_ge(x3_ready, g + 1)
                            norms.moments(dve, step, x3)
                        elif kind == "apply5":
                            norms.apply(dve, g, 2, n0, x3).then_inc(q_normed, 1)

                def one_pass(g, schedule):
                    step = Chain(dve, dve_steps, g * STEPS)
                    attention(g, step)
                    walk(schedule, g + 1, g, step)
                    assert step.n == STEPS, step.n

                walk(FIRST, 0)
                with dve.Fori(0, GROUPS - 1) as g:
                    one_pass(g, SCHEDULE)
                one_pass(GROUPS - 1, LAST)

            @block.scalar
            def _(act):
                act.sem_inc(q_taken, 1)

                def features(x):
                    src = w["xqT"][:, bass.ds(x * GN, GN)]
                    act.activation(xnT[:, :], src, ACT.Identity, scale=vec("a1_lnx_g"), bias=vec("a1_lnx_b")).then_inc(xy_ready, 1)
                    act.activation(ynT[:, :], src, ACT.Identity, scale=vec("a1_lny_g"), bias=vec("a1_lny_b")).then_inc(xy_ready, 1)

                def take(n, x):
                    if n >= KEYS or n % 2 == 0:
                        act.wait_ge(items_filled, x * ITEMS + (n + 1))
                        dst, src = item_out(n)
                        act.copy(dst, src).then_inc(items_by_act, 1)

                def walk(schedule, x, g=None):
                    for kind, *arg in schedule:
                        if kind == "item":
                            take(arg[0], x)
                        elif kind == "turn3":
                            act.wait_ge(n3_turned, g + 1)
                            act.activation(h3T[:, :], ps[:, TURN, :], ACT.Identity, scale=vec("a1_ln3_g"), bias=vec("a1_ln3_b")).then_inc(h3_ready, 1)
                        elif kind == "hid":
                            f = arg[0]
                            act.wait_ge(hid_filled, g * FT + (f + 1))
                            act.activation(hid[:, f, :], ps[:, HID + f % 2, :], ACT.Gelu, bias=w["li2_b"]["a1"][:, f:f + 1]).then_inc(hid_ready, 1)
                        elif kind == "turnq":
                            act.wait_ge(q_turned, g + 1)
                            act.activation(w["xqT"][:, bass.ds(g * GN, GN)], ps[:, TURN, :], ACT.Identity, scale=vec("a2_lnx_g"),
                                           bias=vec("a2_lnx_b")).then_inc(q_taken, 1)

                def turn_out(g, p):
                    act.wait_ge(probs_turned, g * pairs + (p + 1))
                    if p >= 2:
                        act.wait_ge(attended_pair, g * pairs + (p - 1))
                    act.copy(probT[:, p % 2, :, :], ps[:, HID:HID + 2, :].rearrange("p k (h s) -> p (k h) s", s=P)).then_inc(probT_ready, 1)

                def attention(g, last):
                    for kind, n in ON_ACT:
                        if kind == "item":
                            take(n, g)
                        elif kind == "exp":
                            act.wait_ge(shifted, g * pairs + (n + 1))
                            act.activation(prob[:, n % 2, :, :], prob[:, n % 2, :, :], ACT.Exp, scale=SCORE_SCALE).then_inc(exped, 1)
                        elif kind == "out":
                            turn_out(g, n)
                        elif not last:
                            act.wait_ge(items_filled, g * ITEMS + ITEMS)
                            features(g + 1)

                features(0)
                walk(FIRST, 0)
                with act.Fori(0, GROUPS - 1) as g:
                    attention(g, False)
                    walk(SCHEDULE, g + 1, g)
                attention(GROUPS - 1, True)
                walk(LAST, GROUPS, GROUPS - 1)
                act.wait_ge(q_taken, GROUPS + 1)

            @block.tensor
            def _(pe):
                ident = w["ident"]

                def turn(src, done):
                    for i in range(GT):
                        last = nc.tensor.transpose(ps[:, TURN, P * i:P * i + P], src[:, i, :], ident[:, :])
                    last.then_inc(done, 1)

                def make(n, x, g=None):
                    if n == 0:
                        pe.wait_ge(xy_ready, x * 2 + 2)
                        if g is not None:
                            pe.wait_ge(shifted, g * pairs + pairs)
                    if 4 <= n < KEYS:
                        if n % 2 == 0:
                            pe.wait_ge(items_by_act, x * BY_ACT + (n // 2 - 1))
                        else:
                            pe.wait_ge(items_by_dve, x * BY_DVE + (n // 2 - 1))
                    if n == KEYS:
                        pe.wait_ge(q_taken, x + 1)
                    if n >= KEYS + 2:
                        pe.wait_ge(items_by_act, x * BY_ACT + (BY_DVE + n - KEYS - 1))
                    if n < KEYS:
                        last = nc.tensor.matmul(ps[:, item_bank(n), :], w["key_fold"][:, n, :], ynT[:, :], start=True, stop=True)
                    else:
                        b, half = (n - KEYS) // 2, n % 2
                        for par in range(2):
                            last = nc.tensor.matmul(ps[S * par:S * par + S, item_bank(n), :], ynT[:, S * b:S * b + S],
                                                    w["value_fold1"][:, par, 4 * half:4 * half + 4, :].rearrange("p h c -> p (h c)"),
                                                    start=True, stop=True)
                    last.then_inc(items_filled, 1)

                def walk(schedule, x, g=None):
                    for kind, *arg in schedule:
                        if kind == "item":
                            make(arg[0], x, g)
                        elif kind == "turn3":
                            pe.wait_ge(n3_ready, g + 1)
                            pe.wait_ge(q_taken, g + 1)
                            turn(n0, n3_turned)
                        elif kind == "hid":
                            f = arg[0]
                            if f == 0:
                                pe.wait_ge(h3_ready, g + 1)
                            if f >= 2:
                                pe.wait_ge(hid_ready, g * FT + (f - 1))
                            nc.tensor.matmul(ps[:, HID + f % 2, :], w["li2"]["a1"][:, P * f:P * f + P], h3T[:, :], start=True, stop=True).then_inc(hid_filled, 1)
                        elif kind == "mlp":
                            pe.wait_ge(hid_ready, g * FT + FT)
                            for i in range(GT):
                                for f in range(FT):
                                    last = nc.tensor.matmul(ps[:, SUMS, C * i:C * i + C], hid[:, f, P * i:P * i + P], w["li3"]["a1"][:, f, :],
                                                            start=(f == 0), stop=(f == FT - 1))
                            last.then_inc(mlp_done, 1)
                        elif kind == "turnq":
                            pe.wait_ge(q_normed, g + 1)
                            turn(n0, q_turned)

                def attention(g):
                    pe.wait_ge(items_by_act, g * BY_ACT + (KEYS - BY_DVE))
                    pe.wait_ge(items_by_dve, g * BY_DVE + BY_DVE)

                    def scores(p):
                        if p >= 2:
                            pe.wait_ge(shifted, g * pairs + (p - 1))
                        for half in range(2):
                            for u in range(2):
                                b = 2 * p + u
                                last = nc.tensor.matmul(ps[S * u:S * u + S, 2 * (p % 2) + half, :], xnT[:, S * b:S * b + S],
                                                        keys[:, b, 8 * half:8 * half + 8, :].rearrange("p h t -> p (h t)"),
                                                        start=True, stop=True)
                        last.then_inc(scored, 1)

                    def turn_probs(p):
                        pe.wait_ge(masked, g * pairs + (p + 1))
                        if p >= 1:
                            pe.wait_ge(probT_ready, g * pairs + p)
                        flat = prob[:, p % 2, :, :].rearrange("p (k j) t -> p k (j t)", j=2)
                        for k in range(H // 2):
                            last = nc.tensor.transpose(ps[:, HID + k // 4, P * (k % 4):P * (k % 4) + P], flat[:, k, :], ident[:, :])
                        last.then_inc(probs_turned, 1)

                    def sums(p):
                        if p == 0:
                            pe.wait_ge(items_by_act, g * BY_ACT + BY_ACT)
                        pe.wait_ge(probT_ready, g * pairs + (p + 1))
                        for k in range(H // 2):
                            for u in range(2):
                                last = nc.tensor.matmul(ps[S * u:S * u + S, SUMS, C * p:C * p + C], probT[:, p % 2, k, S * u:S * u + S],
                                                        values[:, 2 * p + u, k, :], start=(k == 0), stop=(k == H // 2 - 1))
                        last.then_inc(attended_pair, 1)

                    for kind, n in ON_PE:
                        if kind == "item":
                            make(n, g)
                        else:
                            dict(scores=scores, probs=turn_probs, sums=sums)[kind](n)

                walk(FIRST, 0)
                with pe.Fori(0, GROUPS - 1) as g:
                    attention(g)
                    walk(SCHEDULE, g + 1, g)
                attention(GROUPS - 1)
                walk(LAST, GROUPS, GROUPS - 1)


def cross_attention(nc, a, w, ps, sb):
    RING, SCORE, SUM = 4, 0, 7
    with ExitStack() as ctx:
        sem = lambda n: ctx.enter_context(nc.semaphore("c_" + n))
        raw = sb("raw", [P, 2, TJ, CY])
        ones = sb("ones", [P, TJ])
        squares = sb("squares", [P, TJ, CY])
        total = sb("total", [P, TJ])
        mean = sb("mean", [P, 2, TJ])
        square_sum = sb("square_sum", [P, TJ])
        var = sb("var", [P, TJ])
        rstd = sb("rstd", [P, TJ])
        ctx_n = sb("ctx_n", [P, HB, TJ, CY])
        ctx_parts = sb("ctx_parts", [P, TJ, 2, CY], F16)
        ctx_T = sb("ctx_T", [P, HB, TJ * P], F16)
        q_hi = sb("q_hi", [P, HB, HS], F16)
        q_lo = sb("q_lo", [P, HB, HS], F16)
        part_max = sb("part_max", [P, H // 2, 4])
        neg_max = sb("neg_max", [P, H // 2])
        max_rows = sb("max_rows", [H // 2, P], F16)
        expd = sb("expd", [P, 2, HS])
        raw_in = [sem(f"raw_in{k}") for k in range(2)]
        raw_free, mean_ready, squares_ready, var_ready, rstd_ready = (
            sem("raw_free"), sem("mean_ready"), sem("squares_ready"), sem("var_ready"), sem("rstd_ready"))
        pool_steps, ctx_ready, parts_ready, parts_turned = sem("pool_steps"), sem("ctx_ready"), sem("parts_ready"), sem("parts_turned")
        ring_filled, ring_done, hi_done = sem("ring_filled"), sem("ring_done"), sem("hi_done")
        max_ready, rows_ready, rows_in = sem("max_ready"), sem("rows_ready"), sem("rows_in")
        dve_steps = sem("dve_steps")
        scored, exp_done, summed, sum_out = sem("scored"), sem("exp_done"), sem("summed"), sem("sum_out")

        FULL = T // 512
        REST = T - 512 * FULL
        turn = [("turn", 0), ("turn", 1)]
        query = [("query", k) for k in range(4)]
        score = []
        for q in range(2):
            score += [("score", k, u) for k in range(4 * q, 4 * q + 4) for u in range(FULL)] + [("rest", q)]
        rows = [("rows",)]
        first = turn + query + [("turn2", 0), ("turn2", 1)] + score + rows

        def schedule(i, last):
            ahead1, ahead2 = not (last and i == HB - 1), not (last and i >= HB - 2)
            steps = [[] for _ in range(TJ)]
            if ahead1:
                counts = [3, 3, 3, 3, 3, 3, 2, 2, 2, 2]
                n = 0
                for j, m in enumerate(counts):
                    steps[j] += score[n:n + m]
                    n += m
                assert n == len(score)
                steps[11] += rows
            if ahead2:
                steps[10].append(turn[0])
                steps[12].append(turn[1])
                if i % 2 == 0:
                    steps[10].append(query[0])
                    steps[11].append(query[1])
                    steps[12] += query[2:]
            return steps

        ITEMS = sum(len(s) for i in range(HB) for s in schedule(i, False))
        QUERIES, FIRST = 4 * (HB // 2), len(first)
        PASSES = B // HB

        class Ring:

            def __init__(self, base):
                self.base, self.n = base, 0

            def take(self):
                n = self.n
                self.n += 1
                return n

        def slot_of(x):
            return x % HB

        with nc.Block() as block:
            @block.sync
            def _(sp):
                def load(x, slot):
                    sp.wait_ge(raw_free, x + 1)
                    src = a["ctx_512"][bass.ds(x, 1), :, :].rearrange("o t c -> (o t) c")
                    sp.dma_start(raw[:, slot % 2, 0:TJ - 1, :], src[0:P * (TJ - 1), :].rearrange("(p j) c -> p j c", j=TJ - 1)).then_inc(raw_in[slot % 2], 16)
                    sp.dma_start(raw[0:TLAST, slot % 2, TJ - 1, :], src[P * (TJ - 1):T, :]).then_inc(raw_in[slot % 2], 16)

                def place_max(x, slot):
                    sp.wait_ge(rows_ready, x + 1)
                    sp.dma_start(q_hi[0:1, slot, :], max_rows[:, :]).then_inc(rows_in, 16)

                load(0, 0)
                load(1, 1)
                place_max(0, 0)

                def one_pass(g, last):
                    for i in range(HB):
                        if not (last and i >= HB - 2):
                            load(g * HB + (i + 2), slot_of(i + 2))
                        if not (last and i == HB - 1):
                            place_max(g * HB + (i + 1), slot_of(i + 1))

                with sp.Fori(0, PASSES - 1) as g:
                    one_pass(g, False)
                one_pass(PASSES - 1, True)

            @block.gpsimd
            def _(pool):
                raw_clear = raw[64:P, :, TJ - 1, :]
                pool.memset(raw_clear, 0.0).then_inc(raw_free, 1)
                pool.wait_ge(raw_free, 1)
                pool.memset(ones[:, :], 1.0).then_inc(pool_steps, 1)
                pool.wait_ge(pool_steps, 1)
                pool.sem_inc(raw_free, 1)

                def normalise(x, slot):
                    base = x * 3 + 1
                    r = raw[:, slot % 2, :, :]
                    n = ctx_n[:, slot, :, :]
                    pool.wait_ge(mean_ready, x + 1)
                    pool.tensor_tensor(n, r, spread(mean[:, slot % 2, :], [P, TJ, CY]), ALU.subtract).then_inc(raw_free, 1)
                    pool.wait_ge(raw_free, x + 3)
                    pool.tensor_tensor(squares[:, :, :], n, n, ALU.mult).then_inc(squares_ready, 1)
                    pool.wait_ge(var_ready, x + 1)
                    pool.tensor_tensor(rstd[:, :], var[:, :], w["minus_half"][:, 0:TJ], ALU.pow).then_inc(pool_steps, 1)
                    pool.wait_ge(pool_steps, base + 1)
                    pool.tensor_tensor(n, n, spread(rstd[:, :], [P, TJ, CY]), ALU.mult).then_inc(pool_steps, 1)
                    pool.wait_ge(pool_steps, base + 2)
                    pool.tensor_tensor(n[:, :, 0:1], spread(ones[:, :], [P, TJ, 1]), spread(ones[:, :], [P, TJ, 1]), ALU.mult).then_inc(ctx_ready, 1)
                    pool.wait_ge(ctx_ready, x + 1)
                    pool.wait_ge(parts_turned, x + 1)
                    pool.tensor_tensor(ctx_parts[:, :, 0, :], n, spread(ones[:, :], [P, TJ, CY]), ALU.mult).then_inc(pool_steps, 1)
                    pool.wait_ge(pool_steps, base + 3)
                    pool.tensor_tensor(ctx_parts[:, :, 1, :], n, ctx_parts[:, :, 0, :], ALU.subtract).then_inc(parts_ready, 1)

                normalise(0, 0)
                normalise(1, 1)

                def one_pass(g, last):
                    for i in range(HB if not last else HB - 2):
                        pool.wait_ge(summed, (g * HB + i) * TJ + 2)
                        normalise(g * HB + (i + 2), slot_of(i + 2))

                with pool.Fori(0, PASSES - 1) as g:
                    one_pass(g, False)
                one_pass(PASSES - 1, True)
                pool.wait_ge(parts_ready, B)

            @block.vector
            def _(dve):
                copy = nc.vector.tensor_copy

                def means(x, slot):
                    dve.wait_ge(raw_in[slot % 2], (x - slot % 2) * 16 + 32)
                    nc.vector.tensor_reduce(total[:, :], raw[:, slot % 2, :, :], AX.X, ALU.add).then_inc(dve_steps, 1)
                    dve.wait_ge(dve_steps, x * 2 + 1)
                    nc.vector.tensor_scalar(mean[:, slot % 2, :], total[:, :], 1.0 / CY, None, ALU.mult).then_inc(mean_ready, 1)

                def variances(x):
                    dve.wait_ge(squares_ready, x + 1)
                    nc.vector.tensor_reduce(square_sum[:, :], squares[:, :, :], AX.X, ALU.add).then_inc(dve_steps, 1)
                    dve.wait_ge(dve_steps, x * 2 + 2)
                    nc.vector.tensor_scalar(var[:, :], square_sum[:, :], 1.0 / CY, EPS, ALU.mult, ALU.add).then_inc(var_ready, 1)

                def take(ring, item, x, slot):
                    n = ring.take()
                    bank = ps[:, RING + n % 3, :]
                    kind = item[0]
                    dve.wait_ge(ring_filled, ring.base + (n + 1))
                    if kind == "turn":
                        m = (P * 8, P * (TJ - 8))[item[1]]
                        last = copy(ctx_T[:, slot, P * 8 * item[1]:P * 8 * item[1] + m], bank.bitcast(F16)[:, 0:m])
                    elif kind == "query":
                        dve.wait_ge(hi_done, ring.queries + 1)
                        ring.queries += 1
                        k = item[1]
                        v = lambda t: t[:, slot:slot + 2, :].rearrange("p b (h s) -> p h b s", h=H)[:, 4 * k:4 * k + 4, :, :]
                        last = nc.vector.tensor_tensor(v(q_lo), bank.rearrange("p (h b s) -> p h b s", h=4, b=2), v(q_hi), ALU.subtract)
                    elif kind == "score":
                        last = nc.vector.tensor_reduce(part_max[:, item[1], item[2]:item[2] + 1], bank, AX.X, ALU.max)
                    elif kind == "rest":
                        q = item[1]
                        last = nc.vector.tensor_reduce(part_max[:, 4 * q:4 * q + 4, FULL], bank[:, 0:4 * REST].rearrange("p (k t) -> p k t", k=4),
                                                       AX.X, ALU.max)
                    else:
                        last = copy(max_rows[:, :], ps[0:H // 2, RING + n % 3, 0:P])
                    last.then_inc(ring_done, 1)
                    if kind == "rows":
                        dve.wait_ge(ring_done, ring.base + (n + 1))
                        dve.sem_inc(rows_ready, 1)

                def maxima(ring, x):
                    dve.wait_ge(ring_done, ring.base + ring.n)
                    nc.vector.tensor_reduce(neg_max[:, :], part_max[:, :, :], AX.X, ALU.max, negate=True).then_inc(max_ready, 1)

                ring = Ring(0)
                ring.queries = 0
                means(0, 0)
                variances(0)
                means(1, 1)
                variances(1)
                for item in first:
                    if item[0] == "rows":
                        maxima(ring, 0)
                    if item[0] == "turn2":
                        take(ring, ("turn", item[1]), 1, 1)
                    else:
                        take(ring, item, 0, 0)

                def one_pass(g, last):
                    ring = Ring(g * ITEMS + FIRST)
                    ring.queries = g * QUERIES + 4
                    for i in range(HB):
                        x = g * HB + i
                        ahead2 = not (last and i >= HB - 2)
                        for j, items in enumerate(schedule(i, last)):
                            if ahead2 and j == 0:
                                means(x + 2, slot_of(i + 2))
                            if ahead2 and j == 3:
                                variances(x + 2)
                            for item in items:
                                if item[0] == "rows":
                                    take(ring, item, x + 1, slot_of(i + 1))
                                elif item[0] in ("turn", "query"):
                                    take(ring, item, x + 2, slot_of(i + 2))
                                else:
                                    take(ring, item, x + 1, slot_of(i + 1))
                            if j == 9 and items:
                                maxima(ring, x + 1)

                with dve.Fori(0, PASSES - 1) as g:
                    one_pass(g, False)
                one_pass(PASSES - 1, True)

            @block.scalar
            def _(act):
                act.sem_inc(exp_done, 2)
                act.sem_inc(sum_out, 1)

                def high(n, base, k, slot):
                    act.wait_ge(ring_filled, base + (n + 1))
                    v = q_hi[:, slot:slot + 2, :].rearrange("p b (h s) -> p h b s", h=H)[:, 4 * k:4 * k + 4, :, :]
                    act.copy(v, ps[:, RING + n % 3, :].rearrange("p (h b s) -> p h b s", h=4, b=2)).then_inc(hi_done, 1)

                def sums_out(x):
                    act.wait_ge(summed, x * TJ + (TJ + 2))
                    act.copy(w["attended"][:, bass.ds(x, 1), :].rearrange("p o n -> p (o n)"), ps[:, SUM, :]).then_inc(sum_out, 1)

                for n, item in enumerate(first):
                    if item[0] == "query":
                        high(n, 0, item[1], 0)

                def one_pass(g, last):
                    ring = Ring(g * ITEMS + FIRST)
                    for i in range(HB):
                        x = g * HB + i
                        for j, items in enumerate(schedule(i, last)):
                            t = x * TJ + j
                            act.wait_ge(scored, t + 1)
                            act.wait_ge(summed, t + 1)
                            m = P if j < TJ - 1 else TLAST
                            k = (i * TJ + j) % 2
                            act.activation(expd[0:m, k, :], ps[0:m, SCORE + 2 * k:SCORE + 2 * k + 2, :].rearrange("p k n -> p (k n)"),
                                           ACT.Exp, scale=SCORE_SCALE / QUERY_SCALE).then_inc(exp_done, 1)
                            for item in items:
                                n = ring.take()
                                if item[0] == "query":
                                    high(n, ring.base, item[1], slot_of(i + 2))
                        sums_out(x)

                with act.Fori(0, PASSES - 1) as g:
                    one_pass(g, False)
                one_pass(PASSES - 1, True)
                act.wait_ge(sum_out, B + 1)

            @block.tensor
            def _(pe):
                pe.sem_inc(summed, 2)
                pe.sem_inc(parts_turned, 1)

                def put(ring, item, x, slot):
                    n = ring.take()
                    bank = ps[:, RING + n % 3, :]
                    kind = item[0]
                    if not (isinstance(ring.base, int) and ring.base == 0 and n < 3):
                        pe.wait_ge(ring_done, ring.base + (n - 2 if n else 0))
                    if kind == "turn":
                        if item[1] == 0:
                            pe.wait_ge(parts_ready, x + 1)
                        for j in range(8 * item[1], min(8 * item[1] + 8, TJ)):
                            last = nc.tensor.transpose(bank.bitcast(F16)[:, P * (j % 8):P * (j % 8) + P],
                                                       ctx_parts[:, j, :, :].rearrange("p u c -> p (u c)"), w["ident16"][:, :])
                    elif kind == "query":
                        k = item[1]
                        for h in range(4):
                            last = nc.tensor.matmul(bank[:, P * h:P * h + P], w["query_fold"][:, 4 * k + h, :, :].rearrange("p u c -> p (u c)"),
                                                    w["xqT"][:, bass.ds(x * S, 2 * S)], start=True, stop=True)
                    elif kind == "score":
                        k, u = item[1:]
                        last = nc.tensor.matmul(bank, q_hi[:, slot, P * k:P * k + P], ctx_T[:, slot, 512 * u:512 * u + 512], start=True, stop=True)
                    elif kind == "rest":
                        for k in range(4):
                            last = nc.tensor.matmul(bank[:, REST * k:REST * k + REST], q_hi[:, slot, P * (4 * item[1] + k):P * (4 * item[1] + k) + P],
                                                    ctx_T[:, slot, 512 * FULL:T], start=True, stop=True)
                    else:
                        pe.wait_ge(max_ready, x + 1)
                        last = nc.tensor.transpose(ps[0:H // 2, RING + n % 3, 0:P], neg_max[:, :], w["ident"][:, :])
                    last.then_inc(ring_filled, 1)
                    if kind == "turn" and item[1] == 1:
                        pe.wait_ge(ring_filled, ring.base + (n + 1))
                        pe.sem_inc(parts_turned, 1)

                ring = Ring(0)
                for item in first:
                    if item[0] == "turn2":
                        put(ring, ("turn", item[1]), 1, 1)
                    else:
                        if item == score[0]:
                            pe.wait_ge(ring_done, ring.n)
                        put(ring, item, 0, 0)

                def tile_scores(x, i, j):
                    t = x * TJ + j
                    m = P if j < TJ - 1 else TLAST
                    k = (i * TJ + j) % 2
                    pe.wait_ge(exp_done, t + 1)
                    for half in range(2):
                        for part, q in enumerate((q_hi, q_lo)):
                            last = nc.tensor.matmul(ps[0:m, SCORE + 2 * k + half, :], ctx_T[:, slot_of(i), P * j:P * j + m],
                                                    q[:, slot_of(i), 512 * half:512 * half + 512], start=(part == 0), stop=(part == 1))
                    last.then_inc(scored, 1)

                def tile_sum(x, i, j):
                    t = x * TJ + j
                    m = P if j < TJ - 1 else TLAST
                    k = (i * TJ + j) % 2
                    pe.wait_ge(exp_done, t + 3)
                    if j == 0:
                        pe.wait_ge(sum_out, x + 1)
                        pe.wait_ge(ctx_ready, x + 1)
                    for half in range(2):
                        last = nc.tensor.matmul(ps[CY * half:CY * half + CY, SUM, :], ctx_n[0:m, slot_of(i), j, :],
                                                expd[0:m, k, 512 * half:512 * half + 512], start=(j == 0), stop=(j == TJ - 1))
                    last.then_inc(summed, 1)

                def one_pass(g, last):
                    ring = Ring(g * ITEMS + FIRST)
                    for i in range(HB):
                        x = g * HB + i
                        pe.wait_ge(rows_in, x * 16 + 16)
                        for j, items in enumerate(schedule(i, last)):
                            tile_scores(x, i, j)
                            if j:
                                tile_sum(x, i, j - 1)
                            for item in items:
                                if item[0] in ("turn", "query"):
                                    put(ring, item, x + 2, slot_of(i + 2))
                                else:
                                    put(ring, item, x + 1, slot_of(i + 1))
                        tile_sum(x, i, TJ - 1)

                with pe.Fori(0, PASSES - 1) as g:
                    one_pass(g, False)
                one_pass(PASSES - 1, True)


def finish_tokens(nc, a, out, w, ps, sb):
    with ExitStack() as ctx:
        sem = lambda n: ctx.enter_context(nc.semaphore("f_" + n))
        den = sb("den", [P, 2, B * 512 // P])
        both = sb("both", [P, P])
        out_bias = sb("out_bias", [P, 1, C])
        att = sb("att", [P, GB, H // 2, S])
        x0 = sb("x0", [P, GT, C])
        added = sb("added", [P, GT, C])
        xo = sb("xo", [P, GT, C])
        n0 = sb("n0", [P, GT, C])
        nT = sb("nT", [P, GN])
        hT = sb("hT", [P, GN])
        hid = sb("hid", [P, FT, GN])
        qkvz = sb("qkvz_tok", [P, GT, 4, C])
        q2 = sb("q2", [P, GT, C])
        q2b = sb("q2b", [P, GT, C])
        err = sb("err", [P, GT, C])
        o1 = sb("o1", [P, GT, C])
        o2 = sb("o2", [P, GT, C])
        spare = att[:, :, :, :].rearrange("p b h s -> p b (h s)")
        pairs = spare[:, 0:4, :].rearrange("p (u k) (d c) -> p u (k d) c", u=2, c=C)
        prods = spare[:, 4:6, :].rearrange("p k (d c) -> p (k d) c", c=C)
        logit_max = sb("logit_max", [P, GT])
        shifted_l = sb("shifted_l", [P, GT, NE])
        exp_l = sb("exp_l", [P, GT, NE])
        den_l = sb("den_l", [P, GT])
        top = sb("top", [P, GT])
        rank = sb("rank", [P, GT, NE])
        best = sb("best", [P, GT])
        gate = sb("gate", [P, GT, NE])
        act1 = sb("act1", [P, 2, 2, GN])
        acc = sb("acc", [P, GT, C])
        x0_in, den_in, den_inv, inv_in = sem("x0_in"), sem("den_in"), sem("den_inv"), sem("inv_in")
        dve_steps, pool_steps = sem("dve_steps"), sem("pool_steps")
        both_ready, const_filled, fold_ready = sem("both_ready"), sem("const_filled"), sem("fold_ready")
        var_ready, rstd_ready = sem("var_ready"), sem("rstd_ready")
        inv_spread, att_out, projected, added_ready = sem("inv_spread"), sem("att_out"), sem("projected"), sem("added_ready")
        norm_ready, turned, nT_ready = sem("norm_ready"), sem("turned"), sem("nT_ready")
        hid_filled, hid_ready, mlp_done = sem("hid_filled"), sem("hid_ready"), sem("mlp_done")
        qkvz_filled, qkvz_ready = sem("qkvz_filled"), sem("qkvz_ready")
        shifted_up, prev_filled, q2_ready, sig_ready = sem("shifted_up"), sem("prev_filled"), sem("q2_ready"), sem("sig_ready")
        pairs_ready, half_summed, sums_read, contracted = sem("pairs_ready"), sem("half_summed"), sem("sums_read"), sem("contracted")
        err_ready, lin_done = sem("err_ready"), sem("lin_done")
        logits_filled, logits_shifted, logits_exped = sem("logits_filled"), sem("logits_shifted"), sem("logits_exped")
        up_filled, up_ready, down_filled, acc_done, out_stored = (
            sem("up_filled"), sem("up_ready"), sem("down_filled"), sem("acc_done"), sem("out_stored"))
        norms = Norms(nc, sb, var_ready, rstd_ready, 4, "f")
        TURNS = 4
        STEPS = 22
        INV = float(C) ** -0.5
        RING, SUMS, TURN = 4, 6, 7
        xv = a["x"].rearrange("(i b) s c -> (b s) i c", b=2)
        ov = out.rearrange("(i b) s c -> (b s) i c", b=2)
        vec = lambda n: w["vec"][:, w["vec_of"][n]:w["vec_of"][n] + 1]
        banks4 = lambda b: ps[:, b, :].rearrange("p (i c) -> p i c", i=GT)

        up = lambda *ns: [("up", n) for n in ns]
        down = lambda e: [("down", e)]
        several = lambda kind, *ns: [(kind, n) for n in range(*ns)]
        halves = lambda *ns: [("sum", n, h) for n in range(*ns) for h in range(2)]
        BODY = up(0, 1) + several("inv", 0, 4) + up(2, 3) + several("inv", 4, GB) + down(0) + several("proj", GT)
        BODY += [("moments", 0)] + up(4, 5) + [("apply", 0)] + down(1) + up(6, 7) + [("turn", 0)] + down(2)
        BODY += several("hid", FT) + up(8, 9) + [("mlp",)]
        BODY += [("moments", 1)] + down(3) + up(10, 11) + [("apply", 1), ("turn", 1), ("next",)] + several("qkvz", GT) + down(4) + [("prev",)]
        BODY += halves(0, 3) + up(12, 13) + halves(3, 6) + down(5) + halves(6, 8) + [("y",)]
        BODY += up(14, 15) + [("turn", 2)] + down(6) + [("lin",), ("moments", 2)] + up(16, 17) + [("apply", 2), ("moments", 3)] + down(7)
        BODY += [("apply", 3), ("turn", 3)] + down(8) + [("logits",)]
        before = [s for s in BODY if s[0] not in ("up", "down")]
        experts = [s for s in BODY if s[0] in ("up", "down")]

        with nc.Block() as block:
            @block.sync
            def _(sp):
                rows = [w["attended"][CY * half:CY * half + 1, :, :].rearrange("p b n -> p (b n)") for half in range(2)]
                for half in range(2):
                    sp.dma_start(den[:, half, :], rows[half]).then_inc(den_in, 16)
                sp.dma_start(x0[:, :, :], xv[:, 0:GT, :]).then_inc(x0_in, 16)
                sp.wait_ge(den_inv, 1)
                for half in range(2):
                    sp.dma_start(rows[half], den[:, half, :]).then_inc(inv_in, 16)

                def store(y):
                    sp.wait_ge(acc_done, y * NX + (NX + 2))
                    sp.dma_start(ov[:, bass.ds(y * GT, GT), :], acc[:, :, :]).then_inc(out_stored, 16)

                with sp.Fori(0, GROUPS - 1) as y:
                    sp.wait_ge(added_ready, y + 1)
                    sp.dma_start(x0[:, :, :], xv[:, bass.ds((y + 1) * GT, GT), :]).then_inc(x0_in, 16)
                    store(y)
                store(GROUPS - 1)
                sp.wait_ge(out_stored, 16 * GROUPS)

            @block.gpsimd
            def _(pool):
                step = Chain(pool, pool_steps, 0)
                step(pool.memset(both[:, :], 0.0))
                step(pool.memset(both[0:1, :], 1.0))
                pool.memset(both[CY:CY + 1, :], 1.0).then_inc(both_ready, 1)
                pool.wait_ge(both_ready, 1)

                def walk(x):
                    for kind, *arg in before:
                        if kind == "proj" and arg[0] == 0:
                            pool.wait_ge(x0_in, x * 16 + 16)
                            pool.tensor_tensor(added[:, :, :], x0[:, :, :], w["x3"][:, bass.ds(x * GT, GT), :], ALU.add).then_inc(added_ready, 1)
                        elif kind == "moments":
                            norms.on_pool(pool, x, arg[0], w["minus_half"])
                        elif kind == "sum" and arg[1] == 0:
                            n = arg[0]
                            i = n % GT
                            if n < GT:
                                pool.wait_ge(qkvz_ready, x * GT + (i + 1))
                            else:
                                pool.wait_ge(err_ready, x * GT + (i + 1))
                            if n >= 2:
                                pool.wait_ge(half_summed, x * 4 * GT + (2 * n - 2))
                            if n == GT:
                                pool.wait_ge(sig_ready, x + 1)
                            key = qkvz[:, i, 1 if n < GT else 3, :].rearrange("p (h d) -> p d h", d=DL)
                            val = (qkvz[:, i, 2, :] if n < GT else err[:, i, :]).rearrange("p (h e) -> p h e", e=DL)
                            o = pairs[:, n % 2, :, :].rearrange("p d (h e) -> p d h e", e=DL)
                            for d in range(DL):
                                last = pool.tensor_tensor(o[:, d, :, :], spread(key[:, d, :], [P, HL, DL]), val, ALU.mult)
                            last.then_inc(pairs_ready, 1)

                walk(0)
                with pool.Fori(0, GROUPS - 1) as y:
                    walk(y + 1)

            @block.vector
            def _(dve):
                tt = nc.vector.tensor_tensor
                dve.sem_inc(acc_done, 2)
                dve.wait_ge(const_filled, 1)
                i = w["row_of"]["L0_xattn_a2_li1_b"]
                tt(out_bias[:, 0, :], ps[:, SUMS, 0:C], w["row"][:, i, :], ALU.add).then_inc(fold_ready, 1)
                nc.vector.memset(w["value_fold"][0:1, :, :], 0.0).then_inc(fold_ready, 1)
                nc.vector.memset(w["value_fold"][CY:CY + 1, :, :], 0.0).then_inc(fold_ready, 1)
                dve.wait_ge(den_in, 32)
                nc.vector.reciprocal(den[:, :, :], den[:, :, :]).then_inc(den_inv, 1)
                dve.wait_ge(fold_ready, 3)

                def walk(schedule, x, y=None):
                    step = Chain(dve, dve_steps, x * STEPS)
                    for kind, *arg in schedule:
                        n = arg[0] if arg else None
                        if kind == "inv":
                            dve.wait_ge(inv_spread, x * GB + (n + 1))
                            tt(att[:, n, :, :].rearrange("p h s -> p (h s)"), w["attended"][:, bass.ds(x * GB + n, 1), :].rearrange("p o n -> p (o n)"),
                               ps[:, RING + n % 2, :], ALU.mult).then_inc(att_out, 1)
                        elif kind == "proj" and n == 0:
                            if schedule is BODY:
                                dve.wait_ge(acc_done, y * NX + 3)
                            step(tt(xo[:, :, :], w["x3"][:, bass.ds(x * GT, GT), :], out_bias[:, :, :].broadcast_to([P, GT, C]), ALU.add))
                        elif kind == "moments":
                            if n == 0:
                                dve.wait_ge(projected, x * GT + GT)
                                step(tt(xo[:, :, :], xo[:, :, :], banks4(SUMS), ALU.add))
                            elif n == 1:
                                dve.wait_ge(mlp_done, x + 1)
                                step(tt(xo[:, :, :], xo[:, :, :], banks4(SUMS), ALU.add))
                            elif n == 2:
                                dve.wait_ge(lin_done, x + 1)
                                step(tt(xo[:, :, :], xo[:, :, :], banks4(SUMS), ALU.add))
                            norms.moments(dve, step, xo if n < 3 else n0)
                        elif kind == "apply":
                            if n == 2:
                                step(norms.apply(dve, x, n, n0, xo))
                            else:
                                norms.apply(dve, x, n, n0, xo if n < 3 else n0).then_inc(norm_ready, 1)
                            if n == 0:
                                dve.wait_ge(norm_ready, x * TURNS + 1)
                                step(tt(xo[:, :, :], xo[:, :, :], wide_row(w, "L0_xattn_a2_li3_b"), ALU.add))
                                dve.wait_ge(added_ready, x + 1)
                                step(tt(xo[:, :, :], xo[:, :, :], added[:, :, :], ALU.add))
                        elif kind == "qkvz":
                            dve.wait_ge(qkvz_filled, x * GT + (n + 1))
                            tt(qkvz[:, n, :, :].rearrange("p k c -> p (k c)"), ps[:, RING + n % 2, :],
                               w["qkvz_b"][:, :, :].rearrange("p k c -> p (k c)"), ALU.add).then_inc(qkvz_ready, 1)
                        elif kind == "prev":
                            dve.wait_ge(prev_filled, x + 1)
                            step(nc.vector.tensor_scalar(q2b[:, :, :], banks4(TURN), float(DL) ** -0.5, None, ALU.mult))
                            step(nc.vector.tensor_scalar(q2[:, :, :], q2b[:, :, :], 0.02, None, ALU.mult))
                            tt(q2[:, :, :], q2[:, :, :], q2b[:, :, :], ALU.min).then_inc(q2_ready, 1)
                            dve.wait_ge(shifted_up, x + 1)
                            dve.wait_ge(qkvz_ready, x * GT + GT)
                            dve.wait_ge(q2_ready, x + 1)
                        elif kind == "sum":
                            half = arg[1]
                            dve.wait_ge(half_summed, x * 4 * GT + (2 * n + half + 1))
                            q = qkvz[:, n, 0, :] if n < GT else q2[:, n - GT, :]
                            dh = DL // 2
                            s = ps[:, RING + half, :].rearrange("p (d h e) -> p d h e", h=HL, e=DL)
                            qs = spread(q.rearrange("p (h d) -> p d h", d=DL)[:, dh * half:dh * half + dh, :], [P, dh, HL, DL])
                            tt(prods[:, dh * half:dh * half + dh, :].rearrange("p d (h e) -> p d h e", e=DL), s, qs, ALU.mult).then_inc(sums_read, 1)
                            if half == 1:
                                dve.wait_ge(sums_read, x * 4 * GT + (2 * n + 2))
                                dst = o1[:, n, :] if n < GT else o2[:, n - GT, :]
                                nc.vector.tensor_reduce(dst, prods[:, :, :].rearrange("p d c -> p c d"), AX.X, ALU.add).then_inc(contracted, 1)
                                dve.wait_ge(contracted, x * 2 * GT + (n + 1))
                                if n < GT:
                                    tt(err[:, n, :], ps[:, SUMS, C * n:C * n + C], o1[:, n, :], ALU.subtract).then_inc(err_ready, 1)
                        elif kind == "y":
                            tt(n0[:, :, :], o1[:, :, :], o2[:, :, :], ALU.add).then_inc(norm_ready, 1)
                            step(tt(xo[:, :, :], xo[:, :, :], wide_row(w, "L0_attn_bp"), ALU.add))
                        elif kind == "logits":
                            dve.wait_ge(logits_filled, x + 1)
                            logits = ps[:, SUMS, 0:GT * NE].rearrange("p (i e) -> p i e", i=GT)
                            step(nc.vector.tensor_reduce(logit_max[:, :], logits, AX.X, ALU.max))
                            tt(shifted_l[:, :, :], logits, spread(logit_max[:, :], [P, GT, NE]), ALU.subtract).then_inc(logits_shifted, 1)
                            dve.wait_ge(logits_shifted, x + 1)
                            step(nc.vector.tensor_scalar(rank[:, :, :], shifted_l[:, :, :], 0.0, None, ALU.is_equal))
                            step(tt(rank[:, :, :], rank[:, :, :], w["iota_down"][:, :].unsqueeze(1).broadcast_to([P, GT, NE]), ALU.mult))
                            step(nc.vector.tensor_reduce(best[:, :], rank[:, :, :], AX.X, ALU.max))
                            step(tt(rank[:, :, :], rank[:, :, :], spread(best[:, :], [P, GT, NE]), ALU.is_equal))
                            dve.wait_ge(logits_exped, x + 1)
                            step(nc.vector.tensor_reduce(den_l[:, :], exp_l[:, :, :], AX.X, ALU.add))
                            step(nc.vector.reciprocal(top[:, :], den_l[:, :]))
                            step(tt(gate[:, :, :], rank[:, :, :], spread(top[:, :], [P, GT, NE]), ALU.mult))
                        elif kind == "down":
                            dve.wait_ge(down_filled, y * NX + (n + 1))
                            if n == 0:
                                tt(acc[:, :, :], xo[:, :, :], banks4(2), ALU.add).then_inc(acc_done, 1)
                            else:
                                dve.wait_ge(acc_done, y * NX + (n + 2))
                                for i in range(GT):
                                    last = nc.vector.scalar_tensor_tensor(out=acc[:, i, :], in0=ps[:, 2 + n % 2, C * i:C * i + C],
                                                                          scalar=gate[:, i, n - 1:n], in1=acc[:, i, :], op0=ALU.mult, op1=ALU.add)
                                last.then_inc(acc_done, 1)
                    if schedule is not experts:
                        assert step.n == STEPS, step.n
                    if schedule is BODY:
                        dve.wait_ge(out_stored, y * 16 + 16)
                    elif schedule is before:
                        dve.wait_ge(dve_steps, x * STEPS + STEPS)

                walk(before, 0)
                with dve.Fori(0, GROUPS - 1) as y:
                    walk(BODY, y + 1, y)
                walk(experts, 0, GROUPS - 1)

            @block.scalar
            def _(act):
                def walk(schedule, x, y=None):
                    for kind, *arg in schedule:
                        n = arg[0] if arg else None
                        if kind == "turn":
                            act.wait_ge(turned, x * TURNS + (n + 1))
                            affine = {0: dict(scale=vec("L0_xattn_a2_ln3_g"), bias=vec("L0_xattn_a2_ln3_b")),
                                      3: dict(scale=vec("L0_ffn_ln_gamma"), bias=vec("L0_ffn_ln_beta"))}.get(n, {})
                            act.activation(hT[:, :] if n == 3 else nT[:, :], ps[:, TURN, :], ACT.Identity, **affine).then_inc(nT_ready, 1)
                        elif kind == "hid":
                            act.wait_ge(hid_filled, x * FT + (n + 1))
                            act.activation(hid[:, n, :], ps[:, RING + n % 2, :], ACT.Gelu, bias=w["li2_b"]["a2"][:, n:n + 1]).then_inc(hid_ready, 1)
                        elif kind == "prev":
                            act.wait_ge(qkvz_ready, x * GT + GT)
                            act.activation(qkvz[:, :, 3, :], qkvz[:, :, 3, :], ACT.Sigmoid, scale=0.02 * INV).then_inc(sig_ready, 1)
                        elif kind == "logits":
                            act.wait_ge(logits_shifted, x + 1)
                            act.activation(exp_l[:, :, :], shifted_l[:, :, :], ACT.Exp).then_inc(logits_exped, 1)
                        elif kind == "up":
                            e, k = n // 2, n % 2
                            act.wait_ge(up_filled, y * 2 * NX + (n + 1))
                            if e >= 2:
                                act.wait_ge(down_filled, y * NX + (e - 1))
                            act.activation(act1[:, e % 2, k, :], ps[:, k, :], ACT.Silu, scale=w["s1"][:, n:n + 1]).then_inc(up_ready, 1)

                walk(before, 0)
                with act.Fori(0, GROUPS - 1) as y:
                    walk(BODY, y + 1, y)
                walk(experts, 0, GROUPS - 1)

            @block.tensor
            def _(pe):
                ident = w["ident"]
                pe.wait_ge(both_ready, 1)
                for k in range(H // 2):
                    last = nc.tensor.matmul(ps[:, SUMS, 0:C], both[:, :], w["value_fold"][:, k, :], start=(k == 0), stop=(k == H // 2 - 1))
                last.then_inc(const_filled, 1)
                pe.wait_ge(fold_ready, 3)
                pe.wait_ge(inv_in, 32)

                def walk(schedule, x, y=None):
                    for kind, *arg in schedule:
                        n = arg[0] if arg else None
                        if kind == "inv":
                            if n >= 2:
                                pe.wait_ge(att_out, x * GB + (n - 1))
                            nc.tensor.matmul(ps[:, RING + n % 2, :], w["sel"][:, :, :].rearrange("p u c -> p (u c)"),
                                             w["attended"][:, bass.ds(x * GB + n, 1), :].rearrange("p o n -> p (o n)"), start=True, stop=True).then_inc(inv_spread, 1)
                        elif kind == "proj":
                            pe.wait_ge(att_out, x * GB + (2 * n + 2))
                            for k in range(H // 2):
                                for u in range(2):
                                    last = nc.tensor.matmul(ps[S * u:S * u + S, SUMS, C * n:C * n + C], att[:, 2 * n + u, k, :], w["value_fold"][:, k, :],
                                                            start=(k == 0), stop=(k == H // 2 - 1))
                            last.then_inc(projected, 1)
                        elif kind == "turn":
                            pe.wait_ge(norm_ready, x * TURNS + (n + 1))
                            for i in range(GT):
                                last = nc.tensor.transpose(ps[:, TURN, P * i:P * i + P], n0[:, i, :], ident[:, :])
                            last.then_inc(turned, 1)
                        elif kind == "hid":
                            if n == 0:
                                pe.wait_ge(nT_ready, x * TURNS + 1)
                            if n >= 2:
                                pe.wait_ge(hid_ready, x * FT + (n - 1))
                            nc.tensor.matmul(ps[:, RING + n % 2, :], w["li2"]["a2"][:, P * n:P * n + P], nT[:, :], start=True, stop=True).then_inc(hid_filled, 1)
                        elif kind == "mlp":
                            pe.wait_ge(hid_ready, x * FT + FT)
                            for i in range(GT):
                                for f in range(FT):
                                    last = nc.tensor.matmul(ps[:, SUMS, C * i:C * i + C], hid[:, f, P * i:P * i + P], w["li3"]["a2"][:, f, :],
                                                            start=(f == 0), stop=(f == FT - 1))
                            last.then_inc(mlp_done, 1)
                        elif kind == "next":
                            nc.tensor.matmul(ps[:, SUMS, :], w["next"][:, :], n0[:, :, :].rearrange("p i c -> p (i c)"), start=True, stop=True).then_inc(shifted_up, 1)
                        elif kind == "qkvz":
                            if n == 0:
                                pe.wait_ge(nT_ready, x * TURNS + 2)
                            if n >= 2:
                                pe.wait_ge(qkvz_ready, x * GT + (n - 1))
                            nc.tensor.matmul(ps[:, RING + n % 2, :], nT[:, P * n:P * n + P], w["qkvz"][:, :, :].rearrange("p k c -> p (k c)"),
                                             start=True, stop=True).then_inc(qkvz_filled, 1)
                        elif kind == "prev":
                            pe.wait_ge(qkvz_ready, x * GT + GT)
                            nc.tensor.matmul(ps[:, TURN, :], w["prev"][:, :], qkvz[:, :, 0, :], start=True, stop=True).then_inc(prev_filled, 1)
                        elif kind == "sum":
                            half = arg[1]
                            if half == 0:
                                pe.wait_ge(pairs_ready, x * 2 * GT + (n + 1))
                            if n >= 1:
                                pe.wait_ge(sums_read, x * 4 * GT + (2 * n + half - 1))
                            tri = w["upto"] if n < GT else w["before"]
                            nc.tensor.matmul(ps[:, RING + half, :], tri[:, :], pairs[:, n % 2, 4 * half:4 * half + 4, :].rearrange("p d c -> p (d c)"),
                                             start=True, stop=True).then_inc(half_summed, 1)
                        elif kind == "lin":
                            pe.wait_ge(nT_ready, x * TURNS + 3)
                            for i in range(GT):
                                last = nc.tensor.matmul(ps[:, SUMS, C * i:C * i + C], nT[:, P * i:P * i + P], w["wp"][:, :], start=True, stop=True)
                            last.then_inc(lin_done, 1)
                        elif kind == "logits":
                            pe.wait_ge(nT_ready, x * TURNS + 4)
                            for i in range(GT):
                                last = nc.tensor.matmul(ps[:, SUMS, NE * i:NE * i + NE], hT[:, P * i:P * i + P], w["router"][:, :], start=True, stop=True)
                            last.then_inc(logits_filled, 1)
                        elif kind == "up":
                            if n >= 2:
                                pe.wait_ge(up_ready, y * 2 * NX + (n - 1))
                            nc.tensor.matmul(ps[:, n % 2, :], w["t1T"][:, n, :], hT[:, :], start=True, stop=True).then_inc(up_filled, 1)
                        elif kind == "down":
                            pe.wait_ge(up_ready, y * 2 * NX + (2 * n + 2))
                            pe.wait_ge(acc_done, y * NX + (n + 1))
                            for i in range(GT):
                                for k in range(2):
                                    last = nc.tensor.matmul(ps[:, 2 + n % 2, C * i:C * i + C], act1[:, n % 2, k, P * i:P * i + P], w["t2T"][:, 2 * n + k, :],
                                                            start=(k == 0), stop=(k == 1))
                            last.then_inc(down_filled, 1)

                walk(before, 0)
                with pe.Fori(0, GROUPS - 1) as y:
                    walk(BODY, y + 1, y)
                walk(experts, 0, GROUPS - 1)


_OUT = ((B, S, C), "float32")


def kernel(**inputs):
    import numpy as np
    import concourse.bacc as bacc
    from concourse.bass_utils import run_bass_kernel_spmd

    nc = bacc.Bacc("TRN2", target_bir_lowering=False, num_devices=1)
    arrays, args = {}, {}
    for name, value in inputs.items():
        value = np.ascontiguousarray(value)
        arrays[f"in_{name}"] = value
        args[name] = nc.dram_tensor(f"in_{name}", value.shape, mybir.dt.from_np(value.dtype), kind="ExternalInput").ap()
    out = nc.dram_tensor("out_x", _OUT[0], mybir.dt.from_np(np.dtype(_OUT[1])), kind="ExternalOutput").ap()
    perceiver_kernel(nc, args, out)
    r = run_bass_kernel_spmd(nc, [arrays], core_ids=[0])
    return r.results[0]["out_x"]
```

```python
from contextlib import ExitStack

import concourse.bass as bass
from concourse import mybir

F32 = mybir.dt.float32
F16 = mybir.dt.float16
ALU = mybir.AluOpType
ACT = mybir.ActivationFunctionType
AX = mybir.AxisListType

P = 128
B, S, C = 32, 64, 128
T, CY = 1601, 64
H, D = 16, 32
TOK = B * S
GROUPS = 4
GB = B // GROUPS
GT = GB * S // P
GN = GB * S
FF = 4 * C
FT = FF // P
HL, DL = 16, 8
NE, FE = 8, 256
NX = NE + 1
EPS = 1e-5
MAGIC_MIN_SCALE = 1e-5
SCORE_SCALE = float(D) ** -0.5
QUERY_SCALE = 0.125
TJ = (T + P - 1) // P
TLAST = T - (TJ - 1) * P
HB = 4
HS = H * S
EARLY = B - GB


class Chain:

    def __init__(self, eng, sem, base):
        self.eng, self.sem, self.base, self.n = eng, sem, base, 0

    def __call__(self, ins):
        self.n += 1
        ins.then_inc(self.sem, 1)
        self.eng.wait_ge(self.sem, self.base + self.n)


def spread(ap, shape):
    return ap.unsqueeze(len(ap.shape)).broadcast_to(shape)


def perceiver_kernel(nc, a, out):
    with ExitStack() as whole:
        def sb(name, shape, dt=F32, scope=whole):
            return scope.enter_context(nc.sbuf_tensor(name, shape, dt))

        ps = whole.enter_context(nc.psum_tensor("banks", [P, 8, 512], F32))
        w = {}
        w["ident"] = sb("ident", [P, P])
        w["ident16"] = sb("ident16", [P, P], F16)
        w["minus_half"] = sb("minus_half", [P, 16])
        names = ["a1_lnx_g", "a1_lnx_b", "a1_lny_g", "a1_lny_b", "a1_ln3_g", "a1_ln3_b",
                 "a2_lnx_g", "a2_lnx_b", "a2_ln3_g", "a2_ln3_b"]
        w["vec"] = sb("vec", [P, 32])
        w["vec_of"] = {"L0_xattn_" + n: i for i, n in enumerate(names)}
        w["vec_of"].update({"L0_ffn_ln_gamma": 10, "L0_ffn_ln_beta": 11,
                            "L0_xattn_a2_lny_g": 12, "L0_xattn_a2_lny_b": 13})
        w["li2_b"] = {n: sb(f"li2_b_{n}", [P, FT]) for n in ("a1", "a2")}
        rows = ["xattn_ln1_g", "xattn_ln1_b", "xattn_ln2_g", "xattn_ln2_b", "xattn_a1_li1_b", "xattn_a1_li3_b",
                "xattn_a2_li1_b", "xattn_a2_li3_b", "attn_bp"]
        w["row"] = sb("row", [P, len(rows), C])
        w["row_of"] = {"L0_" + n: i for i, n in enumerate(rows)}
        w["qkvz_b"] = sb("qkvz_b", [P, 4, C])
        w["li2"] = {n: sb(f"li2_{n}", [P, FF]) for n in ("a1", "a2")}
        w["li3"] = {n: sb(f"li3_{n}", [P, FT, C]) for n in ("a1", "a2")}
        w["query_fold"] = sb("query_fold", [P, H, 2, CY])
        w["value_fold"] = sb("value_fold", [P, H // 2, C])
        w["qkvz"] = sb("qkvz", [P, 4, C])
        w["wp"] = sb("wp", [P, C])
        w["upto"] = sb("upto", [P, P])
        w["before"] = sb("before", [P, P])
        w["prev"] = sb("prev", [P, P])
        w["next"] = sb("next", [P, P])
        w["sel"] = sb("sel", [P, 2, CY])
        w["later"] = sb("later", [P, S])
        w["t1T"] = sb("t1T", [P, 2 * NX, P], F16)
        w["t2T"] = sb("t2T", [P, 2 * NX, P])
        w["s1"] = sb("s1", [P, 2 * NX])
        w["s2"] = sb("s2", [P, NX])
        w["router"] = sb("router", [P, NE])
        w["iota_down"] = sb("iota_down", [P, NE])
        w["x3"] = sb("x3", [P, TOK // P, C])
        w["xqT"] = sb("xqT", [P, TOK])

        w["keys"] = sb("keys", [P, H // 4, GB, 4, S])
        w["context"] = Context(nc, a, w, lambda n, s: sb("context_" + n, s),
                               lambda n: whole.enter_context(nc.semaphore("x_" + n)))
        with ExitStack() as scope:
            w["a1"] = {n: sb(f"a1_{n}", [P, H, D], F32, scope) for n in ("wq", "wk", "wv")}
            w["a1"]["li1"] = sb("a1_li1", [P, 4, C], F32, scope)
            w["values"] = sb("values", [P, GB, H // 2, 2, D], F32, scope)
            with ExitStack() as inner:
                prepare_weights(nc, a, w, ps, lambda n, s, d=F32: sb("prep_" + n, s, d, inner))
            with ExitStack() as inner:
                latent_self_attention(nc, a, w, ps, lambda n, s, d=F32: sb("self_" + n, s, d, inner))
        w["attended"] = sb("attended", [P, B, 512])
        w["den"] = sb("den", [P, 2, B * 512 // P])
        with ExitStack() as inner:
            cross_attention(nc, a, w, ps, lambda n, s, d=F32: sb("cross_" + n, s, d, inner))
        with ExitStack() as inner:
            finish_tokens(nc, a, out, w, ps, lambda n, s, d=F32: sb("fin_" + n, s, d, inner))


def prepare_weights(nc, a, w, ps, sb):
    with ExitStack() as ctx:
        sem = lambda n: ctx.enter_context(nc.semaphore("p_" + n))
        wide = {"a2_wq": sb("w_a2_wq", [P, H, D])}
        narrow = {n: sb(f"w_{n}", [CY, H, D]) for n in ("a2_wk", "a2_wv")}
        narrow_g = {n: sb(f"wg_{n}", [CY, H, D]) for n in ("a2_wk", "a2_wv")}
        turned = {n: sb(f"t_{n}", [P, 4, P]) for n in wide}
        turned_raw = {n: sb(f"tr_{n}", [P, 4, CY]) for n in narrow}
        key_turned = sb("key_turned", [P, 4, 2, CY])
        value_turned = sb("value_turned", [P, 4, CY])
        li1 = sb("li1", [P, 4, C])
        w1 = sb("w1", [P, 2 * NX, C])
        w2 = sb("w2", [P, NX, FE])
        low1 = sb("low1", [P, 2 * NX, C])
        low2 = sb("low2", [P, NX, FE])
        half1 = sb("half1", [P, 2 * NX])
        half2 = sb("half2", [P, NX])
        neg1 = sb("neg1", [P, 2 * NX])
        neg2 = sb("neg2", [P, NX])
        router_rows = sb("router_rows", [NE, C])
        NT = TOK // P
        x = sb("x", [P, NT, C])
        n0 = sb("n0", [P, NT, C])
        var_ready, rstd_ready, x_in, x_normed = sem("var_ready"), sem("rstd_ready"), sem("x_in"), sem("x_normed")
        ln1_in = sem("ln1_in")
        norms = Norms(nc, sb, var_ready, rstd_ready, 3, "p", NT)
        attn_in, ffn_in, vec_in, rest_in = sem("attn_in"), sem("ffn_in"), sem("vec_in"), sem("rest_in")
        pool_steps = sem("pool_steps")
        dve_steps = sem("dve_steps")
        scaled, tern1, tern2, compared2 = sem("scaled"), sem("tern1"), sem("tern2"), sem("compared2")
        filled, by_act, by_dve = sem("filled"), sem("by_act"), sem("by_dve")
        attn_n = [0]
        ffn_n = [0]
        vec_n = [0]
        rest_n = [0]

        items = [("turn_wide", n) for n in wide] + [("turn_narrow", n) for n in narrow]
        items += [("value_bias", None)]
        items += [(k, r) for r in range(4) for k in ("query_fold", "value_fold")]
        items += [("turn_x", q) for q in range(NT // 4)] + [("router", None)]
        items += [("t1", q) for q in range(5)] + [("t2", q) for q in range(5)]

        by_vector = [kind in ("turn_narrow", "value_bias") for kind, k in items]

        def wait_taken(eng, n):
            of_dve = sum(by_vector[:n + 1])
            if of_dve:
                eng.wait_ge(by_dve, of_dve)
            eng.wait_ge(by_act, n + 1 - of_dve)

        with nc.Block() as block:
            @block.sync
            def _(sp):
                sp.dma_start(x[:, :, :], a["x"].rearrange("(i b) s c -> (b s) i c", b=2)).then_inc(x_in, 16)
                for n in ("L0_xattn_ln1_g", "L0_xattn_ln1_b"):
                    sp.dma_start(w["row"][:, w["row_of"][n], :], a[n].partition_broadcast(P)).then_inc(ln1_in, 16)
                for n, t in list(wide.items()) + list(narrow.items()):
                    sp.dma_start(t[:, :, :], a["L0_xattn_" + n].rearrange("h c d -> c h d")).then_inc(attn_in, 16)
                    attn_n[0] += 16
                sp.dma_start(li1[:, :, :], a["L0_xattn_a2_li1_w"].rearrange("(k p) c -> p k c", p=P)).then_inc(attn_in, 16)
                attn_n[0] += 16
                for n in ("wq", "wk", "wv"):
                    sp.dma_start(w["a1"][n][:, :, :], a["L0_xattn_a1_" + n].rearrange("h c d -> c h d")).then_inc(rest_in, 16)
                sp.dma_start(w["a1"]["li1"][:, :, :], a["L0_xattn_a1_li1_w"].rearrange("(k p) c -> p k c", p=P)).then_inc(rest_in, 16)
                rest_n[0] += 64
                sp.dma_start(w1[:, 0:2, :], a["L0_ffn_shared_w1"].rearrange("(k p) d -> p k d", p=P)).then_inc(ffn_in, 16)
                sp.dma_start(w1[:, 2:, :], a["L0_ffn_expert_w1"].rearrange("e (k p) d -> p (e k) d", p=P)).then_inc(ffn_in, 16)
                sp.dma_start(w2[:, 0, :], a["L0_ffn_shared_w2"]).then_inc(ffn_in, 16)
                sp.dma_start(w2[:, 1:, :], a["L0_ffn_expert_w2"].rearrange("e d f -> d e f")).then_inc(ffn_in, 16)
                sp.dma_start(router_rows[:, :], a["L0_ffn_router_w"]).then_inc(ffn_in, 16)
                ffn_n[0] = 80
                for n in ("a1", "a2"):
                    sp.dma_start(w["li2"][n][:, :], a[f"L0_xattn_{n}_li2_w"]).then_inc(rest_in, 16)
                    sp.dma_start(w["li3"][n][:, :, :], a[f"L0_xattn_{n}_li3_w"].rearrange("(k p) c -> p k c", p=P)).then_inc(rest_in, 16)
                    rest_n[0] += 32
                for k, n in enumerate(("Wq", "Wk1", "Wv", "Wk2")):
                    sp.dma_start(w["qkvz"][:, k, :], a["L0_attn_" + n]).then_inc(rest_in, 16)
                    rest_n[0] += 16
                sp.dma_start(w["wp"][:, :], a["L0_attn_Wp"]).then_inc(rest_in, 16)
                rest_n[0] += 16
                for n in ("a1", "a2"):
                    for f in range(FT):
                        src = a[f"L0_xattn_{n}_li2_b"][P * f:P * f + P]
                        sp.dma_start(w["li2_b"][n][:, f:f + 1], src.unsqueeze(1)).then_inc(rest_in, 16)
                        rest_n[0] += 16
                for n, i in w["row_of"].items():
                    if n in ("L0_xattn_ln1_g", "L0_xattn_ln1_b"):
                        continue
                    sp.dma_start(w["row"][:, i, :], a[n].partition_broadcast(P)).then_inc(rest_in, 16)
                    rest_n[0] += 16
                for k, n in enumerate(("bq", "bk1", "bv", "bk2")):
                    sp.dma_start(w["qkvz_b"][:, k, :], a["L0_attn_" + n].partition_broadcast(P)).then_inc(rest_in, 16)
                    rest_n[0] += 16
                sp.wait_ge(rest_in, rest_n[0])

            @block.scalar
            def _(act):
                for n, i in w["vec_of"].items():
                    src = a[n]
                    act.dma_start(w["vec"][0:src.shape[0], i:i + 1], src.unsqueeze(1)).then_inc(vec_in, 16)
                    vec_n[0] += 16
                for n, (kind, k) in enumerate(items):
                    if by_vector[n]:
                        continue
                    act.wait_ge(filled, n + 1)
                    bank = ps[:, n % 4, :]
                    four = bank.rearrange("p (k c) -> p k c", k=4)
                    if kind == "turn_wide":
                        last = act.copy(turned[k][:, :, :], four)
                    elif kind == "query_fold":
                        dst = w["query_fold"][:, :, :, :].rearrange("p (q r) u c -> p q r (u c)", r=4)[:, :, k, :]
                        last = act.copy(dst, four)
                    elif kind == "value_fold":
                        dst = w["value_fold"][:, :, :].rearrange("p (q r) c -> p q r c", r=4)[:, :, k, :]
                        last = act.copy(dst, bank[:, 0:2 * C].rearrange("p (k c) -> p k c", k=2))
                    elif kind == "turn_x":
                        last = act.copy(w["xqT"][:, 4 * P * k:4 * P * k + 4 * P], bank)
                    elif kind == "router":
                        last = act.copy(w["router"][:, :], bank[:, 0:NE])
                    else:
                        m = min(4, 2 * NX - 4 * k)
                        last = act.copy(w[kind + "T"][:, 4 * k:4 * k + m, :], four[:, 0:m, :])
                    last.then_inc(by_act, 1)

            @block.gpsimd
            def _(pool):
                step = Chain(pool, pool_steps, 0)

                def blocks(name):
                    return w[name][:, :].rearrange("p (b j) -> p b j", b=2)

                def keep(name, op, base, pattern, mult, fill=0.0, ap=None):
                    v = blocks(name) if ap is None else ap
                    step(pool.affine_select(out=v, in_=v, compare_op=op, fill=fill, base=base, pattern=pattern,
                                            channel_multiplier=mult))

                step(pool.memset(w["ident"][:, :], 0.0))
                keep("ident", ALU.not_equal, 0, [[-1, P]], 1, 1.0, w["ident"][:, :])
                step(pool.memset(w["keys"][:, :, :, :, :], 0.0))
                step(pool.memset(w["values"][:, :, :, :, :], 0.0))
                step(pool.tensor_copy(w["ident16"][:, :], w["ident"][:, :]))
                step(pool.memset(w["minus_half"][:, :], -0.5))
                for k in range(3):
                    norms.on_pool(pool, 0, k, w["minus_half"])
                for name, base in (("upto", 0), ("before", -1)):
                    step(pool.memset(w[name][:, :], 1.0))
                    keep(name, ALU.is_ge, base, [[64, 2], [1, 64]], -1)
                    keep(name, ALU.is_ge, 0, [[-64, 2], [0, 64]], 1)
                step(pool.memset(w["prev"][:, :], 0.0))
                keep("prev", ALU.not_equal, 1, [[-64, 2], [-1, 64]], 1, 1.0)
                keep("prev", ALU.is_ge, 0, [[-64, 2], [0, 64]], 1)
                step(pool.memset(w["next"][:, :], 0.0))
                keep("next", ALU.not_equal, -1, [[-64, 2], [-1, 64]], 1, 1.0)
                keep("next", ALU.is_ge, 63, [[64, 2], [0, 64]], -1)
                step(pool.memset(w["sel"][:, :, :], 0.0))
                step(pool.affine_select(out=w["sel"][:, :, :], in_=w["sel"][:, :, :], compare_op=ALU.not_equal, fill=1.0,
                                        base=0, pattern=[[-64, 2], [0, CY]], channel_multiplier=1))
                step(pool.memset(w["later"][:, :], 1.0))
                for p0 in (0, S):
                    v = w["later"][p0:p0 + S, :]
                    step(pool.affine_select(out=v, in_=v, compare_op=ALU.is_ge, fill=0.0, base=-1,
                                            pattern=[[1, S]], channel_multiplier=-1))
                for e in range(NE):
                    step(pool.memset(w["iota_down"][:, e:e + 1], float(NE - e)))
                pool.wait_ge(compared2, 1)
                step(pool.tensor_tensor(w2[:, :, :], w2[:, :, :], low2[:, :, :], ALU.subtract))
                pool.tensor_tensor(w2[:, :, :], w2[:, :, :], spread(w["s2"][:, :], [P, NX, FE]), ALU.mult).then_inc(tern2, 1)

            @block.vector
            def _(dve):
                step = Chain(dve, dve_steps, 0)
                dve.wait_ge(x_in, 16)
                norms.moments(dve, step, x)
                def thresholds(wide_w, scale, half, neg, width):
                    step(nc.vector.tensor_reduce(half[:, :], wide_w[:, :, :], AX.X, ALU.add, apply_absolute_value=True))
                    step(nc.vector.tensor_scalar(scale[:, :], half[:, :], 1.0 / width, MAGIC_MIN_SCALE, ALU.mult, ALU.max))
                    step(nc.vector.tensor_scalar(half[:, :], scale[:, :], 0.5, None, ALU.mult))
                    step(nc.vector.tensor_scalar(neg[:, :], scale[:, :], -0.5, None, ALU.mult))

                def below(wide_w, low, neg, n, width):
                    step(nc.vector.tensor_tensor(low[:, :, :], wide_w[:, :, :], spread(neg[:, :], [P, n, width]), ALU.is_lt))

                def above(wide_w, half, n, width):
                    return nc.vector.tensor_tensor(wide_w[:, :, :], wide_w[:, :, :], spread(half[:, :], [P, n, width]), ALU.is_gt)

                step(norms.apply(dve, 0, 0, n0, x))
                dve.wait_ge(attn_in, attn_n[0])
                dve.wait_ge(vec_in, vec_n[0])
                g_y = w["vec_of"]["L0_xattn_a2_lny_g"]
                for n in narrow:
                    nc.vector.tensor_scalar(narrow_g[n][:, :, :], narrow[n][:, :, :], w["vec"][0:CY, g_y:g_y + 1], None,
                                            ALU.mult).then_inc(scaled, 1)
                norms.moments(dve, step, n0)
                for n, (kind, k) in enumerate(items):
                    if not by_vector[n]:
                        continue
                    dve.wait_ge(filled, n + 1)
                    bank = ps[:, n % 4, :]
                    if kind == "turn_narrow":
                        raw = turned_raw[k]
                        step(nc.vector.tensor_copy(raw[:, :, :], bank[:, 0:4 * CY].rearrange("p (k c) -> p k c", k=4)))
                        for q in range(4):
                            for u in range(2 if k == "a2_wk" else 1):
                                dst = key_turned[:, q, u, :] if k == "a2_wk" else value_turned[:, q, :]
                                last = nc.vector.tensor_scalar(dst, raw[:, q, :], raw[:, q, 0:1],
                                                               QUERY_SCALE if k == "a2_wk" else 1.0, ALU.subtract, ALU.mult)
                    else:
                        dve.wait_ge(by_dve, 2)
                        last = nc.vector.tensor_copy(value_turned[:, :, 0], bank[:, 0:4])
                    last.then_inc(by_dve, 1)
                dve.wait_ge(ffn_in, ffn_n[0])
                thresholds(w2, w["s2"], half2, neg2, FE)
                step(norms.apply(dve, 0, 1, n0, n0))
                dve.wait_ge(ln1_in, 32)
                step(nc.vector.tensor_tensor(n0[:, :, :], n0[:, :, :], wide_row(w, "L0_xattn_ln1_g", NT), ALU.mult))
                step(nc.vector.tensor_tensor(w["x3"][:, :, :], n0[:, :, :], wide_row(w, "L0_xattn_ln1_b", NT), ALU.add))
                norms.moments(dve, step, w["x3"])
                below(w2, low2, neg2, NX, FE)
                norms.apply(dve, 0, 2, n0, w["x3"]).then_inc(x_normed, 1)
                above(w2, half2, NX, FE).then_inc(compared2, 1)
                thresholds(w1, w["s1"], half1, neg1, C)
                below(w1, low1, neg1, 2 * NX, C)
                step(above(w1, half1, 2 * NX, C))
                nc.vector.tensor_tensor(w1[:, :, :], w1[:, :, :], low1[:, :, :], ALU.subtract).then_inc(tern1, 1)
                dve.wait_ge(tern1, 1)

            @block.tensor
            def _(pe):
                pe.wait_ge(attn_in, attn_n[0])
                pe.wait_ge(pool_steps, 2)
                ident = w["ident"]
                for n, (kind, k) in enumerate(items):
                    if n >= 4:
                        wait_taken(pe, n - 4)
                    bank = ps[:, n % 4, :]
                    four = bank.rearrange("p (k c) -> p k c", k=4)
                    r0 = 32 * k if isinstance(k, int) and k < 4 else 0
                    if kind == "turn_wide":
                        flat = wide[k][:, :, :].rearrange("p (q r) d -> p q (r d)", q=4)
                        for q in range(4):
                            last = nc.tensor.transpose(four[:, q, :], flat[:, q, :], ident[:, :])
                    elif kind == "turn_narrow":
                        pe.wait_ge(scaled, 2)
                        flat = narrow_g[k][:, :, :].rearrange("p (q r) d -> p q (r d)", q=4)
                        for q in range(4):
                            last = nc.tensor.transpose(bank[:, CY * q:CY * q + CY], flat[:, q, :], ident[0:CY, 0:CY])
                    elif kind == "value_bias":
                        pe.wait_ge(vec_in, vec_n[0])
                        flat = narrow["a2_wv"][:, :, :].rearrange("p (q r) d -> p q (r d)", q=4)
                        b_y = w["vec_of"]["L0_xattn_a2_lny_b"]
                        for q in range(4):
                            last = nc.tensor.matmul(bank[:, q:q + 1], flat[:, q, :], w["vec"][0:CY, b_y:b_y + 1], start=True, stop=True)
                    elif kind == "router":
                        pe.wait_ge(ffn_in, ffn_n[0])
                        last = nc.tensor.transpose(bank[:, 0:NE], router_rows[:, :], ident[0:NE, 0:NE])
                    elif kind == "turn_x":
                        pe.wait_ge(x_normed, 1)
                        for q in range(4):
                            last = nc.tensor.transpose(four[:, q, :], n0[:, 4 * k + q, :], ident[:, :])
                    elif kind in ("t1", "t2"):
                        pe.wait_ge(tern1 if kind == "t1" else tern2, 1)
                        src = w1[:, :, :] if kind == "t1" else w2[:, :, :].rearrange("p e (k f) -> p (e k) f", k=2)
                        for q in range(min(4, 2 * NX - 4 * k)):
                            last = nc.tensor.transpose(four[:, q, :], src[:, 4 * k + q, :], ident[:, :])
                    else:
                        wait_taken(pe, 3)
                        for q in range(4):
                            rows = slice(r0, r0 + D)
                            if kind == "query_fold":
                                o, l = four[:, q, :], turned["a2_wq"][rows, q, :]
                                r = key_turned[rows, q, :, :].rearrange("p u c -> p (u c)")
                            else:
                                o = ps[CY * (q // 2):CY * (q // 2) + CY, n % 4, C * (q % 2):C * (q % 2) + C]
                                l, r = value_turned[rows, q, :], li1[rows, q, :]
                            last = nc.tensor.matmul(o, l, r, start=True, stop=True)
                    last.then_inc(filled, 1)


class Norms:

    def __init__(self, nc, sb, var_ready, rstd_ready, per, tag, tiles=GT):
        self.nc, self.per, self.var_ready, self.rstd_ready, self.tiles = nc, per, var_ready, rstd_ready, tiles
        self.stats = sb("stats_" + tag, [P, tiles, 6])
        self.mv = sb("mv_" + tag, [P, tiles, 2])
        self.var = sb("var_" + tag, [P, tiles])
        self.rstd = sb("rstd_" + tag, [P, tiles])

    def moments(self, dve, step, src):
        nc = self.nc
        for i in range(self.tiles):
            last = nc.vector.bn_stats(self.stats[:, i, :], src[:, i, :])
        dve.drain()
        for i in range(self.tiles):
            last = nc.vector.bn_aggr(self.mv[:, i, :], self.stats[:, i, :])
        step(last)
        nc.vector.tensor_scalar(self.var[:, :], self.mv[:, :, 1], EPS, None, ALU.add).then_inc(self.var_ready, 1)

    def apply(self, dve, g, k, dst, src):
        dve.wait_ge(self.rstd_ready, g * self.per + (k + 1))
        for i in range(self.tiles):
            last = self.nc.vector.tensor_scalar(dst[:, i, :], src[:, i, :], self.mv[:, i, 0:1], self.rstd[:, i:i + 1],
                                                ALU.subtract, ALU.mult)
        return last

    def on_vector(self, dve, step, g, k, dst, src):
        self.moments(dve, step, src)
        return self.apply(dve, g, k, dst, src)

    def on_pool(self, pool, g, k, minus_half):
        pool.wait_ge(self.var_ready, g * self.per + (k + 1))
        pool.tensor_tensor(self.rstd[:, :], self.var[:, :], minus_half[:, 0:self.tiles], ALU.pow).then_inc(self.rstd_ready, 1)


def wide_row(w, name, tiles=GT):
    i = w["row_of"][name]
    return w["row"][:, i:i + 1, :].broadcast_to([P, tiles, C])


def latent_self_attention(nc, a, w, ps, sb):
    with ExitStack() as ctx:
        sem = lambda n: ctx.enter_context(nc.semaphore("s_" + n))
        n0 = sb("n0", [P, GT, C])
        xo = sb("xo", [P, GT, C])
        x3 = sb("x3_group", [P, GT, C])
        xnT = sb("xnT", [P, GN])
        ynT = sb("ynT", [P, GN])
        h3T = sb("h3T", [P, GN])
        keys, values = w["keys"], w["values"]
        queries = sb("queries", [P, H // 4, GN])
        att = sb("att", [P, 2, H // 4, P])
        mx = sb("mx", [P, 2, H])
        den = sb("den", [P, 2, H])
        rden = sb("rden", [P, 2, H])
        prob = sb("prob", [P, GT, H, S])
        probT = sb("probT", [P, 2, H // 2, P])
        hid = sb("hid", [P, FT, GN])
        dve_steps = sem("dve_steps")
        late_steps = sem("late_steps")
        var_ready, rstd_ready = sem("var_ready"), sem("rstd_ready")
        xy_ready = sem("xy_ready")
        items_filled, items_by_act, items_by_dve = sem("items_filled"), sem("items_by_act"), sem("items_by_dve")
        scored, shifted, exped, normed, masked = (sem("scored"), sem("shifted"), sem("exped"), sem("normed"), sem("masked"))
        probs_turned, probT_ready, attended_pair = sem("probs_turned"), sem("probT_ready"), sem("attended_pair")
        summed, att_ready = sem("summed"), sem("att_ready")
        n3_ready, n3_turned, h3_ready = sem("n3_ready"), sem("n3_turned"), sem("h3_ready")
        hid_filled, hid_ready, mlp_done = sem("hid_filled"), sem("hid_ready"), sem("mlp_done")
        started, residual = sem("started"), sem("residual")
        x3_ready, q_normed, q_turned, q_taken = sem("x3_ready"), sem("q_normed"), sem("q_turned"), sem("q_taken")
        NORMS = 3
        norms = Norms(nc, sb, var_ready, rstd_ready, NORMS, "s")
        pairs = GT
        QUERY, KEY, VALUE, ITEMS = 0, 4, 8, 12
        TURN, SUMS = 7, 6
        HID = 4
        vec = lambda n: w["vec"][:, w["vec_of"]["L0_xattn_" + n]:w["vec_of"]["L0_xattn_" + n] + 1]
        ON_PE = """turn3 scores0 scores1 hid0 hid1 scores2 hid2 hid3 scores3 mlp turn_probs0 sums0 item0 turn_probs1 item1 item2
                   sums1 out0 turn_probs2 item3 sums2 out1 turn_probs3 sums3 out2 out3 item4 turnq item5 item6 item7
                   item8 item9 item10 item11"""
        ON_ACT = """turn3 exp0 exp1 hid0 hid1 hid2 hid3 exp2 probs0 exp3 features att0 item0 probs1 item1 item2 att1 probs2 item3
                    att2 probs3 att3 item4 turnq item5 item6 item7 item8 item9 item10 item11"""
        ON_DVE = """shift0 shift1 normalise0 shift2 normalise1 shift3 moments4 normalise2 normalise3 item0 item1 apply4 item2 item3
                    moments5 apply5 start moments3 item4 item5 item6 apply3 item7 item8 item9 item10 item11"""
        ON_POOL = "mask0 mask1 power4 mask2 mask3 power5 power3"
        BEFORE = ("turn3", "hid", "mlp", "moments4", "apply4", "moments5", "apply5", "turnq", "power4", "power5")
        NEXT = ("item", "features")

        def stages(order, kinds):
            named = []
            for word in order.split():
                name = word if word in BEFORE or word in ("moments3", "apply3", "power3") else word.rstrip("0123456789")
                kind = "before" if name in BEFORE else "next" if name in NEXT else "this"
                if kind in kinds:
                    named.append((name, int(word[len(name):] or 0)))
            return named

        def passes(engine, order, walk, between=lambda x: None):
            walk(stages(" ".join(w for w in order.split() if w.startswith("item")), ("next",)), -1)
            walk(stages(order, ("this", "next")), 0)
            with engine.Fori(0, GROUPS - 2) as g:
                walk(stages(order, ("before", "this", "next")), g + 1)
            walk(stages(order, ("before", "this")), GROUPS - 1)
            between(GROUPS)
            walk(stages(order, ("before",)), GROUPS)

        assert GT == 4

        def item_parts(n):
            bank = n % 4
            if n < KEY:
                return [[(queries[S * h:S * h + S, n, :], ps[S * h:S * h + S, bank, :])] for h in range(2)]
            if n < VALUE:
                block = lambda r: (keys[D * r:D * r + D, n - KEY, :, r, :], ps[D * r:D * r + D, bank, :].rearrange("p (b t) -> p b t", b=GB))
                return [[block(0), block(1)], [block(2), block(3)]]
            rows = lambda j: slice(S * j, S * j + S)
            m = 2 * (n - VALUE)
            return [[(values[rows(j), m + u, :, j, :], ps[rows(j), bank, 256 * u:256 * u + 256].rearrange("p (k d) -> p k d", d=D)) for u in range(2)]
                    for j in range(2)]

        context = w["context"]

        with nc.Block() as block:
            @block.sync
            def _(sp):
                for x in range(2):
                    context.load(sp, x, x)

            @block.gpsimd
            def _(pool):
                def walk(order, x):
                    for stage, p in order:
                        if stage == "mask":
                            pool.wait_ge(normed, x * pairs + (p + 1))
                            pool.tensor_tensor(prob[:, p, :, :], prob[:, p, :, :],
                                               w["later"][:, :].unsqueeze(1).broadcast_to([P, H, S]), ALU.mult).then_inc(masked, 1)
                        elif stage == "power3":
                            norms.on_pool(pool, x, 0, w["minus_half"])
                        else:
                            norms.on_pool(pool, x - 1, 1 if stage == "power4" else 2, w["minus_half"])

                def context_of_0(x):
                    pool.wait_ge(scored, GROUPS * pairs)
                    pool.wait_ge(rstd_ready, GROUPS * NORMS - 2)
                    context.clear(pool)
                    context.normalise(pool, 0, 0)
                    context.split(pool, 0, 0)

                passes(pool, ON_POOL, walk, context_of_0)
                context.normalise(pool, 1, 1)

            @block.vector
            def _(dve):
                tt = nc.vector.tensor_tensor
                four = lambda b: ps[:, b, :].rearrange("p (i c) -> p i c", i=GT)

                THIS, LATE = 14, 6

                def walk(order, x):
                    y = x - 1
                    step, late = Chain(dve, dve_steps, x * THIS), Chain(dve, late_steps, y * LATE)
                    x1 = lambda: w["x3"][:, bass.ds(x * GT, GT), :]
                    for stage, p in order:
                        if stage == "shift":
                            dve.wait_ge(scored, x * pairs + (p + 1))
                            sc = ps[:, 2 * (p % 2):2 * (p % 2) + 2, :].rearrange("p k (h t) -> p (k h) t", t=S)
                            step(nc.vector.tensor_reduce(mx[:, p % 2, :], sc, AX.X, ALU.max))
                            tt(prob[:, p, :, :], sc, spread(mx[:, p % 2, :], [P, H, S]), ALU.subtract).then_inc(shifted, 1)
                        elif stage == "normalise":
                            dve.wait_ge(exped, x * pairs + (p + 1))
                            step(nc.vector.tensor_reduce(den[:, p % 2, :], prob[:, p, :, :], AX.X, ALU.add))
                            step(nc.vector.reciprocal(rden[:, p % 2, :], den[:, p % 2, :]))
                            tt(prob[:, p, :, :], prob[:, p, :, :], spread(rden[:, p % 2, :], [P, H, S]), ALU.mult).then_inc(normed, 1)
                        elif stage == "item":
                            dve.wait_ge(items_filled, (x + 1) * ITEMS + (p + 1))
                            for dst, src in item_parts(p)[1]:
                                last = nc.vector.tensor_copy(dst, src)
                            last.then_inc(items_by_dve, 1)
                        elif stage == "start":
                            tt(xo[:, :, :], x1(), wide_row(w, "L0_xattn_a1_li1_b"), ALU.add).then_inc(started, 1)
                        elif stage == "moments3":
                            dve.wait_ge(started, x + 1)
                            dve.wait_ge(attended_pair, x * pairs + pairs)
                            step(tt(xo[:, :, :], xo[:, :, :], four(SUMS), ALU.add))
                            norms.moments(dve, step, xo)
                        elif stage == "apply3":
                            if not (isinstance(x, int) and x == 0):
                                dve.wait_ge(q_turned, x)
                            norms.apply(dve, x, 0, n0, xo).then_inc(n3_ready, 1)
                            dve.wait_ge(n3_ready, x + 1)
                            tt(xo[:, :, :], xo[:, :, :], x1(), ALU.add).then_inc(residual, 1)
                            dve.wait_ge(residual, x * 2 + 1)
                            tt(xo[:, :, :], xo[:, :, :], wide_row(w, "L0_xattn_a1_li3_b"), ALU.add).then_inc(residual, 1)
                        elif stage == "moments4":
                            dve.wait_ge(residual, x * 2)
                            dve.wait_ge(mlp_done, x)
                            late(tt(xo[:, :, :], xo[:, :, :], four(SUMS), ALU.add))
                            norms.moments(dve, late, xo)
                        elif stage == "apply4":
                            late(norms.apply(dve, y, 1, xo, xo))
                            late(tt(xo[:, :, :], xo[:, :, :], wide_row(w, "L0_xattn_ln2_g"), ALU.mult))
                            tt(x3[:, :, :], xo[:, :, :], wide_row(w, "L0_xattn_ln2_b"), ALU.add).then_inc(x3_ready, 1)
                            late(tt(w["x3"][:, bass.ds(y * GT, GT), :], xo[:, :, :], wide_row(w, "L0_xattn_ln2_b"), ALU.add))
                        elif stage == "moments5":
                            dve.wait_ge(x3_ready, x)
                            norms.moments(dve, late, x3)
                        elif stage == "apply5":
                            norms.apply(dve, y, 2, n0, x3).then_inc(q_normed, 1)
                    assert step.n in (0, THIS) and late.n in (0, LATE), (step.n, late.n)

                def context_of_both(x):
                    context.means(dve, 0, 0)
                    context.variances(dve, 0)
                    context.means(dve, 1, 1)

                passes(dve, ON_DVE, walk, context_of_both)
                context.variances(dve, 1)

            @block.scalar
            def _(act):
                act.sem_inc(q_taken, 1)

                def features(x):
                    src = w["xqT"][:, bass.ds(x * GN, GN)]
                    act.activation(xnT[:, :], src, ACT.Identity, scale=vec("a1_lnx_g"), bias=vec("a1_lnx_b")).then_inc(xy_ready, 1)
                    act.activation(ynT[:, :], src, ACT.Identity, scale=vec("a1_lny_g"), bias=vec("a1_lny_b")).then_inc(xy_ready, 1)

                def walk(order, x):
                    for stage, p in order:
                        if stage == "exp":
                            act.wait_ge(shifted, x * pairs + (p + 1))
                            act.activation(prob[:, p, :, :], prob[:, p, :, :], ACT.Exp, scale=SCORE_SCALE).then_inc(exped, 1)
                        elif stage == "probs":
                            act.wait_ge(probs_turned, x * pairs + (p + 1))
                            if p >= 2:
                                act.wait_ge(summed, x * pairs + (p - 1))
                            act.copy(probT[:, p % 2, :, :], ps[:, HID:HID + 2, :].rearrange("p k (h s) -> p (k h) s", s=P)).then_inc(probT_ready, 1)
                        elif stage == "att":
                            act.wait_ge(summed, x * pairs + (p + 1))
                            if p >= 2:
                                act.wait_ge(attended_pair, x * pairs + (p - 1))
                            act.copy(att[:, p % 2, :, :], ps[:, TURN, :].rearrange("p (k s) -> p k s", s=P)).then_inc(att_ready, 1)
                        elif stage == "features":
                            act.wait_ge(items_filled, (x + 1) * ITEMS)
                            features(x + 1)
                        elif stage == "item":
                            act.wait_ge(items_filled, (x + 1) * ITEMS + (p + 1))
                            for dst, src in item_parts(p)[0]:
                                last = act.copy(dst, src)
                            last.then_inc(items_by_act, 1)
                        elif stage == "turn3":
                            act.wait_ge(n3_turned, x)
                            act.activation(h3T[:, :], ps[:, TURN, :], ACT.Identity, scale=vec("a1_ln3_g"), bias=vec("a1_ln3_b")).then_inc(h3_ready, 1)
                        elif stage == "hid":
                            act.wait_ge(hid_filled, (x - 1) * FT + (p + 1))
                            act.activation(hid[:, p, :], ps[:, HID + p % 2, :], ACT.Gelu, bias=w["li2_b"]["a1"][:, p:p + 1]).then_inc(hid_ready, 1)
                        elif stage == "turnq":
                            act.wait_ge(q_turned, x)
                            act.activation(w["xqT"][:, bass.ds((x - 1) * GN, GN)], ps[:, TURN, :], ACT.Identity, scale=vec("a2_lnx_g"),
                                           bias=vec("a2_lnx_b")).then_inc(q_taken, 1)

                features(0)
                passes(act, ON_ACT, walk)
                act.wait_ge(q_taken, GROUPS + 1)

            @block.tensor
            def _(pe):
                ident = w["ident"]

                def turn(src, done):
                    for i in range(GT):
                        last = nc.tensor.transpose(ps[:, TURN, P * i:P * i + P], src[:, i, :], ident[:, :])
                    last.then_inc(done, 1)

                def walk(order, x):
                    y = x - 1
                    for stage, p in order:
                        if stage == "item":
                            if p == 0:
                                pe.wait_ge(xy_ready, (x + 1) * 2 + 2)
                                if not (isinstance(x, int) and x < 0):
                                    pe.wait_ge(shifted, x * pairs + pairs)
                            if p >= 4:
                                pe.wait_ge(items_by_act, (x + 1) * ITEMS + (p - 3))
                                pe.wait_ge(items_by_dve, (x + 1) * ITEMS + (p - 3))
                            if p < VALUE:
                                weights = w["a1"]["wq" if p < KEY else "wk"][:, 4 * (p % 4):4 * (p % 4) + 4, :].rearrange("p h d -> p (h d)")
                                last = nc.tensor.matmul(ps[:, p % 4, :], weights, (xnT if p < KEY else ynT)[:, :], start=True, stop=True)
                            else:
                                for u in range(2):
                                    b = 2 * (p - VALUE) + u
                                    for j in range(2):
                                        last = nc.tensor.matmul(ps[S * j:S * j + S, p % 4, 256 * u:256 * u + 256], ynT[:, S * b:S * b + S],
                                                                w["a1"]["wv"][:, j::2, :], start=True, stop=True)
                            last.then_inc(items_filled, 1)
                        elif stage == "scores":
                            if p < 2:
                                pe.wait_ge(items_by_act, x * ITEMS + ITEMS)
                                pe.wait_ge(items_by_dve, x * ITEMS + ITEMS)
                            else:
                                pe.wait_ge(shifted, x * pairs + (p - 1))
                            for q in range(H // 4):
                                for u in range(2):
                                    b = 2 * p + u
                                    last = nc.tensor.matmul(ps[S * u:S * u + S, 2 * (p % 2) + q // 2, 256 * (q % 2):256 * (q % 2) + 256],
                                                            queries[:, q, S * b:S * b + S], keys[:, q, b, :, :].rearrange("p h t -> p (h t)"),
                                                            start=True, stop=True)
                            last.then_inc(scored, 1)
                        elif stage == "turn_probs":
                            pe.wait_ge(masked, x * pairs + (p + 1))
                            if p >= 1:
                                pe.wait_ge(probT_ready, x * pairs + p)
                            flat = prob[:, p, :, :].rearrange("p (k j) t -> p k (j t)", j=2)
                            for k in range(H // 2):
                                last = nc.tensor.transpose(ps[:, HID + k // 4, P * (k % 4):P * (k % 4) + P], flat[:, k, :], ident[:, :])
                            last.then_inc(probs_turned, 1)
                        elif stage == "sums":
                            pe.wait_ge(probT_ready, x * pairs + (p + 1))
                            if p >= 1:
                                pe.wait_ge(att_ready, x * pairs + p)
                            for k in range(H // 2):
                                for u in range(2):
                                    last = nc.tensor.matmul(ps[S * (k % 2):S * (k % 2) + S, TURN, P * (k // 2) + S * u:P * (k // 2) + S * u + S],
                                                            values[:, 2 * p + u, k, :, :].rearrange("p j d -> p (j d)"),
                                                            probT[:, p % 2, k, S * u:S * u + S], start=True, stop=True)
                            last.then_inc(summed, 1)
                        elif stage == "out":
                            pe.wait_ge(att_ready, x * pairs + (p + 1))
                            if p == 0 and not (isinstance(x, int) and x == 0):
                                pe.wait_ge(x3_ready, x)
                            for q in range(H // 4):
                                last = nc.tensor.matmul(ps[:, SUMS, C * p:C * p + C], att[:, p % 2, q, :], w["a1"]["li1"][:, q, :],
                                                        start=(q == 0), stop=(q == H // 4 - 1))
                            last.then_inc(attended_pair, 1)
                        elif stage == "turn3":
                            pe.wait_ge(n3_ready, x)
                            pe.wait_ge(q_taken, x)
                            turn(n0, n3_turned)
                        elif stage == "hid":
                            if p == 0:
                                pe.wait_ge(h3_ready, x)
                            if p >= 2:
                                pe.wait_ge(hid_ready, y * FT + (p - 1))
                            nc.tensor.matmul(ps[:, HID + p % 2, :], w["li2"]["a1"][:, P * p:P * p + P], h3T[:, :], start=True, stop=True).then_inc(hid_filled, 1)
                        elif stage == "mlp":
                            pe.wait_ge(hid_ready, y * FT + FT)
                            for i in range(GT):
                                for f in range(FT):
                                    last = nc.tensor.matmul(ps[:, SUMS, C * i:C * i + C], hid[:, f, P * i:P * i + P], w["li3"]["a1"][:, f, :],
                                                            start=(f == 0), stop=(f == FT - 1))
                            last.then_inc(mlp_done, 1)
                        elif stage == "turnq":
                            pe.wait_ge(q_normed, x)
                            if not (isinstance(x, int) and x == GROUPS):
                                pe.wait_ge(att_ready, x * pairs + pairs)
                            turn(n0, q_turned)

                passes(pe, ON_PE, walk)


def denominators(w, half, b0, b1):
    row = w["attended"][CY * half:CY * half + 1, b0:b1, :].rearrange("p b n -> p (b n)")
    return row, w["den"][:, half, b0 * 512 // P:b1 * 512 // P]


class Context:

    def __init__(self, nc, a, w, sb, sem):
        self.nc, self.a, self.w = nc, a, w
        flat = w["keys"][:, :, :, :, :].rearrange("p q b r t -> p (q b r t)")
        size = TJ * CY
        cut = lambda n, k: flat[:, size * n:size * (n + k)]
        self.raw = cut(0, 2).rearrange("p (k j c) -> p k j c", k=2, c=CY)
        self.n = cut(2, HB).rearrange("p (k j c) -> p k j c", k=HB, c=CY)
        self.squares = cut(2 + HB, 1).rearrange("p (j c) -> p j c", c=CY)
        self.parts = cut(3 + HB, 1).bitcast(F16).rearrange("p (j u c) -> p j u c", u=2, c=CY)
        self.ones = sb("ones", [P, TJ])
        self.total = sb("total", [P, TJ])
        self.mean = sb("mean", [P, 2, TJ])
        self.square_sum = sb("square_sum", [P, TJ])
        self.var = sb("var", [P, TJ])
        self.rstd = sb("rstd", [P, TJ])
        self.raw_in = [sem(f"raw_in{k}") for k in range(2)]
        self.raw_free, self.mean_ready, self.squares_ready, self.var_ready = (
            sem("raw_free"), sem("mean_ready"), sem("squares_ready"), sem("var_ready"))
        self.pool_steps, self.ctx_ready, self.parts_ready, self.parts_turned = (
            sem("pool_steps"), sem("ctx_ready"), sem("parts_ready"), sem("parts_turned"))
        self.dve_steps, self.high_ready = sem("dve_steps"), sem("high_ready")

    def load(self, sp, x, slot):
        sp.wait_ge(self.raw_free, x + 1)
        src = self.a["ctx_512"][bass.ds(x, 1), :, :].rearrange("o t c -> (o t) c")
        sp.dma_start(self.raw[:, slot % 2, 0:TJ - 1, :], src[0:P * (TJ - 1), :].rearrange("(p j) c -> p j c", j=TJ - 1)).then_inc(self.raw_in[slot % 2], 16)
        sp.dma_start(self.raw[0:TLAST, slot % 2, TJ - 1, :], src[P * (TJ - 1):T, :]).then_inc(self.raw_in[slot % 2], 16)

    def clear(self, pool):
        pool.memset(self.raw[64:P, :, TJ - 1, :], 0.0).then_inc(self.raw_free, 1)
        pool.wait_ge(self.raw_free, 1)
        pool.memset(self.ones[:, :], 1.0).then_inc(self.pool_steps, 1)
        pool.wait_ge(self.pool_steps, 1)
        pool.sem_inc(self.raw_free, 1)

    def normalise(self, pool, x, slot):
        base = x * 2 + 1
        n = self.n[:, slot, :, :]
        pool.wait_ge(self.mean_ready, x + 1)
        pool.tensor_tensor(n, self.raw[:, slot % 2, :, :], spread(self.mean[:, slot % 2, :], [P, TJ, CY]), ALU.subtract).then_inc(self.raw_free, 1)
        pool.wait_ge(self.raw_free, x + 3)
        pool.tensor_tensor(self.squares, n, n, ALU.mult).then_inc(self.squares_ready, 1)
        pool.wait_ge(self.var_ready, x + 1)
        pool.tensor_tensor(self.rstd[:, :], self.var[:, :], self.w["minus_half"][:, 0:TJ], ALU.pow).then_inc(self.pool_steps, 1)
        pool.wait_ge(self.pool_steps, base + 1)
        pool.tensor_tensor(n, n, spread(self.rstd[:, :], [P, TJ, CY]), ALU.mult).then_inc(self.pool_steps, 1)
        pool.wait_ge(self.pool_steps, base + 2)
        pool.tensor_tensor(n[:, :, 0:1], spread(self.ones[:, :], [P, TJ, 1]), spread(self.ones[:, :], [P, TJ, 1]), ALU.mult).then_inc(self.ctx_ready, 1)

    def split(self, pool, x, slot):
        n = self.n[:, slot, :, :]
        pool.wait_ge(self.ctx_ready, x + 1)
        if not (isinstance(x, int) and x == 0):
            pool.wait_ge(self.parts_turned, x)
        pool.tensor_tensor(self.parts[:, :, 0, :], n, spread(self.ones[:, :], [P, TJ, CY]), ALU.mult).then_inc(self.high_ready, 1)
        pool.wait_ge(self.high_ready, x + 1)
        pool.tensor_tensor(self.parts[:, :, 1, :], n, self.parts[:, :, 0, :], ALU.subtract).then_inc(self.parts_ready, 1)

    def means(self, dve, x, slot):
        dve.wait_ge(self.raw_in[slot % 2], (x - slot % 2) * 16 + 32)
        self.nc.vector.tensor_reduce(self.total[:, :], self.raw[:, slot % 2, :, :], AX.X, ALU.add).then_inc(self.dve_steps, 1)
        dve.wait_ge(self.dve_steps, x * 2 + 1)
        self.nc.vector.tensor_scalar(self.mean[:, slot % 2, :], self.total[:, :], 1.0 / CY, None, ALU.mult).then_inc(self.mean_ready, 1)

    def variances(self, dve, x):
        dve.wait_ge(self.squares_ready, x + 1)
        self.nc.vector.tensor_reduce(self.square_sum[:, :], self.squares, AX.X, ALU.add).then_inc(self.dve_steps, 1)
        dve.wait_ge(self.dve_steps, x * 2 + 2)
        self.nc.vector.tensor_scalar(self.var[:, :], self.square_sum[:, :], 1.0 / CY, EPS, ALU.mult, ALU.add).then_inc(self.var_ready, 1)


def cross_attention(nc, a, w, ps, sb):
    RING, SCORE, SUM = 4, 0, 7
    with ExitStack() as ctx:
        sem = lambda n: ctx.enter_context(nc.semaphore("c_" + n))
        context = w["context"]
        ctx_n, ctx_parts = context.n, context.parts
        ctx_T = sb("ctx_T", [P, HB, TJ * P], F16)
        q_hi = sb("q_hi", [P, HB, HS], F16)
        q_lo = sb("q_lo", [P, HB, HS], F16)
        part_max = sb("part_max", [P, H // 2, 4])
        neg_max = sb("neg_max", [P, H // 2])
        max_rows = sb("max_rows", [H // 2, P], F16)
        expd = sb("expd", [P, 2, HS])
        ctx_ready, parts_ready, parts_turned = context.ctx_ready, context.parts_ready, context.parts_turned
        ring_filled, ring_done, hi_done = sem("ring_filled"), sem("ring_done"), sem("hi_done")
        max_ready, rows_ready, rows_in = sem("max_ready"), sem("rows_ready"), sem("rows_in")
        scored, exp_done, summed, sum_out = sem("scored"), sem("exp_done"), sem("summed"), sem("sum_out")
        den_in, den_inv, inv_in = sem("den_in"), sem("den_inv"), sem("inv_in")

        FULL = T // 512
        REST = T - 512 * FULL
        turn = [("turn", 0), ("turn", 1)]
        query = [("query", k) for k in range(4)]
        score = []
        for q in range(2):
            score += [("score", k, u) for k in range(4 * q, 4 * q + 4) for u in range(FULL)] + [("rest", q)]
        rows = [("rows",)]
        first = turn + query + score[:12] + [("turn2", 0), ("turn2", 1)] + score[12:] + rows

        def schedule(i, last):
            ahead1, ahead2 = not (last and i == HB - 1), not (last and i >= HB - 2)
            steps = [[] for _ in range(TJ)]
            if ahead1:
                counts = [3, 3, 3, 3, 3, 3, 2, 2, 2, 2]
                n = 0
                for j, m in enumerate(counts):
                    steps[j] += score[n:n + m]
                    n += m
                assert n == len(score)
                steps[11] += rows
            if ahead2:
                steps[10].append(turn[0])
                steps[12].append(turn[1])
                if i % 2 == 0:
                    steps[10].append(query[0])
                    steps[11].append(query[1])
                    steps[12] += query[2:]
            return steps

        ITEMS = sum(len(s) for i in range(HB) for s in schedule(i, False))
        QUERIES, FIRST = 4 * (HB // 2), len(first)
        PASSES = B // HB

        class Ring:

            def __init__(self, base):
                self.base, self.n = base, 0

            def take(self):
                n = self.n
                self.n += 1
                return n

        def slot_of(x):
            return x % HB

        with nc.Block() as block:
            @block.sync
            def _(sp):
                def place_max(x, slot):
                    sp.wait_ge(rows_ready, x + 1)
                    sp.dma_start(q_hi[0:1, slot, :], max_rows[:, :]).then_inc(rows_in, 16)

                place_max(0, 0)

                def one_pass(g, last):
                    for i in range(HB):
                        if not (last and i >= HB - 2):
                            context.load(sp, g * HB + (i + 2), slot_of(i + 2))
                        if not (last and i == HB - 1):
                            place_max(g * HB + (i + 1), slot_of(i + 1))

                with sp.Fori(0, PASSES - 1) as g:
                    one_pass(g, False)
                sp.wait_ge(sum_out, EARLY + 1)
                for half in range(2):
                    row, place = denominators(w, half, 0, EARLY)
                    sp.dma_start(place, row).then_inc(den_in, 16)
                one_pass(PASSES - 1, True)
                sp.wait_ge(den_inv, 1)
                for half in range(2):
                    row, place = denominators(w, half, 0, EARLY)
                    sp.dma_start(row, place).then_inc(inv_in, 16)
                sp.wait_ge(inv_in, 32)

            @block.gpsimd
            def _(pool):
                context.split(pool, 1, 1)

                def one_pass(g, last):
                    for i in range(HB if not last else HB - 2):
                        pool.wait_ge(summed, (g * HB + i) * TJ + 2)
                        context.normalise(pool, g * HB + (i + 2), slot_of(i + 2))
                        context.split(pool, g * HB + (i + 2), slot_of(i + 2))

                with pool.Fori(0, PASSES - 1) as g:
                    one_pass(g, False)
                one_pass(PASSES - 1, True)
                pool.wait_ge(parts_ready, B)

            @block.vector
            def _(dve):
                copy = nc.vector.tensor_copy

                def take(ring, item, x, slot):
                    n = ring.take()
                    bank = ps[:, RING + n % 3, :]
                    kind = item[0]
                    dve.wait_ge(ring_filled, ring.base + (n + 1))
                    if kind == "turn":
                        m = (P * 8, P * (TJ - 8))[item[1]]
                        last = copy(ctx_T[:, slot, P * 8 * item[1]:P * 8 * item[1] + m], bank.bitcast(F16)[:, 0:m])
                    elif kind == "query":
                        dve.wait_ge(hi_done, ring.queries + 1)
                        ring.queries += 1
                        k = item[1]
                        v = lambda t: t[:, slot:slot + 2, :].rearrange("p b (h s) -> p h b s", h=H)[:, 4 * k:4 * k + 4, :, :]
                        last = nc.vector.tensor_tensor(v(q_lo), bank.rearrange("p (h b s) -> p h b s", h=4, b=2), v(q_hi), ALU.subtract)
                    elif kind == "score":
                        last = nc.vector.tensor_reduce(part_max[:, item[1], item[2]:item[2] + 1], bank, AX.X, ALU.max)
                    elif kind == "rest":
                        q = item[1]
                        last = nc.vector.tensor_reduce(part_max[:, 4 * q:4 * q + 4, FULL], bank[:, 0:4 * REST].rearrange("p (k t) -> p k t", k=4),
                                                       AX.X, ALU.max)
                    else:
                        last = copy(max_rows[:, :], ps[0:H // 2, RING + n % 3, 0:P])
                    last.then_inc(ring_done, 1)
                    if kind == "rows":
                        dve.wait_ge(ring_done, ring.base + (n + 1))
                        dve.sem_inc(rows_ready, 1)

                def maxima(ring, x):
                    dve.wait_ge(ring_done, ring.base + ring.n)
                    nc.vector.tensor_reduce(neg_max[:, :], part_max[:, :, :], AX.X, ALU.max, negate=True).then_inc(max_ready, 1)

                ring = Ring(0)
                ring.queries = 0
                for item in first:
                    if item[0] == "rows":
                        maxima(ring, 0)
                    if item[0] == "turn2":
                        take(ring, ("turn", item[1]), 1, 1)
                    else:
                        take(ring, item, 0, 0)

                def one_pass(g, last):
                    ring = Ring(g * ITEMS + FIRST)
                    ring.queries = g * QUERIES + 4
                    for i in range(HB):
                        x = g * HB + i
                        ahead2 = not (last and i >= HB - 2)
                        for j, items in enumerate(schedule(i, last)):
                            if ahead2 and j == 0:
                                context.means(dve, x + 2, slot_of(i + 2))
                            if ahead2 and j == 3:
                                context.variances(dve, x + 2)
                            for item in items:
                                if item[0] == "rows":
                                    take(ring, item, x + 1, slot_of(i + 1))
                                elif item[0] in ("turn", "query"):
                                    take(ring, item, x + 2, slot_of(i + 2))
                                else:
                                    take(ring, item, x + 1, slot_of(i + 1))
                            if j == 9 and items:
                                maxima(ring, x + 1)

                with dve.Fori(0, PASSES - 1) as g:
                    one_pass(g, False)
                one_pass(PASSES - 1, True)
                early = w["den"][:, :, 0:EARLY * 512 // P]
                dve.wait_ge(den_in, 32)
                nc.vector.reciprocal(early, early).then_inc(den_inv, 1)

            @block.scalar
            def _(act):
                act.sem_inc(exp_done, 2)
                act.sem_inc(sum_out, 1)

                def high(n, base, k, slot):
                    act.wait_ge(ring_filled, base + (n + 1))
                    v = q_hi[:, slot:slot + 2, :].rearrange("p b (h s) -> p h b s", h=H)[:, 4 * k:4 * k + 4, :, :]
                    act.copy(v, ps[:, RING + n % 3, :].rearrange("p (h b s) -> p h b s", h=4, b=2)).then_inc(hi_done, 1)

                def sums_out(x):
                    act.wait_ge(summed, x * TJ + (TJ + 2))
                    act.copy(w["attended"][:, bass.ds(x, 1), :].rearrange("p o n -> p (o n)"), ps[:, SUM, :]).then_inc(sum_out, 1)

                for n, item in enumerate(first):
                    if item[0] == "query":
                        high(n, 0, item[1], 0)

                def one_pass(g, last):
                    ring = Ring(g * ITEMS + FIRST)
                    for i in range(HB):
                        x = g * HB + i
                        for j, items in enumerate(schedule(i, last)):
                            t = x * TJ + j
                            act.wait_ge(scored, t + 1)
                            act.wait_ge(summed, t + 1)
                            m = P if j < TJ - 1 else TLAST
                            k = (i * TJ + j) % 2
                            act.activation(expd[0:m, k, :], ps[0:m, SCORE + 2 * k:SCORE + 2 * k + 2, :].rearrange("p k n -> p (k n)"),
                                           ACT.Exp, scale=SCORE_SCALE / QUERY_SCALE).then_inc(exp_done, 1)
                            for item in items:
                                n = ring.take()
                                if item[0] == "query":
                                    high(n, ring.base, item[1], slot_of(i + 2))
                        sums_out(x)

                with act.Fori(0, PASSES - 1) as g:
                    one_pass(g, False)
                one_pass(PASSES - 1, True)
                act.wait_ge(sum_out, B + 1)

            @block.tensor
            def _(pe):
                pe.sem_inc(summed, 2)

                def put(ring, item, x, slot):
                    n = ring.take()
                    bank = ps[:, RING + n % 3, :]
                    kind = item[0]
                    if not (isinstance(ring.base, int) and ring.base == 0 and n < 3):
                        pe.wait_ge(ring_done, ring.base + (n - 2 if n else 0))
                    if kind == "turn":
                        if item[1] == 0:
                            pe.wait_ge(parts_ready, x + 1)
                        for j in range(8 * item[1], min(8 * item[1] + 8, TJ)):
                            last = nc.tensor.transpose(bank.bitcast(F16)[:, P * (j % 8):P * (j % 8) + P],
                                                       ctx_parts[:, j, :, :].rearrange("p u c -> p (u c)"), w["ident16"][:, :])
                    elif kind == "query":
                        k = item[1]
                        for h in range(4):
                            last = nc.tensor.matmul(bank[:, P * h:P * h + P], w["query_fold"][:, 4 * k + h, :, :].rearrange("p u c -> p (u c)"),
                                                    w["xqT"][:, bass.ds(x * S, 2 * S)], start=True, stop=True)
                    elif kind == "score":
                        k, u = item[1:]
                        last = nc.tensor.matmul(bank, q_hi[:, slot, P * k:P * k + P], ctx_T[:, slot, 512 * u:512 * u + 512], start=True, stop=True)
                    elif kind == "rest":
                        for k in range(4):
                            last = nc.tensor.matmul(bank[:, REST * k:REST * k + REST], q_hi[:, slot, P * (4 * item[1] + k):P * (4 * item[1] + k) + P],
                                                    ctx_T[:, slot, 512 * FULL:T], start=True, stop=True)
                    else:
                        pe.wait_ge(max_ready, x + 1)
                        last = nc.tensor.transpose(ps[0:H // 2, RING + n % 3, 0:P], neg_max[:, :], w["ident"][:, :])
                    last.then_inc(ring_filled, 1)
                    if kind == "turn" and item[1] == 1:
                        pe.wait_ge(ring_filled, ring.base + (n + 1))
                        pe.sem_inc(parts_turned, 1)

                ring = Ring(0)
                for item in first:
                    if item[0] == "turn2":
                        put(ring, ("turn", item[1]), 1, 1)
                    else:
                        if item == score[0]:
                            pe.wait_ge(ring_done, ring.n)
                        put(ring, item, 0, 0)

                def tile_scores(x, i, j):
                    t = x * TJ + j
                    m = P if j < TJ - 1 else TLAST
                    k = (i * TJ + j) % 2
                    pe.wait_ge(exp_done, t + 1)
                    for half in range(2):
                        for part, q in enumerate((q_hi, q_lo)):
                            last = nc.tensor.matmul(ps[0:m, SCORE + 2 * k + half, :], ctx_T[:, slot_of(i), P * j:P * j + m],
                                                    q[:, slot_of(i), 512 * half:512 * half + 512], start=(part == 0), stop=(part == 1))
                    last.then_inc(scored, 1)

                def tile_sum(x, i, j):
                    t = x * TJ + j
                    m = P if j < TJ - 1 else TLAST
                    k = (i * TJ + j) % 2
                    pe.wait_ge(exp_done, t + 3)
                    if j == 0:
                        pe.wait_ge(sum_out, x + 1)
                        pe.wait_ge(ctx_ready, x + 1)
                    for half in range(2):
                        last = nc.tensor.matmul(ps[CY * half:CY * half + CY, SUM, :], ctx_n[0:m, slot_of(i), j, :],
                                                expd[0:m, k, 512 * half:512 * half + 512], start=(j == 0), stop=(j == TJ - 1))
                    last.then_inc(summed, 1)

                def one_pass(g, last):
                    ring = Ring(g * ITEMS + FIRST)
                    for i in range(HB):
                        x = g * HB + i
                        pe.wait_ge(rows_in, x * 16 + 16)
                        for j, items in enumerate(schedule(i, last)):
                            tile_scores(x, i, j)
                            if j:
                                tile_sum(x, i, j - 1)
                            for item in items:
                                if item[0] in ("turn", "query"):
                                    put(ring, item, x + 2, slot_of(i + 2))
                                else:
                                    put(ring, item, x + 1, slot_of(i + 1))
                        tile_sum(x, i, TJ - 1)

                with pe.Fori(0, PASSES - 1) as g:
                    one_pass(g, False)
                one_pass(PASSES - 1, True)


def finish_tokens(nc, a, out, w, ps, sb):
    with ExitStack() as ctx:
        sem = lambda n: ctx.enter_context(nc.semaphore("f_" + n))
        HELD = 4
        both = sb("both", [P, P])
        out_bias = sb("out_bias", [P, 1, C])
        flat = w["keys"][:, :, :, :, :].rearrange("p q b r t -> p (q b r t)")
        att = flat[:, 0:GB * 512].rearrange("p (b h s) -> p b h s", b=GB, s=S)
        x0 = sb("x0", [P, GT, C])
        added = sb("added", [P, GT, C])
        xo = sb("xo", [P, GT, C])
        n0 = sb("n0", [P, GT, C])
        nT = sb("nT", [P, GN])
        hT = sb("hT", [P, GN])
        hT_parts = sb("hT_parts", [P, 2, GN], F16)
        hid = flat[:, GB * 512:GB * 512 + FT * GN].rearrange("p (f n) -> p f n", f=FT)
        qkvz = flat[:, GB * 512 + FT * GN:].rearrange("p (i k c) -> p i k c", i=GT, k=4)
        q2 = sb("q2", [P, GT, C])
        q2b = sb("q2b", [P, GT, C])
        err = sb("err", [P, GT, C])
        o1 = sb("o1", [P, GT, C])
        o2 = sb("o2", [P, GT, C])
        spare = att[:, :, :, :].rearrange("p b h s -> p b (h s)")
        pairs = spare[:, 0:4, :].rearrange("p (u k) (d c) -> p u (k d) c", u=2, c=C)
        prods = spare[:, 4:6, :].rearrange("p k (d c) -> p (k d) c", c=C)
        logit_max = sb("logit_max", [P, GT])
        shifted_l = sb("shifted_l", [P, GT, NE])
        exp_l = sb("exp_l", [P, GT, NE])
        den_l = sb("den_l", [P, GT])
        top = sb("top", [P, GT])
        rank = sb("rank", [P, GT, NE])
        best = sb("best", [P, GT])
        gate = sb("gate", [P, GT, NE])
        act1 = sb("act1", [P, HELD, 2, GN])
        acc = sb("acc", [P, GT, C])
        x0_in, den_in, den_inv, inv_in = sem("x0_in"), sem("den_in"), sem("den_inv"), sem("inv_in")
        dve_steps, pool_steps = sem("dve_steps"), sem("pool_steps")
        both_ready, const_filled, fold_ready = sem("both_ready"), sem("const_filled"), sem("fold_ready")
        var_ready, rstd_ready = sem("var_ready"), sem("rstd_ready")
        inv_spread, att_out, projected, added_ready = sem("inv_spread"), sem("att_out"), sem("projected"), sem("added_ready")
        norm_ready, turned, nT_ready = sem("norm_ready"), sem("turned"), sem("nT_ready")
        high_ready, low_ready = sem("high_ready"), sem("low_ready")
        hid_filled, hid_ready, mlp_done = sem("hid_filled"), sem("hid_ready"), sem("mlp_done")
        qkvz_filled, qkvz_ready = sem("qkvz_filled"), sem("qkvz_ready")
        shifted_up, prev_filled, q2_ready, sig_ready = sem("shifted_up"), sem("prev_filled"), sem("q2_ready"), sem("sig_ready")
        pairs_ready, half_summed, sums_read, contracted = sem("pairs_ready"), sem("half_summed"), sem("sums_read"), sem("contracted")
        err_ready, lin_done = sem("err_ready"), sem("lin_done")
        logits_filled, logits_shifted, logits_exped = sem("logits_filled"), sem("logits_shifted"), sem("logits_exped")
        up_filled, up_ready, down_filled, acc_done, out_stored = (
            sem("up_filled"), sem("up_ready"), sem("down_filled"), sem("acc_done"), sem("out_stored"))
        norms = Norms(nc, sb, var_ready, rstd_ready, 4, "f")
        TURNS = 4
        STEPS = 22
        INV = float(C) ** -0.5
        RING, SUMS, TURN = 4, 6, 7
        xv = a["x"].rearrange("(i b) s c -> (b s) i c", b=2)
        ov = out.rearrange("(i b) s c -> (b s) i c", b=2)
        vec = lambda n: w["vec"][:, w["vec_of"][n]:w["vec_of"][n] + 1]
        banks4 = lambda b: ps[:, b, :].rearrange("p (i c) -> p i c", i=GT)

        up = lambda *ns: [("up", n) for n in ns]
        down = lambda e: [("down", e)]
        several = lambda kind, *ns: [(kind, n) for n in range(*ns)]
        halves = lambda *ns: [("sum", n, h) for n in range(*ns) for h in range(2)]
        BODY = up(0, 1) + several("inv", 0, 4) + down(0) + several("inv", 4, GB) + several("proj", GT)
        BODY += [("moments", 0)] + up(2, 3, 4, 5) + [("apply", 0)] + down(1) + [("turn", 0)] + up(6)
        BODY += several("hid", FT) + up(7, 8) + [("mlp",)]
        BODY += [("moments", 1)] + up(9, 10) + down(2) + [("apply", 1)] + down(3) + [("turn", 1), ("next",)] + several("qkvz", GT) + up(11) + [("prev",)]
        BODY += halves(0, 1) + up(12) + halves(1, 2) + up(13) + halves(2, 4) + down(4) + halves(4, 6) + up(14) + halves(6, 8) + [("y",)]
        BODY += up(15) + [("turn", 2)] + up(16) + [("lin",), ("moments", 2)] + up(17) + down(5) + [("apply", 2), ("moments", 3)]
        BODY += down(6) + [("apply", 3)] + down(7) + [("turn", 3)] + down(8) + [("logits",)]
        before = [s for s in BODY if s[0] not in ("up", "down")]
        experts = [s for s in BODY if s[0] in ("up", "down")]

        with nc.Block() as block:
            @block.sync
            def _(sp):
                for half in range(2):
                    row, place = denominators(w, half, EARLY, B)
                    sp.dma_start(place, row).then_inc(den_in, 16)
                sp.dma_start(x0[:, :, :], xv[:, 0:GT, :]).then_inc(x0_in, 16)
                sp.wait_ge(den_inv, 1)
                for half in range(2):
                    row, place = denominators(w, half, EARLY, B)
                    sp.dma_start(row, place).then_inc(inv_in, 16)

                def store(y):
                    sp.wait_ge(acc_done, y * NX + (NX + 2))
                    sp.dma_start(ov[:, bass.ds(y * GT, GT), :], acc[:, :, :]).then_inc(out_stored, 16)

                with sp.Fori(0, GROUPS - 1) as y:
                    sp.wait_ge(added_ready, y + 1)
                    sp.dma_start(x0[:, :, :], xv[:, bass.ds((y + 1) * GT, GT), :]).then_inc(x0_in, 16)
                    store(y)
                store(GROUPS - 1)
                sp.wait_ge(out_stored, 16 * GROUPS)

            @block.gpsimd
            def _(pool):
                step = Chain(pool, pool_steps, 0)
                step(pool.memset(both[:, :], 0.0))
                step(pool.memset(both[0:1, :], 1.0))
                pool.memset(both[CY:CY + 1, :], 1.0).then_inc(both_ready, 1)
                pool.wait_ge(both_ready, 1)

                def walk(x):
                    for kind, *arg in before:
                        if kind == "proj" and arg[0] == 0:
                            pool.wait_ge(x0_in, x * 16 + 16)
                            pool.tensor_tensor(added[:, :, :], x0[:, :, :], w["x3"][:, bass.ds(x * GT, GT), :], ALU.add).then_inc(added_ready, 1)
                        elif kind == "moments":
                            norms.on_pool(pool, x, arg[0], w["minus_half"])
                        elif kind == "sum" and arg[1] == 0:
                            n = arg[0]
                            i = n % GT
                            if n < GT:
                                pool.wait_ge(qkvz_ready, x * GT + (i + 1))
                            else:
                                pool.wait_ge(err_ready, x * GT + (i + 1))
                            if n >= 2:
                                pool.wait_ge(half_summed, x * 4 * GT + (2 * n - 2))
                            if n == GT:
                                pool.wait_ge(sig_ready, x + 1)
                            key = qkvz[:, i, 1 if n < GT else 3, :].rearrange("p (h d) -> p d h", d=DL)
                            val = (qkvz[:, i, 2, :] if n < GT else err[:, i, :]).rearrange("p (h e) -> p h e", e=DL)
                            o = pairs[:, n % 2, :, :].rearrange("p d (h e) -> p d h e", e=DL)
                            pool.tensor_tensor(o, spread(key, [P, DL, HL, DL]), val.unsqueeze(1).broadcast_to([P, DL, HL, DL]),
                                               ALU.mult).then_inc(pairs_ready, 1)

                walk(0)
                with pool.Fori(0, GROUPS - 1) as y:
                    walk(y + 1)

            @block.vector
            def _(dve):
                tt = nc.vector.tensor_tensor
                dve.sem_inc(acc_done, 2)
                dve.wait_ge(const_filled, 1)
                i = w["row_of"]["L0_xattn_a2_li1_b"]
                tt(out_bias[:, 0, :], ps[:, SUMS, 0:C], w["row"][:, i, :], ALU.add).then_inc(fold_ready, 1)
                nc.vector.memset(w["value_fold"][0:1, :, :], 0.0).then_inc(fold_ready, 1)
                nc.vector.memset(w["value_fold"][CY:CY + 1, :, :], 0.0).then_inc(fold_ready, 1)
                late = w["den"][:, :, EARLY * 512 // P:]
                dve.wait_ge(den_in, 32)
                nc.vector.reciprocal(late, late).then_inc(den_inv, 1)
                dve.wait_ge(fold_ready, 3)

                def walk(schedule, x, y=None):
                    step = Chain(dve, dve_steps, x * STEPS)
                    for kind, *arg in schedule:
                        n = arg[0] if arg else None
                        if kind == "inv":
                            dve.wait_ge(inv_spread, x * GB + (n + 1))
                            tt(att[:, n, :, :].rearrange("p h s -> p (h s)"), w["attended"][:, bass.ds(x * GB + n, 1), :].rearrange("p o n -> p (o n)"),
                               ps[:, RING + n % 2, :], ALU.mult).then_inc(att_out, 1)
                        elif kind == "proj" and n == 0:
                            if schedule is BODY:
                                dve.wait_ge(acc_done, y * NX + 3)
                            step(tt(xo[:, :, :], w["x3"][:, bass.ds(x * GT, GT), :], out_bias[:, :, :].broadcast_to([P, GT, C]), ALU.add))
                        elif kind == "moments":
                            if n == 0:
                                dve.wait_ge(projected, x * GT + GT)
                                step(tt(xo[:, :, :], xo[:, :, :], banks4(SUMS), ALU.add))
                            elif n == 1:
                                dve.wait_ge(mlp_done, x + 1)
                                step(tt(xo[:, :, :], xo[:, :, :], banks4(SUMS), ALU.add))
                            elif n == 2:
                                dve.wait_ge(lin_done, x + 1)
                                step(tt(xo[:, :, :], xo[:, :, :], banks4(SUMS), ALU.add))
                            norms.moments(dve, step, xo if n < 3 else n0)
                        elif kind == "apply":
                            if n == 2:
                                step(norms.apply(dve, x, n, n0, xo))
                            else:
                                norms.apply(dve, x, n, n0, xo if n < 3 else n0).then_inc(norm_ready, 1)
                            if n == 0:
                                dve.wait_ge(norm_ready, x * TURNS + 1)
                                step(tt(xo[:, :, :], xo[:, :, :], wide_row(w, "L0_xattn_a2_li3_b"), ALU.add))
                                dve.wait_ge(added_ready, x + 1)
                                step(tt(xo[:, :, :], xo[:, :, :], added[:, :, :], ALU.add))
                        elif kind == "qkvz":
                            dve.wait_ge(qkvz_filled, x * GT + (n + 1))
                            tt(qkvz[:, n, :, :].rearrange("p k c -> p (k c)"), ps[:, RING + n % 2, :],
                               w["qkvz_b"][:, :, :].rearrange("p k c -> p (k c)"), ALU.add).then_inc(qkvz_ready, 1)
                        elif kind == "prev":
                            dve.wait_ge(prev_filled, x + 1)
                            step(nc.vector.tensor_scalar(q2b[:, :, :], banks4(TURN), float(DL) ** -0.5, None, ALU.mult))
                            step(nc.vector.tensor_scalar(q2[:, :, :], q2b[:, :, :], 0.02, None, ALU.mult))
                            tt(q2[:, :, :], q2[:, :, :], q2b[:, :, :], ALU.min).then_inc(q2_ready, 1)
                            dve.wait_ge(shifted_up, x + 1)
                            dve.wait_ge(qkvz_ready, x * GT + GT)
                            dve.wait_ge(q2_ready, x + 1)
                        elif kind == "sum":
                            half = arg[1]
                            dve.wait_ge(half_summed, x * 4 * GT + (2 * n + half + 1))
                            q = qkvz[:, n, 0, :] if n < GT else q2[:, n - GT, :]
                            dh = DL // 2
                            s = ps[:, RING + half, :].rearrange("p (d h e) -> p d h e", h=HL, e=DL)
                            qs = spread(q.rearrange("p (h d) -> p d h", d=DL)[:, dh * half:dh * half + dh, :], [P, dh, HL, DL])
                            tt(prods[:, dh * half:dh * half + dh, :].rearrange("p d (h e) -> p d h e", e=DL), s, qs, ALU.mult).then_inc(sums_read, 1)
                            if half == 1:
                                dve.wait_ge(sums_read, x * 4 * GT + (2 * n + 2))
                                dst = o1[:, n, :] if n < GT else o2[:, n - GT, :]
                                nc.vector.tensor_reduce(dst, prods[:, :, :].rearrange("p d c -> p c d"), AX.X, ALU.add).then_inc(contracted, 1)
                                dve.wait_ge(contracted, x * 2 * GT + (n + 1))
                                if n < GT:
                                    tt(err[:, n, :], ps[:, SUMS, C * n:C * n + C], o1[:, n, :], ALU.subtract).then_inc(err_ready, 1)
                        elif kind == "y":
                            tt(n0[:, :, :], o1[:, :, :], o2[:, :, :], ALU.add).then_inc(norm_ready, 1)
                            step(tt(xo[:, :, :], xo[:, :, :], wide_row(w, "L0_attn_bp"), ALU.add))
                        elif kind == "logits":
                            dve.wait_ge(high_ready, x + 1)
                            tt(hT_parts[:, 1, :], hT[:, :], hT_parts[:, 0, :], ALU.subtract).then_inc(low_ready, 1)
                            dve.wait_ge(logits_filled, x + 1)
                            logits = ps[:, SUMS, 0:GT * NE].rearrange("p (i e) -> p i e", i=GT)
                            step(nc.vector.tensor_reduce(logit_max[:, :], logits, AX.X, ALU.max))
                            tt(shifted_l[:, :, :], logits, spread(logit_max[:, :], [P, GT, NE]), ALU.subtract).then_inc(logits_shifted, 1)
                            dve.wait_ge(logits_shifted, x + 1)
                            step(nc.vector.tensor_scalar(rank[:, :, :], shifted_l[:, :, :], 0.0, None, ALU.is_equal))
                            step(tt(rank[:, :, :], rank[:, :, :], w["iota_down"][:, :].unsqueeze(1).broadcast_to([P, GT, NE]), ALU.mult))
                            step(nc.vector.tensor_reduce(best[:, :], rank[:, :, :], AX.X, ALU.max))
                            step(tt(rank[:, :, :], rank[:, :, :], spread(best[:, :], [P, GT, NE]), ALU.is_equal))
                            dve.wait_ge(logits_exped, x + 1)
                            step(nc.vector.tensor_reduce(den_l[:, :], exp_l[:, :, :], AX.X, ALU.add))
                            step(nc.vector.reciprocal(top[:, :], den_l[:, :]))
                            step(tt(gate[:, :, :], rank[:, :, :], spread(top[:, :], [P, GT, NE]), ALU.mult))
                        elif kind == "down":
                            dve.wait_ge(down_filled, y * NX + (n + 1))
                            if n == 0:
                                tt(acc[:, :, :], xo[:, :, :], banks4(2), ALU.add).then_inc(acc_done, 1)
                            else:
                                dve.wait_ge(acc_done, y * NX + (n + 2))
                                for i in range(GT):
                                    last = nc.vector.scalar_tensor_tensor(out=acc[:, i, :], in0=ps[:, 2 + n % 2, C * i:C * i + C],
                                                                          scalar=gate[:, i, n - 1:n], in1=acc[:, i, :], op0=ALU.mult, op1=ALU.add)
                                last.then_inc(acc_done, 1)
                    if schedule is not experts:
                        assert step.n == STEPS, step.n
                    if schedule is BODY:
                        dve.wait_ge(out_stored, y * 16 + 16)
                    elif schedule is before:
                        dve.wait_ge(dve_steps, x * STEPS + STEPS)

                walk(before, 0)
                with dve.Fori(0, GROUPS - 1) as y:
                    walk(BODY, y + 1, y)
                walk(experts, 0, GROUPS - 1)

            @block.scalar
            def _(act):
                def walk(schedule, x, y=None):
                    for kind, *arg in schedule:
                        n = arg[0] if arg else None
                        if kind == "turn":
                            act.wait_ge(turned, x * TURNS + (n + 1))
                            affine = {0: dict(scale=vec("L0_xattn_a2_ln3_g"), bias=vec("L0_xattn_a2_ln3_b")),
                                      3: dict(scale=vec("L0_ffn_ln_gamma"), bias=vec("L0_ffn_ln_beta"))}.get(n, {})
                            act.activation(hT[:, :] if n == 3 else nT[:, :], ps[:, TURN, :], ACT.Identity, **affine).then_inc(nT_ready, 1)
                            if n == 3:
                                act.wait_ge(nT_ready, x * TURNS + 4)
                                act.copy(hT_parts[:, 0, :], hT[:, :]).then_inc(high_ready, 1)
                        elif kind == "hid":
                            act.wait_ge(hid_filled, x * FT + (n + 1))
                            act.activation(hid[:, n, :], ps[:, RING + n % 2, :], ACT.Gelu, bias=w["li2_b"]["a2"][:, n:n + 1]).then_inc(hid_ready, 1)
                        elif kind == "prev":
                            act.wait_ge(qkvz_ready, x * GT + GT)
                            act.activation(qkvz[:, :, 3, :], qkvz[:, :, 3, :], ACT.Sigmoid, scale=0.02 * INV).then_inc(sig_ready, 1)
                        elif kind == "logits":
                            act.wait_ge(logits_shifted, x + 1)
                            act.activation(exp_l[:, :, :], shifted_l[:, :, :], ACT.Exp).then_inc(logits_exped, 1)
                        elif kind == "up":
                            e, k = n // 2, n % 2
                            act.wait_ge(up_filled, y * 2 * NX + (n + 1))
                            if e >= HELD:
                                act.wait_ge(down_filled, y * NX + (e - HELD + 1))
                            act.activation(act1[:, e % HELD, k, :], ps[:, k, :], ACT.Silu, scale=w["s1"][:, n:n + 1]).then_inc(up_ready, 1)

                walk(before, 0)
                with act.Fori(0, GROUPS - 1) as y:
                    walk(BODY, y + 1, y)
                walk(experts, 0, GROUPS - 1)

            @block.tensor
            def _(pe):
                ident = w["ident"]
                pe.wait_ge(both_ready, 1)
                for k in range(H // 2):
                    last = nc.tensor.matmul(ps[:, SUMS, 0:C], both[:, :], w["value_fold"][:, k, :], start=(k == 0), stop=(k == H // 2 - 1))
                last.then_inc(const_filled, 1)

                def walk(schedule, x, y=None):
                    for kind, *arg in schedule:
                        n = arg[0] if arg else None
                        if kind == "inv":
                            if n >= 2:
                                pe.wait_ge(att_out, x * GB + (n - 1))
                            nc.tensor.matmul(ps[:, RING + n % 2, :], w["sel"][:, :, :].rearrange("p u c -> p (u c)"),
                                             w["attended"][:, bass.ds(x * GB + n, 1), :].rearrange("p o n -> p (o n)"), start=True, stop=True).then_inc(inv_spread, 1)
                        elif kind == "proj":
                            if isinstance(x, int) and n == 0:
                                pe.wait_ge(fold_ready, 3)
                            pe.wait_ge(att_out, x * GB + (2 * n + 2))
                            for k in range(H // 2):
                                for u in range(2):
                                    last = nc.tensor.matmul(ps[S * u:S * u + S, SUMS, C * n:C * n + C], att[:, 2 * n + u, k, :], w["value_fold"][:, k, :],
                                                            start=(k == 0), stop=(k == H // 2 - 1))
                            last.then_inc(projected, 1)
                        elif kind == "turn":
                            pe.wait_ge(norm_ready, x * TURNS + (n + 1))
                            for i in range(GT):
                                last = nc.tensor.transpose(ps[:, TURN, P * i:P * i + P], n0[:, i, :], ident[:, :])
                            last.then_inc(turned, 1)
                        elif kind == "hid":
                            if n == 0:
                                pe.wait_ge(nT_ready, x * TURNS + 1)
                            if n >= 2:
                                pe.wait_ge(hid_ready, x * FT + (n - 1))
                            nc.tensor.matmul(ps[:, RING + n % 2, :], w["li2"]["a2"][:, P * n:P * n + P], nT[:, :], start=True, stop=True).then_inc(hid_filled, 1)
                        elif kind == "mlp":
                            pe.wait_ge(hid_ready, x * FT + FT)
                            for i in range(GT):
                                for f in range(FT):
                                    last = nc.tensor.matmul(ps[:, SUMS, C * i:C * i + C], hid[:, f, P * i:P * i + P], w["li3"]["a2"][:, f, :],
                                                            start=(f == 0), stop=(f == FT - 1))
                            last.then_inc(mlp_done, 1)
                        elif kind == "next":
                            nc.tensor.matmul(ps[:, SUMS, :], w["next"][:, :], n0[:, :, :].rearrange("p i c -> p (i c)"), start=True, stop=True).then_inc(shifted_up, 1)
                        elif kind == "qkvz":
                            if n == 0:
                                pe.wait_ge(nT_ready, x * TURNS + 2)
                            if n >= 2:
                                pe.wait_ge(qkvz_ready, x * GT + (n - 1))
                            nc.tensor.matmul(ps[:, RING + n % 2, :], nT[:, P * n:P * n + P], w["qkvz"][:, :, :].rearrange("p k c -> p (k c)"),
                                             start=True, stop=True).then_inc(qkvz_filled, 1)
                        elif kind == "prev":
                            pe.wait_ge(qkvz_ready, x * GT + GT)
                            nc.tensor.matmul(ps[:, TURN, :], w["prev"][:, :], qkvz[:, :, 0, :], start=True, stop=True).then_inc(prev_filled, 1)
                        elif kind == "sum":
                            half = arg[1]
                            if half == 0:
                                pe.wait_ge(pairs_ready, x * 2 * GT + (n + 1))
                            if n >= 1:
                                pe.wait_ge(sums_read, x * 4 * GT + (2 * n + half - 1))
                            tri = w["upto"] if n < GT else w["before"]
                            nc.tensor.matmul(ps[:, RING + half, :], tri[:, :], pairs[:, n % 2, 4 * half:4 * half + 4, :].rearrange("p d c -> p (d c)"),
                                             start=True, stop=True).then_inc(half_summed, 1)
                        elif kind == "lin":
                            pe.wait_ge(nT_ready, x * TURNS + 3)
                            for i in range(GT):
                                last = nc.tensor.matmul(ps[:, SUMS, C * i:C * i + C], nT[:, P * i:P * i + P], w["wp"][:, :], start=True, stop=True)
                            last.then_inc(lin_done, 1)
                        elif kind == "logits":
                            pe.wait_ge(nT_ready, x * TURNS + 4)
                            for i in range(GT):
                                last = nc.tensor.matmul(ps[:, SUMS, NE * i:NE * i + NE], hT[:, P * i:P * i + P], w["router"][:, :], start=True, stop=True)
                            last.then_inc(logits_filled, 1)
                        elif kind == "up":
                            if n >= 2:
                                pe.wait_ge(up_ready, y * 2 * NX + (n - 1))
                            if n == 0:
                                pe.wait_ge(high_ready, y + 1)
                                pe.wait_ge(low_ready, y + 1)
                            for part in range(2):
                                last = nc.tensor.matmul(ps[:, n % 2, :], w["t1T"][:, n, :], hT_parts[:, part, :], start=(part == 0), stop=(part == 1))
                            last.then_inc(up_filled, 1)
                        elif kind == "down":
                            pe.wait_ge(up_ready, y * 2 * NX + (2 * n + 2))
                            pe.wait_ge(acc_done, y * NX + (n + 1))
                            for i in range(GT):
                                for k in range(2):
                                    last = nc.tensor.matmul(ps[:, 2 + n % 2, C * i:C * i + C], act1[:, n % HELD, k, P * i:P * i + P], w["t2T"][:, 2 * n + k, :],
                                                            start=(k == 0), stop=(k == 1))
                            last.then_inc(down_filled, 1)

                walk(before, 0)
                pe.wait_ge(inv_in, 32)
                with pe.Fori(0, GROUPS - 1) as y:
                    walk(BODY, y + 1, y)
                walk(experts, 0, GROUPS - 1)


_OUT = ((B, S, C), "float32")


def kernel(**inputs):
    import numpy as np
    import concourse.bacc as bacc
    from concourse.bass_utils import run_bass_kernel_spmd

    nc = bacc.Bacc("TRN2", target_bir_lowering=False, num_devices=1)
    arrays, args = {}, {}
    for name, value in inputs.items():
        value = np.ascontiguousarray(value)
        arrays[f"in_{name}"] = value
        args[name] = nc.dram_tensor(f"in_{name}", value.shape, mybir.dt.from_np(value.dtype), kind="ExternalInput").ap()
    out = nc.dram_tensor("out_x", _OUT[0], mybir.dt.from_np(np.dtype(_OUT[1])), kind="ExternalOutput").ap()
    perceiver_kernel(nc, args, out)
    r = run_bass_kernel_spmd(nc, [arrays], core_ids=[0])
    return r.results[0]["out_x"]
```
